# Optimizing a Trainium2 kernel written in Bass

```python
import numpy as np
import jax
import jax.numpy as jnp

def _softmax(x, axis=-1):
    return jax.nn.softmax(x, axis=axis)

def _gelu(x):
    return jax.nn.gelu(x, approximate=True)

def _silu(x):
    return jax.nn.silu(x)

def _sigmoid(x):
    return jax.nn.sigmoid(x)

def _layernorm(x, axis=-1, eps=1e-05):
    m = jnp.mean(x, axis=axis, keepdims=True)
    v = jnp.var(x, axis=axis, keepdims=True)
    return (x - m) / jnp.sqrt(v + eps)

def _scatter_add(tgt, idx, src, axis=0):
    return tgt.at[idx].add(src)

def _segment_sum(src, seg, n):
    return jax.ops.segment_sum(src, seg, n)
kernel_name = 'mk_hybrid_d2_jaxref_r4_d148ab'

def setup_inputs(seed: int=0):
    np.random.seed(seed)
    _w = jnp.asarray

    def _L0_attn_a_setup():
        import jax, jax.numpy as jnp
        import numpy as np
        import math
        B, S, D = (4, 512, 256)
        H = 16
        HD = D // H
        DL = 64
        LAMBDA_DECAY = 0.01
        key = jax.random.key(seed)
        ks = jax.random.split(key, 8)
        sc = lambda fan_in: 1.0 / math.sqrt(fan_in)
        return {'x': jax.random.normal(ks[0], (B, S, D), dtype=jnp.float32), 'W_q': jax.random.normal(ks[1], (D, D), dtype=jnp.float32) * sc(D), 'W_k': jax.random.normal(ks[2], (D, D), dtype=jnp.float32) * sc(D), 'W_v': jax.random.normal(ks[3], (D, D), dtype=jnp.float32) * sc(D), 'W_o': jax.random.normal(ks[4], (D, D), dtype=jnp.float32) * sc(D), 'W_down_kv': jax.random.normal(ks[5], (D, DL), dtype=jnp.float32) * sc(D), 'W_up_k': jax.random.normal(ks[6], (DL, D), dtype=jnp.float32) * sc(DL), 'W_up_v': jax.random.normal(ks[7], (DL, D), dtype=jnp.float32) * sc(DL)}
    _L0_attn_a_in = _L0_attn_a_setup()

    def _L0_attn_b_setup():
        import jax, jax.numpy as jnp
        import numpy as np
        D_MODEL = 256
        NHEAD = 16
        HEAD_DIM = D_MODEL // NHEAD
        LN_EPS = 1e-05

        def _retention_scan(v, lam_h):
            B, L, H, DH = v.shape
            a = jnp.broadcast_to(lam_h[None, None, :, None], v.shape)

            def combine(x, y):
                a1, b1 = x
                a2, b2 = y
                return (a1 * a2, a2 * b1 + b2)
            _, states = jax.lax.associative_scan(combine, (a, v), axis=1)
            return states
        key = jax.random.key(seed)
        ks = jax.random.split(key, 6)
        B, L, D = (4, 1024, D_MODEL)
        s = 1.0 / np.sqrt(D)
        return {'x': jax.random.normal(ks[0], (B, L, D), jnp.float32), 'Wq': jax.random.normal(ks[1], (D, D), jnp.float32) * s, 'Wv': jax.random.normal(ks[2], (D, D), jnp.float32) * s, 'Wg': jax.random.normal(ks[3], (D, D), jnp.float32) * s, 'Wo': jax.random.normal(ks[4], (D, D), jnp.float32) * s, 'beta': jnp.full((NHEAD,), -0.2, jnp.float32), 'ln_gamma': jnp.ones((D_MODEL,), jnp.float32), 'ln_beta': jnp.zeros((D_MODEL,), jnp.float32)}
    _L0_attn_b_in = _L0_attn_b_setup()

    def _L0_ffn_setup():
        import jax, jax.numpy as jnp
        import numpy as np
        N, T, D = (4, 1024, 256)
        NUM_EXPERTS = 8
        EXPERT_CAP = 2.0
        MLP_RATIO = 4
        HIDDEN = MLP_RATIO * D
        key = jax.random.key(seed)
        k1, k2, k3, k4 = jax.random.split(key, 4)
        x = jax.random.normal(k1, (N, T, D), dtype=jnp.float32)
        gate_w = jax.random.truncated_normal(k2, -2.0, 2.0, (D, NUM_EXPERTS), dtype=jnp.float32) * 0.02
        w1 = jax.random.normal(k3, (NUM_EXPERTS, D, HIDDEN), dtype=jnp.float32) * 0.02
        w2 = jax.random.normal(k4, (NUM_EXPERTS, HIDDEN, D), dtype=jnp.float32) * 0.02
        return {'x': x, 'gate_w': gate_w, 'w1': w1, 'w2': w2}
    _L0_ffn_in = _L0_ffn_setup()

    def _L1_attn_a_setup():
        import jax, jax.numpy as jnp
        import numpy as np
        EMB = 256
        HEADS = 16
        HEAD_DIM = EMB // HEADS
        BLOCK = 64
        N_GLOBAL = 4
        WINDOW = 128
        ROPE_BASE = 10000.0

        def rotate_half(x):
            x1 = x[..., ::2]
            x2 = x[..., 1::2]
            return jnp.stack((-x2, x1), axis=-1).reshape(x.shape)

        def rope_cos_sin(seq_len, dtype=jnp.float32):
            inv_freq = 1.0 / ROPE_BASE ** (jnp.arange(0, HEAD_DIM, 2, dtype=jnp.float32) / HEAD_DIM)
            pos = jnp.arange(seq_len, dtype=jnp.float32)
            freqs = jnp.outer(pos, inv_freq)
            emb = jnp.concatenate([freqs, freqs], -1)
            return (jnp.cos(emb)[None, None].astype(dtype), jnp.sin(emb)[None, None].astype(dtype))

        def block_mask(seq_len):
            i = jnp.arange(seq_len)[:, None]
            j = jnp.arange(seq_len)[None, :]
            blk = i // BLOCK == j // BLOCK
            glob = (i < N_GLOBAL) | (j < N_GLOBAL)
            slide = jnp.abs(i - j) <= WINDOW
            return (blk | glob | slide) & (j <= i)
        key = jax.random.key(seed)
        kx, kq, ko = jax.random.split(key, 3)
        B, S = (2, 512)
        x = jax.random.normal(kx, (B, S, EMB), jnp.float32)
        qkv_w = jax.random.normal(kq, (3 * EMB, EMB), jnp.float32) * EMB ** (-0.5)
        out_w = jax.random.normal(ko, (EMB, EMB), jnp.float32) * EMB ** (-0.5)
        return {'x': x, 'qkv_w': qkv_w, 'out_w': out_w}
    _L1_attn_a_in = _L1_attn_a_setup()

    def _L1_attn_b_setup():
        import jax, jax.numpy as jnp
        import numpy as np
        HIDDEN = 256
        EXPAND = 1
        INPUT_DIM = HIDDEN * EXPAND
        CONV_K = 4
        NORM_EPS = 1e-05

        def causal_depthwise_conv(x, w):
            B, T, D = x.shape
            K = w.shape[1]
            xp = jnp.pad(x, ((0, 0), (K - 1, 0), (0, 0)))
            out = jnp.zeros_like(x)
            for k in range(K):
                out = out + xp[:, k:k + T, :] * w[:, k]
            return out

        def hgrn_forward(x, Wi, Wf, Wg, conv_i, conv_f, g_norm_weight, Wo):
            B, T, H = x.shape
            i_raw = jnp.einsum('bth,hd->btd', x, Wi)
            f_raw = jnp.einsum('bth,hd->btd', x, Wf)
            g_raw = jnp.einsum('bth,hd->btd', x, Wg)
            i_raw = causal_depthwise_conv(i_raw, conv_i)
            f_raw = causal_depthwise_conv(f_raw, conv_f)
            forget_gate = jax.nn.sigmoid(f_raw)
            i = jax.nn.silu(i_raw) * (1.0 - forget_gate)

            def step(h, fi):
                f_t, i_t = fi
                h = f_t * h + i_t
                return (h, h)
            h0 = jnp.zeros((B, i.shape[-1]), dtype=x.dtype)
            _, o_rec = jax.lax.scan(step, h0, (forget_gate.swapaxes(0, 1), i.swapaxes(0, 1)))
            o_rec = o_rec.swapaxes(0, 1)
            rms = jax.lax.rsqrt(jnp.mean(o_rec * o_rec, axis=-1, keepdims=True) + NORM_EPS)
            o = o_rec * rms * g_norm_weight * jax.nn.silu(g_raw)
            return jnp.einsum('btd,dh->bth', o, Wo)
        key = jax.random.key(seed)
        ks = jax.random.split(key, 8)
        B, T, H, D = (4, 512, HIDDEN, INPUT_DIM)
        s = 1.0 / np.sqrt(H)
        return {'x': jax.random.normal(ks[0], (B, T, H), dtype=jnp.float32), 'Wi': jax.random.normal(ks[1], (H, D), dtype=jnp.float32) * s, 'Wf': jax.random.normal(ks[2], (H, D), dtype=jnp.float32) * s, 'Wg': jax.random.normal(ks[3], (H, D), dtype=jnp.float32) * s, 'conv_i': jax.random.normal(ks[4], (D, CONV_K), dtype=jnp.float32) * 0.5, 'conv_f': jax.random.normal(ks[5], (D, CONV_K), dtype=jnp.float32) * 0.5, 'g_norm_weight': jnp.ones((D,), dtype=jnp.float32), 'Wo': jax.random.normal(ks[6], (D, H), dtype=jnp.float32) / np.sqrt(D)}
    _L1_attn_b_in = _L1_attn_b_setup()

    def _L1_ffn_setup():
        import jax, jax.numpy as jnp
        import numpy as np
        D_MODEL, D_FF, RANK = (256, 1024, 64)
        B, S = (4, 1024)
        key = jax.random.key(seed)
        ks = jax.random.split(key, 7)
        return {'x': jax.random.normal(ks[0], (B, S, D_MODEL), dtype=jnp.float32), 'U1': jax.random.normal(ks[1], (D_MODEL, RANK), dtype=jnp.float32) * 0.02, 'V1': jax.random.normal(ks[2], (RANK, D_FF), dtype=jnp.float32) * 0.02, 'b1': jnp.zeros((D_FF,), dtype=jnp.float32), 'U2': jax.random.normal(ks[3], (D_FF, RANK), dtype=jnp.float32) * 0.02, 'V2': jax.random.normal(ks[4], (RANK, D_MODEL), dtype=jnp.float32) * 0.02, 'b2': jnp.zeros((D_MODEL,), dtype=jnp.float32)}
    _L1_ffn_in = _L1_ffn_setup()
    _d = {'L0_attn_a_x': _L0_attn_a_in['x'], 'L0_attn_a_W_q': _L0_attn_a_in['W_q'], 'L0_attn_a_W_k': _L0_attn_a_in['W_k'], 'L0_attn_a_W_v': _L0_attn_a_in['W_v'], 'L0_attn_a_W_o': _L0_attn_a_in['W_o'], 'L0_attn_a_W_down_kv': _L0_attn_a_in['W_down_kv'], 'L0_attn_a_W_up_k': _L0_attn_a_in['W_up_k'], 'L0_attn_a_W_up_v': _L0_attn_a_in['W_up_v'], 'L0_attn_b_Wq': _L0_attn_b_in['Wq'], 'L0_attn_b_Wv': _L0_attn_b_in['Wv'], 'L0_attn_b_Wg': _L0_attn_b_in['Wg'], 'L0_attn_b_Wo': _L0_attn_b_in['Wo'], 'L0_attn_b_beta': _L0_attn_b_in['beta'], 'L0_attn_b_ln_gamma': _L0_attn_b_in['ln_gamma'], 'L0_attn_b_ln_beta': _L0_attn_b_in['ln_beta'], 'L0_ffn_gate_w': _L0_ffn_in['gate_w'], 'L0_ffn_w1': _L0_ffn_in['w1'], 'L0_ffn_w2': _L0_ffn_in['w2'], 'L1_attn_a_qkv_w': _L1_attn_a_in['qkv_w'], 'L1_attn_a_out_w': _L1_attn_a_in['out_w'], 'L1_attn_b_Wi': _L1_attn_b_in['Wi'], 'L1_attn_b_Wf': _L1_attn_b_in['Wf'], 'L1_attn_b_Wg': _L1_attn_b_in['Wg'], 'L1_attn_b_conv_i': _L1_attn_b_in['conv_i'], 'L1_attn_b_conv_f': _L1_attn_b_in['conv_f'], 'L1_attn_b_g_norm_weight': _L1_attn_b_in['g_norm_weight'], 'L1_attn_b_Wo': _L1_attn_b_in['Wo'], 'L1_ffn_U1': _L1_ffn_in['U1'], 'L1_ffn_V1': _L1_ffn_in['V1'], 'L1_ffn_b1': _L1_ffn_in['b1'], 'L1_ffn_U2': _L1_ffn_in['U2'], 'L1_ffn_V2': _L1_ffn_in['V2'], 'L1_ffn_b2': _L1_ffn_in['b2']}
    _x0 = _d['L0_attn_a_x']
    _d['L0_attn_a_x'] = jax.random.normal(jax.random.fold_in(jax.random.key(seed), 1), (4, 1024, 256), dtype=_x0.dtype)
    del _x0
    return _d

def reference(L0_attn_a_x, L0_attn_a_W_q, L0_attn_a_W_k, L0_attn_a_W_v, L0_attn_a_W_o, L0_attn_a_W_down_kv, L0_attn_a_W_up_k, L0_attn_a_W_up_v, L0_attn_b_Wq, L0_attn_b_Wv, L0_attn_b_Wg, L0_attn_b_Wo, L0_attn_b_beta, L0_attn_b_ln_gamma, L0_attn_b_ln_beta, L0_ffn_gate_w, L0_ffn_w1, L0_ffn_w2, L1_attn_a_qkv_w, L1_attn_a_out_w, L1_attn_b_Wi, L1_attn_b_Wf, L1_attn_b_Wg, L1_attn_b_conv_i, L1_attn_b_conv_f, L1_attn_b_g_norm_weight, L1_attn_b_Wo, L1_ffn_U1, L1_ffn_V1, L1_ffn_b1, L1_ffn_U2, L1_ffn_V2, L1_ffn_b2):

    def _L0_attn_a_ref(x, W_q, W_k, W_v, W_o, W_down_kv, W_up_k, W_up_v):
        import jax, jax.numpy as jnp
        import numpy as np
        import math
        B, S, D = (4, 512, 256)
        H = 16
        HD = D // H
        DL = 64
        LAMBDA_DECAY = 0.01
        b, s, d = x.shape
        q = x @ W_q
        k = x @ W_k
        v = x @ W_v
        latent_kv = (k + v) @ W_down_kv
        k_rec = (latent_kv @ W_up_k).reshape(b, s, H, HD).transpose(0, 2, 1, 3)
        v_rec = (latent_kv @ W_up_v).reshape(b, s, H, HD).transpose(0, 2, 1, 3)
        qh = q.reshape(b, s, H, HD).transpose(0, 2, 1, 3)
        scores = jnp.einsum('bhqd,bhkd->bhqk', qh, k_rec) / math.sqrt(d)
        t = jnp.arange(s, dtype=jnp.float32)
        decay = jnp.exp(-LAMBDA_DECAY * jnp.abs(t[:, None] - t[None, :]))
        scores = scores * decay[None, None, :, :]
        attn = jax.nn.softmax(scores, axis=-1)
        out = jnp.einsum('bhqk,bhkd->bhqd', attn, v_rec)
        out = out.transpose(0, 2, 1, 3).reshape(b, s, d)
        return out @ W_o

    def _L0_attn_b_ref(x, Wq, Wv, Wg, Wo, beta, ln_gamma, ln_beta):
        import jax, jax.numpy as jnp
        import numpy as np
        D_MODEL = 256
        NHEAD = 16
        HEAD_DIM = D_MODEL // NHEAD
        LN_EPS = 1e-05

        def _retention_scan(v, lam_h):
            B, L, H, DH = v.shape
            a = jnp.broadcast_to(lam_h[None, None, :, None], v.shape)

            def combine(x, y):
                a1, b1 = x
                a2, b2 = y
                return (a1 * a2, a2 * b1 + b2)
            _, states = jax.lax.associative_scan(combine, (a, v), axis=1)
            return states
        B, L, D = x.shape
        H, DH = (NHEAD, HEAD_DIM)
        q = (x @ Wq.T).reshape(B, L, H, DH)
        v = (x @ Wv.T).reshape(B, L, H, DH)
        lam_h = jax.nn.sigmoid(beta)
        state = _retention_scan(v, lam_h)
        y = (q * state).reshape(B, L, D)
        mu = jnp.mean(y, axis=-1, keepdims=True)
        var = jnp.mean((y - mu) ** 2, axis=-1, keepdims=True)
        y = (y - mu) * jax.lax.rsqrt(var + LN_EPS) * ln_gamma + ln_beta
        gate = jax.nn.silu(x @ Wg.T)
        y = y * gate
        return y @ Wo.T

    def _L0_ffn_ref(x, gate_w, w1, w2):
        import jax, jax.numpy as jnp
        import numpy as np
        N, T, D = (4, 1024, 256)
        NUM_EXPERTS = 8
        EXPERT_CAP = 2.0
        MLP_RATIO = 4
        HIDDEN = MLP_RATIO * D
        x = x.astype(jnp.float32)
        n, t, d = x.shape
        k = int(EXPERT_CAP * t / NUM_EXPERTS)
        scores = jnp.einsum('ntd,de->nte', x, gate_w)
        probs = jax.nn.softmax(scores, axis=-1)
        probs = jnp.transpose(probs, (0, 2, 1))
        g, m = jax.lax.top_k(probs, k)
        xin = jax.vmap(lambda xb, mb: xb[mb])(x, m)
        h = jax.nn.gelu(jnp.einsum('nekd,edf->nekf', xin, w1))
        h = jnp.einsum('nekf,efd->nekd', h, w2)
        weighted = g[..., None] * h
        flat_idx = (m + jnp.arange(n, dtype=m.dtype)[:, None, None] * t).reshape(-1)
        out = jnp.zeros((n * t, d), dtype=jnp.float32).at[flat_idx].add(weighted.reshape(-1, d))
        out = out.reshape(n, t, d)
        return out.astype(jnp.bfloat16)

    def _L1_attn_a_ref(x, qkv_w, out_w):
        import jax, jax.numpy as jnp
        import numpy as np
        EMB = 256
        HEADS = 16
        HEAD_DIM = EMB // HEADS
        BLOCK = 64
        N_GLOBAL = 4
        WINDOW = 128
        ROPE_BASE = 10000.0

        def rotate_half(x):
            x1 = x[..., ::2]
            x2 = x[..., 1::2]
            return jnp.stack((-x2, x1), axis=-1).reshape(x.shape)

        def rope_cos_sin(seq_len, dtype=jnp.float32):
            inv_freq = 1.0 / ROPE_BASE ** (jnp.arange(0, HEAD_DIM, 2, dtype=jnp.float32) / HEAD_DIM)
            pos = jnp.arange(seq_len, dtype=jnp.float32)
            freqs = jnp.outer(pos, inv_freq)
            emb = jnp.concatenate([freqs, freqs], -1)
            return (jnp.cos(emb)[None, None].astype(dtype), jnp.sin(emb)[None, None].astype(dtype))

        def block_mask(seq_len):
            i = jnp.arange(seq_len)[:, None]
            j = jnp.arange(seq_len)[None, :]
            blk = i // BLOCK == j // BLOCK
            glob = (i < N_GLOBAL) | (j < N_GLOBAL)
            slide = jnp.abs(i - j) <= WINDOW
            return (blk | glob | slide) & (j <= i)
        B, S, E = x.shape
        scale = HEAD_DIM ** (-0.5)
        qkv = x @ qkv_w.T
        qkv = qkv.reshape(B, S, 3, HEADS, HEAD_DIM)
        qkv = jnp.transpose(qkv, (2, 0, 3, 1, 4))
        q, k, v = (qkv[0], qkv[1], qkv[2])
        cos, sin = rope_cos_sin(S, x.dtype)
        q = q * cos + rotate_half(q) * sin
        k = k * cos + rotate_half(k) * sin
        mask = block_mask(S)
        scores = jnp.einsum('bhqd,bhkd->bhqk', q, k) * scale
        scores = jnp.where(mask[None, None], scores, jnp.finfo(scores.dtype).min)
        attn = jax.nn.softmax(scores, axis=-1)
        out = jnp.einsum('bhqk,bhkd->bhqd', attn, v)
        out = jnp.transpose(out, (0, 2, 1, 3)).reshape(B, S, E)
        return out @ out_w.T

    def _L1_attn_b_ref(x, Wi, Wf, Wg, conv_i, conv_f, g_norm_weight, Wo):
        import jax, jax.numpy as jnp
        import numpy as np
        HIDDEN = 256
        EXPAND = 1
        INPUT_DIM = HIDDEN * EXPAND
        CONV_K = 4
        NORM_EPS = 1e-05

        def causal_depthwise_conv(x, w):
            B, T, D = x.shape
            K = w.shape[1]
            xp = jnp.pad(x, ((0, 0), (K - 1, 0), (0, 0)))
            out = jnp.zeros_like(x)
            for k in range(K):
                out = out + xp[:, k:k + T, :] * w[:, k]
            return out

        def hgrn_forward(x, Wi, Wf, Wg, conv_i, conv_f, g_norm_weight, Wo):
            B, T, H = x.shape
            i_raw = jnp.einsum('bth,hd->btd', x, Wi)
            f_raw = jnp.einsum('bth,hd->btd', x, Wf)
            g_raw = jnp.einsum('bth,hd->btd', x, Wg)
            i_raw = causal_depthwise_conv(i_raw, conv_i)
            f_raw = causal_depthwise_conv(f_raw, conv_f)
            forget_gate = jax.nn.sigmoid(f_raw)
            i = jax.nn.silu(i_raw) * (1.0 - forget_gate)

            def step(h, fi):
                f_t, i_t = fi
                h = f_t * h + i_t
                return (h, h)
            h0 = jnp.zeros((B, i.shape[-1]), dtype=x.dtype)
            _, o_rec = jax.lax.scan(step, h0, (forget_gate.swapaxes(0, 1), i.swapaxes(0, 1)))
            o_rec = o_rec.swapaxes(0, 1)
            rms = jax.lax.rsqrt(jnp.mean(o_rec * o_rec, axis=-1, keepdims=True) + NORM_EPS)
            o = o_rec * rms * g_norm_weight * jax.nn.silu(g_raw)
            return jnp.einsum('btd,dh->bth', o, Wo)
        return hgrn_forward(x, Wi, Wf, Wg, conv_i, conv_f, g_norm_weight, Wo)

    def _L1_ffn_ref(x, U1, V1, b1, U2, V2, b2):
        import jax, jax.numpy as jnp
        import numpy as np
        D_MODEL, D_FF, RANK = (256, 1024, 64)
        B, S = (4, 1024)
        P = jnp.einsum('bsd,dr->bsr', x, U1)
        H = jax.nn.gelu(jnp.einsum('bsr,rf->bsf', P, V1) + b1)
        Q = jnp.einsum('bsf,fr->bsr', H, U2)
        return jnp.einsum('bsr,rd->bsd', Q, V2) + b2
    x = L0_attn_a_x
    x = x + _L0_attn_a_ref(_layernorm(x, axis=-1), L0_attn_a_W_q, L0_attn_a_W_k, L0_attn_a_W_v, L0_attn_a_W_o, L0_attn_a_W_down_kv, L0_attn_a_W_up_k, L0_attn_a_W_up_v)
    x = x + _L0_ffn_ref(_layernorm(x, axis=-1), L0_ffn_gate_w, L0_ffn_w1, L0_ffn_w2)
    x = x + _L0_attn_b_ref(_layernorm(x, axis=-1), L0_attn_b_Wq, L0_attn_b_Wv, L0_attn_b_Wg, L0_attn_b_Wo, L0_attn_b_beta, L0_attn_b_ln_gamma, L0_attn_b_ln_beta)
    x = x + _L0_ffn_ref(_layernorm(x, axis=-1), L0_ffn_gate_w, L0_ffn_w1, L0_ffn_w2)
    x = x + _L1_attn_a_ref(_layernorm(x, axis=-1), L1_attn_a_qkv_w, L1_attn_a_out_w)
    x = x + _L1_ffn_ref(_layernorm(x, axis=-1), L1_ffn_U1, L1_ffn_V1, L1_ffn_b1, L1_ffn_U2, L1_ffn_V2, L1_ffn_b2)
    x = x + _L1_attn_b_ref(_layernorm(x, axis=-1), L1_attn_b_Wi, L1_attn_b_Wf, L1_attn_b_Wg, L1_attn_b_conv_i, L1_attn_b_conv_f, L1_attn_b_g_norm_weight, L1_attn_b_Wo)
    x = x + _L1_ffn_ref(_layernorm(x, axis=-1), L1_ffn_U1, L1_ffn_V1, L1_ffn_b1, L1_ffn_U2, L1_ffn_V2, L1_ffn_b2)
    return x

_drawn_inputs = setup_inputs


def setup_inputs(seed=0):
    import zlib

    import numpy as np

    out = dict(_drawn_inputs(seed))
    spreads = {'L0_attn_b_beta': (-0.20000000298023224, 0.6),
     'L0_attn_b_ln_gamma': (1.0, 0.2),
     'L0_attn_b_ln_beta': (0.0, 0.1),
     'L1_attn_b_g_norm_weight': (1.0, 0.6),
     'L1_ffn_b1': (0.0, 0.8),
     'L1_ffn_b2': (0.0, 0.604)}
    factors = {'L1_ffn_U1': 8.0,
     'L1_ffn_V1': 8.0,
     'L1_ffn_U2': 6.613,
     'L1_ffn_V2': 6.523,
     'L0_attn_a_W_q': 3.398,
     'L0_attn_a_W_up_k': 3.437,
     'L1_attn_b_Wf': 4.399,
     'L1_attn_b_conv_f': 3.837}
    for name, (base, spread) in spreads.items():
        noise = np.random.default_rng([zlib.crc32(name.encode()), seed]).standard_normal(out[name].shape)
        drawn = base * np.exp(spread * noise) if base else spread * noise
        out[name] = jnp.asarray(drawn.astype(out[name].dtype))
    for name, factor in factors.items():
        out[name] = (out[name] * factor).astype(out[name].dtype)
    return out
```

```python
import numpy as np
from contextlib import ExitStack

import concourse.bass as bass
from concourse import mybir

F32 = mybir.dt.float32
BF16 = mybir.dt.bfloat16
U32 = mybir.dt.uint32
ALU = mybir.AluOpType
ACT = mybir.ActivationFunctionType
AXX = mybir.AxisListType.X
ds = bass.ds

P = 128
B, T, D = 4, 1024, 256
NT = B * T // P
TB = T // P
DC = D // P
G = 4
GT = G * P
NG = NT // G
H, HD = 16, 16
EPS = 1e-5
START = 4


class Phase:

    def __init__(self, nc, ctx, name):
        self.nc, self.ctx, self.name = nc, ctx, name
        self.sems, self.dma_sems, self.all_sems = [], [], []
        ctx.callback(self.finish)

    def sb(self, name, shape, dt=F32):
        return self.ctx.enter_context(self.nc.sbuf_tensor(f"{self.name}_{name}", shape, dt))

    def ps(self, name, shape, dt=F32):
        return self.ctx.enter_context(self.nc.psum_tensor(f"{self.name}_{name}", shape, dt))

    def sem(self, name):
        s = self.nc.alloc_semaphore(f"{self.name}_{name}")
        self.sems.append(s)
        self.all_sems.append(s)
        return s

    def dma_sem(self, name, start=0):
        s = self.nc.alloc_semaphore(f"{self.name}_{name}")
        self.all_sems.append(s)
        if start:
            self.dma_sems.append((s, start))
        return s

    def finish(self):
        if self.all_sems:
            self.nc.clear_and_free_semaphores(self.all_sems)
            self.nc.all_engine_barrier()

    def start(self, eng):
        for s in self.sems:
            eng.sem_inc(s, START)
        for s, n in self.dma_sems:
            eng.sem_inc(s, n)


class LayerNorm:

    def __init__(self, ph, X, ident, hT, ps_t, h_out=None):
        self.nc, self.X, self.ident, self.hT, self.ps_t, self.h_out = ph.nc, X, ident, hT, ps_t, h_out
        self.st = ph.sb("ln_st", [P, G, 6])
        self.mv = ph.sb("ln_mv", [P, G, 2])
        self.ve = ph.sb("ln_ve", [P, G])
        self.mhalf = ph.sb("ln_mhalf", [P, G])
        self.eps = ph.sb("ln_eps", [P, G])
        self.rstd = ph.sb("ln_rstd", [P, G])
        self.h = ph.sb("ln_h", [P, G, D])
        self.moments = ph.sem("ln_moments")
        self.veps = ph.sem("ln_veps")
        self.rs = ph.sem("ln_rs")
        self.hrow = ph.sem("ln_hrow")
        self.trans = ph.sem("ln_trans")
        self.hTok = ph.sem("ln_hT")

    def pool_setup(self):
        self.nc.gpsimd.memset(self.eps[:, :], EPS)
        self.nc.gpsimd.memset(self.mhalf[:, :], -0.5).then_inc(self.rs, 1)

    def vector(self, v, g):
        for j in range(G):
            self.nc.vector.bn_stats(self.st[:, j, :], self.X[:, ds(g * G + j, 1), :])
        v.drain()
        for j in range(G):
            self.nc.vector.bn_aggr(self.mv[:, j, :], self.st[:, j, :]).then_inc(self.moments, 1)
        v.wait_ge(self.rs, START + g + 2)
        v.wait_ge(self.trans, START + g * DC)
        for j in range(G):
            self.nc.vector.tensor_scalar(self.h[:, j, :], self.X[:, ds(g * G + j, 1), :], self.mv[:, j, 0:1],
                                         self.rstd[:, j:j + 1], ALU.subtract, ALU.mult).then_inc(self.hrow, 1)

    def pool(self, p, g):
        p.wait_ge(self.moments, START + (g + 1) * G)
        self.nc.gpsimd.tensor_tensor(self.ve[:, :], self.mv[:, :, 1], self.eps[:, :], ALU.add).then_inc(self.veps, 1)
        p.wait_ge(self.veps, START + g + 1)
        p.wait_ge(self.hrow, START + g * G)
        self.nc.gpsimd.tensor_tensor(self.rstd[:, :], self.ve[:, :], self.mhalf[:, :], ALU.pow).then_inc(self.rs, 1)

    def tensor(self, t, g):
        t.wait_ge(self.hrow, START + (g + 1) * G)
        t.wait_ge(self.hTok, START + g * DC)
        for c in range(DC):
            for j in range(G):
                last = self.nc.tensor.transpose(self.ps_t[:, c, j * P:(j + 1) * P],
                                                self.h[:, j, c * P:(c + 1) * P], self.ident[:, :])
            last.then_inc(self.trans, 1)

    def scalar(self, s, g, slot=None):
        for c in range(DC):
            s.wait_ge(self.trans, START + g * DC + c + 1)
            to = self.hT[:, c, ds(g * GT, GT)] if slot is None else self.hT[:, slot, c, :]
            self.nc.scalar.copy(to, self.ps_t[:, c, :]).then_inc(self.hTok, 1)


def load_once(eng, sem, pairs):
    for dst, src in pairs:
        eng.dma_start(dst, src).then_inc(sem, 16)
    return 16 * len(pairs)


def low_rank_ffn(nc, ph, X, ident, U1, V1, b1, U2, V2, b2, ones):
    R, FF = U1.shape[1], V1.shape[1]
    M = FF // P
    hT = ph.sb("hT", [P, DC, B * T])
    u1 = ph.sb("u1", [P, DC, R])
    v1 = ph.sb("v1", [R, FF])
    bias1 = ph.sb("bias1", [P, M])
    u2 = ph.sb("u2", [P, M, R])
    v2 = ph.sb("v2", [R + 1, D])
    PT = ph.sb("PT", [R, GT])
    HT = ph.sb("HT", [P, M, GT])
    QT = ph.sb("QT", [R + 1, GT])
    ps_t = ph.ps("ps_t", [P, DC, GT])
    ps_p = ph.ps("ps_p", [P, GT])
    ps_h = ph.ps("ps_h", [P, 2, GT])
    ps_q = ph.ps("ps_q", [P, GT])
    ps_o = ph.ps("ps_o", [P, 2, GT])
    ln = LayerNorm(ph, X, ident, hT, ps_t)
    weights = ph.dma_sem("weights")
    p_mm, p_sb = ph.sem("p_mm"), ph.sem("p_sb")
    h_mm, h_sb = ph.sem("h_mm"), ph.sem("h_sb")
    q_mm, q_sb = ph.sem("q_mm"), ph.sem("q_sb")
    o_mm, o_add = ph.sem("o_mm"), ph.sem("o_add")
    pairs = [(u1[:, :, :], U1.rearrange("(c p) r -> p c r", p=P)), (v1[:, :], V1),
             (bias1[:, :], b1.rearrange("(m p) -> p m", p=P)),
             (u2[:, :, :], U2.rearrange("(m p) r -> p m r", p=P)), (v2[0:R, :], V2),
             (v2[R:R + 1, :], b2.rearrange("(a d) -> a d", a=1)), (QT[R:R + 1, :], ones[0:1, 0:GT])]
    loaded = 16 * len(pairs)

    with nc.Block() as block:
        @block.sync
        def _(sp):
            ph.start(sp)
            with nc.allow_non_contiguous_dma(reason="a bias laid out over partitions"):
                load_once(sp, weights, pairs)
            sp.wait_ge(weights, loaded)

        @block.gpsimd
        def _(pool):
            ln.pool_setup()
            pool.wait_ge(ln.rs, START + 1)
            with pool.Fori(0, NG) as g:
                ln.pool(pool, g)

        @block.vector
        def _(dve):
            def add(g):
                for k in range(G // 2):
                    dve.wait_ge(o_mm, START + g * (G // 2) + k + 1)
                    x2 = X[:, ds(g * G + 2 * k, 2), :]
                    nc.vector.tensor_tensor(x2, ps_o[:, k, :].rearrange("p (j d) -> p j d", j=2), x2,
                                            ALU.add).then_inc(o_add, 1)
            ln.vector(dve, 0)
            with dve.Fori(0, NG - 1) as g:
                ln.vector(dve, g + 1)
                add(g)
            add(NG - 1)

        @block.scalar
        def _(act):
            act.wait_ge(weights, loaded)

            def turn(g, last):
                act.wait_ge(p_mm, START + g + 1)
                nc.scalar.copy(PT[:, :], ps_p[0:R, :]).then_inc(p_sb, 1)
                if not last:
                    ln.scalar(act, g + 1)
                for m in range(M):
                    act.wait_ge(h_mm, START + g * M + m + 1)
                    if m == 0:
                        act.wait_ge(q_mm, START + g)
                    nc.scalar.activation(HT[:, m, :], ps_h[:, m % 2, :], ACT.Gelu_apprx_tanh,
                                         bias=bias1[:, m:m + 1]).then_inc(h_sb, 1)
                act.wait_ge(q_mm, START + g + 1)
                act.wait_ge(o_mm, START + g * (G // 2))
                nc.scalar.copy(QT[0:R, :], ps_q[0:R, :]).then_inc(q_sb, 1)
            ln.scalar(act, 0)
            with act.Fori(0, NG - 1) as g:
                turn(g, False)
            turn(NG - 1, True)

        @block.tensor
        def _(pe):
            pe.wait_ge(weights, loaded)

            def down(g, m):
                pe.wait_ge(h_sb, START + g * M + m + 1)
                i = nc.tensor.matmul(ps_q[0:R, :], u2[:, m, :], HT[:, m, :], start=(m == 0), stop=(m == M - 1))
                if m == M - 1:
                    i.then_inc(q_mm, 1)

            def turn(g, last):
                pe.wait_ge(ln.hTok, START + (g + 1) * DC)
                for c in range(DC):
                    i = nc.tensor.matmul(ps_p[0:R, :], u1[:, c, :], hT[:, c, ds(g * GT, GT)],
                                         start=(c == 0), stop=(c == DC - 1))
                i.then_inc(p_mm, 1)
                if not last:
                    ln.tensor(pe, g + 1)
                pe.wait_ge(p_sb, START + g + 1)
                pe.wait_ge(q_sb, START + g)
                for m in range(M + 1):
                    if m < M:
                        if m >= 2:
                            pe.wait_ge(h_sb, START + g * M + m - 1)
                        nc.tensor.matmul(ps_h[:, m % 2, :], v1[:, m * P:(m + 1) * P], PT[:, :],
                                         start=True, stop=True).then_inc(h_mm, 1)
                    if m:
                        down(g, m - 1)
                pe.wait_ge(q_sb, START + g + 1)
                pe.wait_ge(o_add, START + g * (G // 2))
                for k in range(G // 2):
                    for j in (2 * k, 2 * k + 1):
                        i = nc.tensor.matmul(ps_o[:, k, (j % 2) * D:(j % 2 + 1) * D], QT[:, j * P:(j + 1) * P],
                                             v2[:, :], start=True, stop=True)
                    i.then_inc(o_mm, 1)
            ln.tensor(pe, 0)
            with pe.Fori(0, NG - 1) as g:
                turn(g, False)
            turn(NG - 1, True)


def retention(nc, ph, X, ident, a):
    hT = ph.sb("hT", [P, DC, B * T])
    wq, wv, wg, wo = (ph.sb(n, [P, DC, D]) for n in ("wq", "wv", "wg", "wo"))
    mean_w = ph.sb("mean_w", [P, P])
    beta_in, lam = ph.sb("beta_in", [P, DC]), ph.sb("lam", [P, DC])
    gamma, shift = ph.sb("gamma", [P, DC]), ph.sb("shift", [P, DC])
    eps = ph.sb("eps", [P, 1])
    S = ph.sb("S", [P, DC, GT])
    carry = ph.sb("carry", [P, DC])
    Y, SQ = ph.sb("Y", [P, DC, GT]), ph.sb("SQ", [P, DC, GT])
    gate = ph.sb("gate", [P, DC, GT])
    Z = ph.sb("Z", [P, DC, GT])
    sd, rstd = ph.sb("sd", [P, GT]), ph.sb("rstd", [P, GT])
    ps_t = ph.ps("ps_t", [P, DC, GT])
    ps_v = ph.ps("ps_v", [P, DC, GT])
    ps_q = ph.ps("ps_q", [P, DC, GT])
    ps_m, ps_r = ph.ps("ps_m", [P, GT]), ph.ps("ps_r", [P, GT])
    ln = LayerNorm(ph, X, ident, hT, ps_t)
    weights = ph.dma_sem("weights")
    consts = ph.sem("consts")
    v_mm, scan = ph.sem("v_mm"), ph.sem("scan")
    q_mm, y_ok = ph.sem("q_mm"), ph.sem("y_ok")
    g_mm, gate_ok = ph.sem("g_mm"), ph.sem("gate_ok")
    m_mm, d_ok = ph.sem("m_mm"), ph.sem("d_ok")
    sq_ok, r_mm = ph.sem("sq_ok"), ph.sem("r_mm")
    sd_ok, z_ok = ph.sem("sd_ok"), ph.sem("z_ok")
    o_mm, o_add = ph.sem("o_mm"), ph.sem("o_add")
    part = lambda w: w.rearrange("(c p) n -> p c n", p=P)
    col = lambda w: w.rearrange("(c p) -> p c", p=P)
    pairs = [(wv[:, :, :], part(a["WvT"])), (wq[:, :, :], part(a["WqT"])), (wg[:, :, :], part(a["WgT"])),
             (wo[:, :, :], part(a["WoT"])), (beta_in[:, :], col(a["beta_rows"])),
             (gamma[:, :], col(a["L0_attn_b_ln_gamma"])), (shift[:, :], col(a["L0_attn_b_ln_beta"]))]
    loaded = 16 * len(pairs)
    HB = T // GT

    with nc.Block() as block:
        @block.sync
        def _(sp):
            ph.start(sp)
            with nc.allow_non_contiguous_dma(reason="vectors laid out over partitions"):
                load_once(sp, weights, pairs)
            sp.wait_ge(weights, loaded)

        @block.gpsimd
        def _(pool):
            ln.pool_setup()
            pool.wait_ge(ln.rs, START + 1)
            with pool.Fori(0, NG) as g:
                ln.pool(pool, g)

        @block.vector
        def _(dve):
            nc.vector.memset(eps[:, :], EPS)
            nc.vector.memset(mean_w[:, :], 1.0 / D).then_inc(consts, 1)
            ln.vector(dve, 0)
            dve.wait_ge(consts, START + 2)

            def turn(b, h, last):
                g = b * HB + h
                dve.wait_ge(z_ok, START + g * DC)
                for c in range(DC):
                    dve.wait_ge(v_mm, START + g * DC + c + 1)
                    nc.vector.tensor_tensor_scan(S[:, c, :], lam[:, c:c + 1].to_broadcast([P, GT]), ps_v[:, c, :],
                                                 0.0 if h == 0 else carry[:, c:c + 1],
                                                 ALU.mult, ALU.add).then_inc(scan, 1)
                for c in range(DC):
                    dve.wait_ge(q_mm, START + g * DC + c + 1)
                    dve.wait_ge(scan, START + g * DC + c + 1)
                    nc.vector.tensor_tensor(Y[:, c, :], ps_q[:, c, :], S[:, c, :], ALU.mult).then_inc(y_ok, 1)
                nc.vector.tensor_copy(carry[:, :], S[:, :, GT - 1])
                if not last:
                    ln.vector(dve, g + 1)
                dve.wait_ge(m_mm, START + g + 1)
                for c in range(DC):
                    nc.vector.tensor_tensor(Y[:, c, :], Y[:, c, :], ps_m[:, :], ALU.subtract).then_inc(d_ok, 1)
                dve.wait_ge(sd_ok, START + g + 1)
                nc.vector.reciprocal(rstd[:, :], sd[:, :])
                dve.drain()
                for c in range(DC):
                    nc.vector.scalar_tensor_tensor(Z[:, c, :], Y[:, c, :], gamma[:, c:c + 1], rstd[:, :],
                                                   ALU.mult, ALU.mult)
                dve.drain()
                dve.wait_ge(gate_ok, START + (g + 1) * DC)
                for c in range(DC):
                    nc.vector.scalar_tensor_tensor(Z[:, c, :], Z[:, c, :], shift[:, c:c + 1], gate[:, c, :],
                                                   ALU.add, ALU.mult).then_inc(z_ok, 1)
                for k in range(G // 2):
                    dve.wait_ge(o_mm, START + g * (G // 2) + k + 1)
                    x2 = X[:, ds(g * G + 2 * k, 2), :]
                    nc.vector.tensor_tensor(x2, ps_q[:, k, :].rearrange("p (j d) -> p j d", j=2), x2,
                                            ALU.add).then_inc(o_add, 1)
            with dve.Fori(0, B - 1) as b:
                for h in range(HB):
                    turn(b, h, False)
            for h in range(HB):
                turn(B - 1, h, h == HB - 1)

        @block.scalar
        def _(act):
            act.wait_ge(weights, loaded)
            act.wait_ge(consts, START + 1)
            nc.scalar.activation(lam[:, :], beta_in[:, :], ACT.Sigmoid).then_inc(consts, 1)
            ln.scalar(act, 0)

            def turn(g, last):
                if not last:
                    ln.scalar(act, g + 1)
                act.wait_ge(g_mm, START + g * DC + 1)
                act.wait_ge(z_ok, START + g * DC)
                for c in range(DC):
                    act.wait_ge(g_mm, START + g * DC + c + 1)
                    nc.scalar.activation(gate[:, c, :], ps_v[:, c, :], ACT.Silu).then_inc(gate_ok, 1)
                for c in range(DC):
                    act.wait_ge(d_ok, START + g * DC + c + 1)
                    nc.scalar.activation(SQ[:, c, :], Y[:, c, :], ACT.Square).then_inc(sq_ok, 1)
                act.wait_ge(r_mm, START + g + 1)
                nc.scalar.activation(sd[:, :], ps_r[:, :], ACT.Sqrt, bias=eps[:, 0:1]).then_inc(sd_ok, 1)
            with act.Fori(0, NG - 1) as g:
                turn(g, False)
            turn(NG - 1, True)

        @block.tensor
        def _(pe):
            pe.wait_ge(weights, loaded)
            pe.wait_ge(consts, START + 1)

            def project(out, w, g, done):
                for c in range(DC):
                    for k in range(DC):
                        i = nc.tensor.matmul(out[:, c, :], w[:, k, c * P:(c + 1) * P], hT[:, k, ds(g * GT, GT)],
                                             start=(k == 0), stop=(k == DC - 1))
                    i.then_inc(done, 1)

            def mean(out, src, done):
                for c in range(DC):
                    i = nc.tensor.matmul(out[:, :], mean_w[:, :], src[:, c, :], start=(c == 0), stop=(c == DC - 1))
                i.then_inc(done, 1)

            def turn(g, last):
                pe.wait_ge(ln.hTok, START + (g + 1) * DC)
                pe.wait_ge(gate_ok, START + g * DC)
                project(ps_v, wv, g, v_mm)
                pe.wait_ge(o_add, START + g * (G // 2))
                project(ps_q, wq, g, q_mm)
                pe.wait_ge(scan, START + (g + 1) * DC)
                project(ps_v, wg, g, g_mm)
                if not last:
                    ln.tensor(pe, g + 1)
                pe.wait_ge(y_ok, START + (g + 1) * DC)
                mean(ps_m, Y, m_mm)
                pe.wait_ge(sq_ok, START + (g + 1) * DC)
                mean(ps_r, SQ, r_mm)
                pe.wait_ge(z_ok, START + (g + 1) * DC)
                for k in range(G // 2):
                    for j in (2 * k, 2 * k + 1):
                        for c in range(DC):
                            i = nc.tensor.matmul(ps_q[:, k, (j % 2) * D:(j % 2 + 1) * D],
                                                 Z[:, c, j * P:(j + 1) * P], wo[:, c, :],
                                                 start=(c == 0), stop=(c == DC - 1))
                    i.then_inc(o_mm, 1)
            ln.tensor(pe, 0)
            with pe.Fori(0, NG - 1) as g:
                turn(g, False)
            turn(NG - 1, True)


def gated_recurrence(nc, ph, X, ident, a):
    K = 4
    hT = ph.sb("hT", [P, DC, B * T])
    wi, wf, wg, wo = (ph.sb(n, [P, DC, D]) for n in ("wi", "wf", "wg", "wo"))
    conv_i, conv_f = ph.sb("conv_i", [P, DC, K]), ph.sb("conv_f", [P, DC, K])
    gnorm = ph.sb("gnorm", [P, DC])
    mean_w = ph.sb("mean_w", [P, P])
    eps = ph.sb("eps", [P, 1])
    RAW = ph.sb("RAW", [P, 2, DC, K - 1 + GT])
    CV = ph.sb("CV", [P, 2, DC, GT])
    FG, OM = ph.sb("FG", [P, DC, GT]), ph.sb("OM", [P, DC, GT])
    SI = ph.sb("SI", [P, DC, GT])
    O = ph.sb("O", [P, DC, GT])
    carry = ph.sb("carry", [P, DC])
    SQ, gate, Z = (ph.sb(n, [P, DC, GT]) for n in ("SQ", "gate", "Z"))
    sd, rms = ph.sb("sd", [P, GT]), ph.sb("rms", [P, GT])
    ps_t = ph.ps("ps_t", [P, DC, GT])
    ps_i = ph.ps("ps_i", [P, DC, GT])
    ps_f = ph.ps("ps_f", [P, DC, GT])
    ps_r = ph.ps("ps_r", [P, GT])
    ln = LayerNorm(ph, X, ident, hT, ps_t)
    weights = ph.dma_sem("weights")
    consts = ph.sem("consts")
    raw_mm, raw_ok = ph.sem("raw_mm"), ph.sem("raw_ok")
    conv_ok, act_ok = ph.sem("conv_ok"), ph.sem("act_ok")
    i_ok, o_ok = ph.sem("i_ok"), ph.sem("o_ok")
    g_mm, gate_ok = ph.sem("g_mm"), ph.sem("gate_ok")
    sq_ok, r_mm, sd_ok = ph.sem("sq_ok"), ph.sem("r_mm"), ph.sem("sd_ok")
    z_ok, o_mm, o_add = ph.sem("z_ok"), ph.sem("o_mm"), ph.sem("o_add")
    part = lambda w: w.rearrange("(c p) n -> p c n", p=P)
    pairs = [(wi[:, :, :], part(a["L1_attn_b_Wi"])), (wf[:, :, :], part(a["L1_attn_b_Wf"])),
             (wg[:, :, :], part(a["L1_attn_b_Wg"])), (wo[:, :, :], part(a["L1_attn_b_Wo"])),
             (conv_i[:, :, :], part(a["L1_attn_b_conv_i"])), (conv_f[:, :, :], part(a["L1_attn_b_conv_f"])),
             (gnorm[:, :], a["L1_attn_b_g_norm_weight"].rearrange("(c p) -> p c", p=P))]
    loaded = 16 * len(pairs)
    HB = T // GT

    with nc.Block() as block:
        @block.sync
        def _(sp):
            ph.start(sp)
            with nc.allow_non_contiguous_dma(reason="vectors laid out over partitions"):
                load_once(sp, weights, pairs)
            sp.wait_ge(weights, loaded)

        @block.gpsimd
        def _(pool):
            ln.pool_setup()
            pool.wait_ge(ln.rs, START + 1)
            with pool.Fori(0, NG) as g:
                ln.pool(pool, g)

        @block.vector
        def _(dve):
            nc.vector.memset(eps[:, :], EPS)
            nc.vector.memset(mean_w[:, :], 1.0 / D).then_inc(consts, 1)
            ln.vector(dve, 0)
            dve.wait_ge(weights, loaded)

            def turn(b, h, last):
                g = b * HB + h
                dve.wait_ge(act_ok, START + g * 3 * DC)
                for s, w in ((0, conv_i), (1, conv_f)):
                    for c in range(DC):
                        dve.wait_ge(raw_ok, START + g * 2 * DC + s * DC + c + 1)
                        nc.vector.tensor_scalar(CV[:, s, c, :], RAW[:, s, c, 0:GT], w[:, c, 0:1], None, ALU.mult)
                for k in range(1, K):
                    dve.drain()
                    for s, w in ((0, conv_i), (1, conv_f)):
                        for c in range(DC):
                            i = nc.vector.scalar_tensor_tensor(CV[:, s, c, :], RAW[:, s, c, k:k + GT],
                                                               w[:, c, k:k + 1], CV[:, s, c, :], ALU.mult, ALU.add)
                            if k == K - 1:
                                i.then_inc(conv_ok, 1)
                if not last:
                    ln.vector(dve, g + 1)
                dve.wait_ge(act_ok, START + (g + 1) * 3 * DC)
                for c in range(DC):
                    nc.vector.tensor_tensor(SI[:, c, :], SI[:, c, :], OM[:, c, :], ALU.mult).then_inc(i_ok, 1)
                for c in range(DC):
                    dve.wait_ge(i_ok, START + g * DC + c + 1)
                    nc.vector.tensor_tensor_scan(O[:, c, :], FG[:, c, :], SI[:, c, :],
                                                 0.0 if h == 0 else carry[:, c:c + 1],
                                                 ALU.mult, ALU.add).then_inc(o_ok, 1)
                dve.drain()
                nc.vector.tensor_copy(carry[:, :], O[:, :, GT - 1])
                dve.wait_ge(sd_ok, START + g + 1)
                nc.vector.reciprocal(rms[:, :], sd[:, :])
                dve.drain()
                for c in range(DC):
                    nc.vector.scalar_tensor_tensor(Z[:, c, :], O[:, c, :], gnorm[:, c:c + 1], rms[:, :],
                                                   ALU.mult, ALU.mult)
                dve.drain()
                dve.wait_ge(gate_ok, START + (g + 1) * DC)
                for c in range(DC):
                    nc.vector.tensor_tensor(Z[:, c, :], Z[:, c, :], gate[:, c, :], ALU.mult).then_inc(z_ok, 1)
                for k in range(G // 2):
                    dve.wait_ge(o_mm, START + g * (G // 2) + k + 1)
                    x2 = X[:, ds(g * G + 2 * k, 2), :]
                    nc.vector.tensor_tensor(x2, ps_f[:, k, :].rearrange("p (j d) -> p j d", j=2), x2,
                                            ALU.add).then_inc(o_add, 1)
            with dve.Fori(0, B - 1) as b:
                for h in range(HB):
                    turn(b, h, False)
            for h in range(HB):
                turn(B - 1, h, h == HB - 1)

        @block.scalar
        def _(act):
            act.wait_ge(weights, loaded)
            act.wait_ge(consts, START + 1)
            ln.scalar(act, 0)

            def turn(b, h, last):
                g = b * HB + h
                act.wait_ge(conv_ok, START + g * 2 * DC)
                for s, ps in ((0, ps_i), (1, ps_f)):
                    for c in range(DC):
                        if h == 0:
                            nc.scalar.memzero(RAW[:, s, c, 0:K - 1])
                        else:
                            nc.scalar.copy(RAW[:, s, c, 0:K - 1], RAW[:, s, c, GT:GT + K - 1])
                act.drain()
                for s, ps in ((0, ps_i), (1, ps_f)):
                    for c in range(DC):
                        act.wait_ge(raw_mm, START + g * 2 * DC + s * DC + c + 1)
                        nc.scalar.copy(RAW[:, s, c, K - 1:], ps[:, c, :]).then_inc(raw_ok, 1)
                if not last:
                    ln.scalar(act, g + 1)
                act.wait_ge(z_ok, START + g * DC)
                for c in range(DC):
                    act.wait_ge(g_mm, START + g * DC + c + 1)
                    nc.scalar.activation(gate[:, c, :], ps_i[:, c, :], ACT.Silu).then_inc(gate_ok, 1)
                act.wait_ge(conv_ok, START + (g + 1) * 2 * DC)
                for c in range(DC):
                    nc.scalar.activation(SI[:, c, :], CV[:, 0, c, :], ACT.Silu).then_inc(act_ok, 1)
                for c in range(DC):
                    nc.scalar.activation(FG[:, c, :], CV[:, 1, c, :], ACT.Sigmoid).then_inc(act_ok, 1)
                act.wait_ge(act_ok, START + (g + 1) * 3 * DC - DC)
                for c in range(DC):
                    nc.scalar.activation(OM[:, c, :], FG[:, c, :], ACT.Copy, bias=1.0, scale=-1.0).then_inc(act_ok, 1)
                for c in range(DC):
                    act.wait_ge(o_ok, START + g * DC + c + 1)
                    nc.scalar.activation(SQ[:, c, :], O[:, c, :], ACT.Square).then_inc(sq_ok, 1)
                act.wait_ge(r_mm, START + g + 1)
                nc.scalar.activation(sd[:, :], ps_r[:, :], ACT.Sqrt, bias=eps[:, 0:1]).then_inc(sd_ok, 1)
            with act.Fori(0, B - 1) as b:
                for h in range(HB):
                    turn(b, h, False)
            for h in range(HB):
                turn(B - 1, h, h == HB - 1)

        @block.tensor
        def _(pe):
            pe.wait_ge(weights, loaded)
            pe.wait_ge(consts, START + 1)

            def project(out, w, g, done):
                for c in range(DC):
                    for k in range(DC):
                        i = nc.tensor.matmul(out[:, c, :], w[:, k, c * P:(c + 1) * P], hT[:, k, ds(g * GT, GT)],
                                             start=(k == 0), stop=(k == DC - 1))
                    i.then_inc(done, 1)

            def turn(g, last):
                pe.wait_ge(ln.hTok, START + (g + 1) * DC)
                pe.wait_ge(gate_ok, START + g * DC)
                project(ps_i, wi, g, raw_mm)
                pe.wait_ge(o_add, START + g * (G // 2))
                project(ps_f, wf, g, raw_mm)
                pe.wait_ge(raw_ok, START + g * 2 * DC + DC)
                project(ps_i, wg, g, g_mm)
                if not last:
                    ln.tensor(pe, g + 1)
                pe.wait_ge(sq_ok, START + (g + 1) * DC)
                for c in range(DC):
                    i = nc.tensor.matmul(ps_r[:, :], mean_w[:, :], SQ[:, c, :], start=(c == 0), stop=(c == DC - 1))
                i.then_inc(r_mm, 1)
                pe.wait_ge(z_ok, START + (g + 1) * DC)
                for k in range(G // 2):
                    for j in (2 * k, 2 * k + 1):
                        for c in range(DC):
                            i = nc.tensor.matmul(ps_f[:, k, (j % 2) * D:(j % 2 + 1) * D],
                                                 Z[:, c, j * P:(j + 1) * P], wo[:, c, :],
                                                 start=(c == 0), stop=(c == DC - 1))
                    i.then_inc(o_mm, 1)
            ln.tensor(pe, 0)
            with pe.Fori(0, NG - 1) as g:
                turn(g, False)
            turn(NG - 1, True)


def expert_ffn(nc, ph, X, ident, a):
    E, FF = a["L0_ffn_w1"].shape[0], a["L0_ffn_w1"].shape[2]
    KT = 2 * T // E
    C = KT // P
    R = B * E
    M = FF // P
    h_rows = nc.dram_tensor(f"{ph.name}_h_rows", (B * T, D), F32, kind="Internal").ap()
    acc = nc.dram_tensor(f"{ph.name}_acc", (B * T, D), F32, kind="Internal").ap()
    idxT = ph.sb("idxT", [P, C, R], U32)
    gT = ph.sb("gT", [P, C, R])
    with ExitStack() as own:
        route(nc, Phase(nc, own, ph.name + "r"), X, ident, a, E, R, C, KT, h_rows, acc, idxT, gT)
    with ExitStack() as own:
        experts(nc, Phase(nc, own, ph.name + "e"), ident, a, E, C, M, h_rows, acc, idxT, gT)
    with ExitStack() as own:
        add_rounded(nc, Phase(nc, own, ph.name + "a"), X, acc)


def route(nc, ph, X, ident, a, E, R, C, KT, h_rows, acc, idxT, gT):
    hT = ph.sb("hT", [P, DC, B * T])
    gate_w = ph.sb("gate_w", [P, DC, E])
    base = ph.sb("base", [R, 1])
    zeros = ph.sb("zeros", [P, G, D])
    scT = ph.sb("scT", [E, B * T])
    sc, ex, pr = (ph.sb(n, [P, TB, B, E]) for n in ("sc", "ex", "pr"))
    mx, sm, rc = (ph.sb(n, [P, TB, B]) for n in ("mx", "sm", "rc"))
    PR = [ph.sb(f"PR{i}", [R, T]) for i in range(2)]
    vals, idx = ph.sb("vals", [R, KT]), ph.sb("idx", [R, KT], U32)
    rowf = ph.sb("rowf", [R, KT])
    ps_t = ph.ps("ps_t", [P, DC, GT])
    ps_s = ph.ps("ps_s", [P, GT])
    ps_x = ph.ps("ps_x", [P, TB, B, E])
    ps_p = ph.ps("ps_p", [P, 2, GT])
    ps_i = ph.ps("ps_i", [P, 2, C, R])
    ln = LayerNorm(ph, X, ident, hT, ps_t)
    weights, rows_out, zeroed = ph.dma_sem("weights"), ph.dma_sem("rows_out"), ph.dma_sem("zeroed")
    zeros_ok = ph.sem("zeros_ok")
    s_mm, s_sb = ph.sem("s_mm"), ph.sem("s_sb")
    x_tr, x_ok, e_ok, p_ok = ph.sem("x_tr"), ph.sem("x_ok"), ph.sem("e_ok"), ph.sem("p_ok")
    p_tr, p_sb, top_ok = ph.sem("p_tr"), ph.sem("p_sb"), ph.sem("top_ok")
    i_tr, i_ok = ph.sem("i_tr"), ph.sem("i_ok")

    with nc.Block() as block:
        @block.sync
        def _(sp):
            ph.start(sp)
            sp.dma_start(gate_w[:, :, :], a["L0_ffn_gate_w"].rearrange("(c p) e -> p c e", p=P)).then_inc(weights, 16)
            sp.dma_start(base[:, :], a["batch_base"]).then_inc(weights, 16)
            sp.wait_ge(zeros_ok, START + 1)
            for g in range(NG):
                sp.dma_start(acc[g * GT:(g + 1) * GT, :].rearrange("(j p) d -> p j d", p=P),
                             zeros[:, :, :]).then_inc(zeroed, 16)
            with sp.Fori(0, NG) as g:
                sp.wait_ge(ln.hrow, START + (g + 1) * G)
                sp.dma_start(h_rows[ds(g * GT, GT), :].rearrange("(j p) d -> p j d", p=P),
                             ln.h[:, :, :]).then_inc(rows_out, 16)
            sp.wait_ge(rows_out, 16 * NG)
            sp.wait_ge(zeroed, 16 * NG)

        @block.gpsimd
        def _(pool):
            ln.pool_setup()
            pool.wait_ge(ln.rs, START + 1)
            with pool.Fori(0, NG) as g:
                ln.pool(pool, g)

        @block.vector
        def _(dve):
            nc.vector.memset(zeros[:, :, :], 0.0).then_inc(zeros_ok, 1)
            ln.vector(dve, 0)
            with dve.Fori(1, NG) as g:
                dve.wait_ge(rows_out, 16 * g)
                ln.vector(dve, g)
            wide = lambda m: m[:, :, :].rearrange("p j b -> p (j b)").unsqueeze(2).to_broadcast([P, TB * B, E])
            flat = lambda m: m[:, :, :, :].rearrange("p j b e -> p (j b) e")
            dve.wait_ge(x_tr, START + 1)
            nc.vector.tensor_copy(flat(sc), flat(ps_x))
            dve.drain()
            nc.vector.tensor_reduce(mx[:, :, :].rearrange("p j b -> p (j b)"), flat(sc), AXX, ALU.max)
            dve.drain()
            nc.vector.tensor_tensor(flat(sc), flat(sc), wide(mx), ALU.subtract).then_inc(x_ok, 1)
            dve.wait_ge(e_ok, START + 1)
            nc.vector.tensor_reduce(sm[:, :, :].rearrange("p j b -> p (j b)"), flat(ex), AXX, ALU.add)
            dve.drain()
            nc.vector.reciprocal(rc[:, :, :], sm[:, :, :])
            dve.drain()
            nc.vector.tensor_tensor(flat(pr), flat(ex), wide(rc), ALU.mult).then_inc(p_ok, 1)
            dve.wait_ge(p_sb, START + 2)
            dve.wait_ge(weights, 32)
            for r in range(KT // 8):
                now, after, eight = PR[r % 2], PR[(r + 1) % 2], slice(8 * r, 8 * r + 8)
                nc.vector.max(vals[:, eight], now[:, :])
                dve.drain()
                nc.vector.max_index(idx[:, eight], vals[:, eight], now[:, :])
                if r < KT // 8 - 1:
                    nc.vector.match_replace(after[:, :], vals[:, eight], now[:, :], -1.0)
                dve.drain()
            nc.vector.tensor_copy(rowf[:, :], idx[:, :])
            dve.drain()
            nc.vector.tensor_scalar(rowf[:, :], rowf[:, :], base[:, 0:1], None, ALU.add).then_inc(top_ok, 1)
            dve.wait_ge(i_tr, START + 1)
            nc.vector.tensor_copy(idxT[:, :, :], ps_i[:, 0, :, :]).then_inc(i_ok, 1)
            nc.vector.tensor_copy(gT[:, :, :], ps_i[:, 1, :, :]).then_inc(i_ok, 1)

        @block.scalar
        def _(act):
            with act.Fori(0, NG) as g:
                ln.scalar(act, g)
                act.wait_ge(s_mm, START + g + 1)
                nc.scalar.copy(scT[:, ds(g * GT, GT)], ps_s[0:E, :]).then_inc(s_sb, 1)
            act.wait_ge(x_ok, START + 1)
            nc.scalar.activation(ex[:, :, :, :], sc[:, :, :, :], ACT.Exp).then_inc(e_ok, 1)
            for k in range(2):
                act.wait_ge(p_tr, START + k + 1)
                nc.scalar.copy(PR[0][:, k * GT:(k + 1) * GT], ps_p[0:R, k, :]).then_inc(p_sb, 1)

        @block.tensor
        def _(pe):
            pe.wait_ge(weights, 32)
            with pe.Fori(0, NG) as g:
                ln.tensor(pe, g)
                pe.wait_ge(ln.hTok, START + (g + 1) * DC)
                pe.wait_ge(s_sb, START + g)
                for c in range(DC):
                    i = nc.tensor.matmul(ps_s[0:E, :], gate_w[:, c, :], hT[:, c, ds(g * GT, GT)],
                                         start=(c == 0), stop=(c == DC - 1))
                i.then_inc(s_mm, 1)
            pe.wait_ge(s_sb, START + NG)
            for b in range(B):
                for j in range(TB):
                    i = nc.tensor.transpose(ps_x[:, j, b, :], scT[:, (b * TB + j) * P:(b * TB + j + 1) * P],
                                            ident[0:E, 0:E])
            i.then_inc(x_tr, 1)
            pe.wait_ge(p_ok, START + 1)
            for j in range(TB):
                i = nc.tensor.transpose(ps_p[0:R, j // G, (j % G) * P:(j % G + 1) * P],
                                        pr[:, j, :, :].rearrange("p b e -> p (b e)"), ident[:, :])
                if j % G == G - 1:
                    i.then_inc(p_tr, 1)
            pe.wait_ge(top_ok, START + 1)
            for s, src in enumerate((rowf, vals)):
                for c in range(C):
                    i = nc.tensor.transpose(ps_i[:, s, c, :], src[:, c * P:(c + 1) * P], ident[0:R, 0:R])
            i.then_inc(i_tr, 1)


def experts(nc, ph, ident, a, E, C, M, h_rows, acc, idxT, gT):
    HV = 2
    BH = B // HV
    w1 = [ph.sb(f"w1_{i}", [P, DC, M * P]) for i in range(2)]
    w2 = [ph.sb(f"w2_{i}", [P, M, D]) for i in range(2)]
    cols = ph.sb("cols", [P, B, C], U32)
    xg = ph.sb("xg", [P, HV, G, D])
    xgT = ph.sb("xgT", [P, HV, DC, GT])
    HT = ph.sb("HT", [P, HV, M, GT])
    ys = ph.sb("ys", [P, HV, G, D])
    ps_t = ph.ps("ps_t", [P, DC, GT])
    ps_h = ph.ps("ps_h", [P, 2, GT])
    ps_o = ph.ps("ps_o", [P, 2, GT])
    loads = [ph.dma_sem(f"loads{i}") for i in range(2)]
    gathered = [ph.dma_sem(f"gathered{v}") for v in range(HV)]
    added = [ph.dma_sem(f"added{v}") for v in range(HV)]
    cols_ok, tr, xT_ok = ph.sem("cols_ok"), ph.sem("tr"), ph.sem("xT_ok")
    h_mm, h_sb, o_mm, y_ok = ph.sem("h_mm"), ph.sem("h_sb"), ph.sem("o_mm"), ph.sem("y_ok")
    passed = ph.sem("passed")
    EP = E // 2
    cells = lambda t, e: t[:, :, :].rearrange("p c (b e) -> p b c e", e=E)[:, :, :, ds(e, 1)]

    with nc.Block() as block:
        @block.sync
        def _(sp):
            ph.start(sp)

            def load(ep, s):
                sp.dma_start(w1[s][:, :, :], a["L0_ffn_w1"][ds(ep * 2 + s, 1), :, :].rearrange(
                    "a (c p) f -> p (a c) f", p=P)).then_inc(loads[s], 16)
                sp.dma_start(w2[s][:, :, :], a["L0_ffn_w2"][ds(ep * 2 + s, 1), :, :].rearrange(
                    "a (m p) d -> p (a m) d", p=P)).then_inc(loads[s], 16)
            for s in range(2):
                load(0, s)
            with sp.Fori(1, EP) as ep:
                for s in range(2):
                    sp.wait_ge(o_mm, START + (ep * 2 + s - 1) * 2 * HV)
                    load(ep, s)
            sp.wait_ge(added[0], 16 * G * E)
            sp.wait_ge(added[1], 16 * G * E)

        @block.gpsimd
        def _(pool):
            def gather(e, v):
                pool.wait_ge(tr, START + HV * (e - 1) + v + 1)
                pool.sem_inc(passed, 1)
                rows(v)

            def rows(v):
                for k in range(G):
                    pool.indirect_dma_start(out=xg[:, v, k, :], out_offset=None, in_=h_rows[:, :],
                                            in_offset=bass.IndirectOffsetOnAxis(
                                                ap=cols[:, BH * v + k // C, k % C:k % C + 1], axis=0)
                                            ).then_inc(gathered[v], 16)

            def scatter(e, v, first=False):
                if not first:
                    pool.wait_ge(added[v], 16 * G * e)
                for k in range(G):
                    pool.wait_ge(y_ok, START + (e * HV + v) * G + k + 1)
                    pool.sem_inc(passed, 1)
                    pool.indirect_dma_start(out=acc[:, :], out_offset=bass.IndirectOffsetOnAxis(
                                                ap=keep[:, BH * v + k // C, k % C:k % C + 1], axis=0),
                                            in_=ys[:, v, k, :], in_offset=None,
                                            compute_op=ALU.add).then_inc(added[v], 16)
            keep = ph.sb("keep", [P, B, C], U32)

            nc.gpsimd.tensor_copy(cols[:, :, :].unsqueeze(3), cells(idxT, 0)).then_inc(cols_ok, 1)
            pool.wait_ge(cols_ok, START + 1)
            for v in range(HV):
                rows(v)
            def step(e, first):
                for v in range(HV):
                    pool.wait_ge(gathered[v], 16 * G * (e + 1))
                    if not first:
                        pool.wait_ge(added[v], 16 * G * e)
                pool.sem_inc(passed, 1)
                nc.gpsimd.tensor_copy(keep[:, :, :], cols[:, :, :]).then_inc(cols_ok, 1)
                pool.wait_ge(cols_ok, START + 2 * e + 2)
                pool.sem_inc(passed, 1)
                nc.gpsimd.tensor_copy(cols[:, :, :].unsqueeze(3), cells(idxT, e + 1)).then_inc(cols_ok, 1)
                pool.wait_ge(cols_ok, START + 2 * e + 3)
                pool.sem_inc(passed, 1)
                for v in range(HV):
                    gather(e + 1, v)
                    scatter(e, v, first)
            step(0, True)
            with pool.Fori(1, E - 1) as e:
                step(e, False)
            for v in range(HV):
                pool.wait_ge(gathered[v], 16 * G * E)
                pool.wait_ge(added[v], 16 * G * (E - 1))
            nc.gpsimd.tensor_copy(keep[:, :, :], cols[:, :, :]).then_inc(cols_ok, 1)
            pool.wait_ge(cols_ok, START + 2 * E)
            for v in range(HV):
                scatter(E - 1, v)

        @block.vector
        def _(dve):
            def weigh(e, first):
                for v in range(HV):
                    if not first:
                        dve.wait_ge(added[v], 16 * G * e)
                    for k in range(G):
                        if k % 2 == 0:
                            dve.wait_ge(o_mm, START + (e * HV + v) * 2 + k // 2 + 1)
                        b, c = BH * v + k // C, k % C
                        nc.vector.tensor_scalar(ys[:, v, k, :], ps_o[:, k // 2, (k % 2) * D:(k % 2 + 1) * D],
                                                gT[:, c, ds(b * E + e, 1)], None, ALU.mult).then_inc(y_ok, 1)
            weigh(0, True)
            with dve.Fori(1, E) as e:
                weigh(e, False)

        @block.scalar
        def _(act):
            def transposed(i, v):
                act.wait_ge(tr, START + i + 1)
                for c in range(DC):
                    nc.scalar.copy(xgT[:, v, c, :], ps_t[:, c, :]).then_inc(xT_ok, 1)

            def hidden(i, v):
                for m in range(M):
                    act.wait_ge(h_mm, START + i * M + m + 1)
                    nc.scalar.activation(HT[:, v, m, :], ps_h[:, m % 2, :], ACT.Gelu_apprx_tanh).then_inc(h_sb, 1)
            transposed(0, 0)
            with act.Fori(0, E - 1) as e:
                for v in range(HV):
                    hidden(e * HV + v, v)
                    transposed(e * HV + v + 1, (v + 1) % HV)
            hidden((E - 1) * HV, 0)
            transposed((E - 1) * HV + 1, 1)
            hidden((E - 1) * HV + 1, 1)

        @block.tensor
        def _(pe):
            def transposes(e, i, v):
                pe.wait_ge(gathered[v], 16 * G * (e + 1))
                pe.wait_ge(xT_ok, START + i * DC)
                for c in range(DC):
                    for k in range(G):
                        x = nc.tensor.transpose(ps_t[:, c, k * P:(k + 1) * P], xg[:, v, k, c * P:(c + 1) * P],
                                                ident[:, :])
                x.then_inc(tr, 1)

            def products(ep, s, v, last):
                e = ep * 2 + s
                i = e * HV + v
                pe.wait_ge(xT_ok, START + (i + 1) * DC)
                if v == 0:
                    pe.wait_ge(loads[s], 32 * (ep + 1))
                for m in range(M):
                    if m >= 2:
                        pe.wait_ge(h_sb, START + i * M + m - 1)
                    for c in range(DC):
                        x = nc.tensor.matmul(ps_h[:, m % 2, :], w1[s][:, c, m * P:(m + 1) * P], xgT[:, v, c, :],
                                             start=(c == 0), stop=(c == DC - 1))
                    x.then_inc(h_mm, 1)
                if not last:
                    transposes(ep * 2 + s + (1 if v else 0), i + 1, (v + 1) % HV)
                pe.wait_ge(h_sb, START + (i + 1) * M)
                pe.wait_ge(y_ok, START + i * G)
                for k in range(G):
                    for m in range(M):
                        x = nc.tensor.matmul(ps_o[:, k // 2, (k % 2) * D:(k % 2 + 1) * D],
                                             HT[:, v, m, k * P:(k + 1) * P], w2[s][:, m, :],
                                             start=(m == 0), stop=(m == M - 1))
                    if k % 2:
                        x.then_inc(o_mm, 1)
            transposes(0, 0, 0)
            with pe.Fori(0, EP - 1) as ep:
                for s in range(2):
                    for v in range(HV):
                        products(ep, s, v, False)
            for s in range(2):
                for v in range(HV):
                    products(EP - 1, s, v, s == 1 and v == HV - 1)


def add_rounded(nc, ph, X, acc):
    A = ph.sb("A", [P, NG, G, D])
    A16 = ph.sb("A16", [P, NG, G, D], BF16)
    loads = [ph.dma_sem(f"loads{g}") for g in range(NG)]
    rounded = ph.sem("rounded")
    with nc.Block() as block:
        @block.sync
        def _(sp):
            ph.start(sp)
            for g in range(NG):
                sp.dma_start(A[:, g, :, :], acc[g * GT:(g + 1) * GT, :].rearrange("(j p) d -> p j d", p=P)
                             ).then_inc(loads[g], 16)

        @block.vector
        def _(dve):
            for g in range(NG):
                dve.wait_ge(loads[g], 16)
                nc.vector.tensor_copy(A16[:, g, :, :], A[:, g, :, :]).then_inc(rounded, 1)
                dve.wait_ge(rounded, START + g + 1)
                nc.vector.tensor_tensor(X[:, g * G:(g + 1) * G, :], X[:, g * G:(g + 1) * G, :], A16[:, g, :, :],
                                        ALU.add)


PARTS = 3
PAIRS = [(0, 0), (1, 0), (2, 0), (0, 1), (1, 1), (0, 2)]
STACK = len(PAIRS) * HD


def attention(nc, ph, X, ident, a, kind):
    parts = nc.dram_tensor(f"{ph.name}_parts", (2, PARTS, B * D, T), BF16, kind="Internal").ap()
    V = ph.sb("V", [P, B, H, TB, HD + 1])
    with ExitStack() as own:
        if kind == "decay":
            project_latent(nc, Phase(nc, own, ph.name + "p"), X, ident, a, parts, V)
        else:
            project_rotary(nc, Phase(nc, own, ph.name + "p"), X, ident, a, parts, V)
    AO = ph.sb("AO", [P, B, TB, H, HD])
    with ExitStack() as own:
        if kind == "decay":
            heads_decay(nc, Phase(nc, own, ph.name + "h"), ident, a, parts, V, AO)
        else:
            heads(nc, Phase(nc, own, ph.name + "h"), ident, a, parts, V, AO, kind)
    with ExitStack() as own:
        project_out(nc, Phase(nc, own, ph.name + "o"), X, ident,
                    a["L0_attn_a_W_o"] if kind == "decay" else a["out_wT"], AO)


class Split:

    def __init__(self, ph, parts):
        self.nc, self.parts = ph.nc, parts
        self.F = ph.sb("sp_F", [P, 2, DC, GT])
        self.R = ph.sb("sp_R", [P, 2, DC, GT])
        self.out = [ph.sb(f"sp_{n}", [P, 2, DC, GT], BF16) for n in range(PARTS)]
        self.f_ok = ph.sem("sp_f")
        self.first, self.rest = ph.sem("sp_first"), ph.sem("sp_rest")
        self.second, self.third = ph.sem("sp_second"), ph.sem("sp_third")
        self.written = ph.dma_sem("sp_written", 16)

    def scalar(self, act, g):
        act.wait_ge(self.written, 16 + 16 * 2 * PARTS * g)
        act.wait_ge(self.f_ok, START + 2 * g + 2)
        self.nc.scalar.copy(self.out[0][:, :, :, :], self.F[:, :, :, :]).then_inc(self.first, 1)
        act.wait_ge(self.rest, START + g + 1)
        self.nc.scalar.copy(self.out[1][:, :, :, :], self.R[:, :, :, :]).then_inc(self.second, 1)

    def vector(self, dve, g):
        dve.wait_ge(self.first, START + g + 1)
        dve.wait_ge(self.third, START + g)
        self.nc.vector.tensor_tensor(self.R[:, :, :, :], self.F[:, :, :, :], self.out[0][:, :, :, :],
                                     ALU.subtract).then_inc(self.rest, 1)

    def pool(self, pool, g):
        pool.wait_ge(self.second, START + g + 1)
        self.nc.gpsimd.tensor_tensor(self.out[2][:, :, :, :], self.R[:, :, :, :], self.out[1][:, :, :, :],
                                     ALU.subtract).then_inc(self.third, 1)

    def sync(self, sp, b, h, g):
        for n, done in enumerate((self.first, self.second, self.third)):
            sp.wait_ge(done, START + g + 1)
            for s in range(2):
                sp.dma_start(self.parts[s, n, ds(b * D, D), h * GT:(h + 1) * GT].rearrange("(c p) t -> p c t", p=P),
                             self.out[n][:, s, :, :]).then_inc(self.written, 16)


def project_latent(nc, ph, X, ident, a, parts, V):
    DL = a["L0_attn_a_W_down_kv"].shape[1]
    HB = T // GT
    hT = ph.sb("hT", [P, DC, B * T])
    wq = ph.sb("wq", [P, DC, D])
    wkT, wvT = ph.sb("wkT", [P, DC, D]), ph.sb("wvT", [P, DC, D])
    wd = ph.sb("wd", [P, DC, DL])
    wuk, wuv = ph.sb("wuk", [DL, D]), ph.sb("wuv", [DL, D])
    wlat = ph.sb("wlat", [P, DC, DL])
    latT = ph.sb("latT", [DL, GT])
    ps_t = ph.ps("ps_t", [P, DC, GT])
    ps_q = ph.ps("ps_q", [P, DC, GT])
    ps_k = ph.ps("ps_k", [P, DC, GT])
    ps_l = ph.ps("ps_l", [P, GT])
    ps_v = ph.ps("ps_v", [P, 2, D])
    ln = LayerNorm(ph, X, ident, hT, ps_t)
    split = Split(ph, parts)
    weights = ph.dma_sem("weights")
    consts, wl_mm = ph.sem("consts"), ph.sem("wl_mm")
    q_mm, k_mm, l_mm, l_ok = ph.sem("q_mm"), ph.sem("k_mm"), ph.sem("l_mm"), ph.sem("l_ok")
    v_mm, v_ok = ph.sem("v_mm"), ph.sem("v_ok")
    part = lambda w: w.rearrange("(c p) n -> p c n", p=P)
    pairs = [(wkT[:, :, :], part(a["WkT"])), (wvT[:, :, :], part(a["WvT_a"])), (wq[:, :, :], part(a["L0_attn_a_W_q"])),
             (wd[:, :, :], part(a["L0_attn_a_W_down_kv"])), (wuk[:, :], a["L0_attn_a_W_up_k"]),
             (wuv[:, :], a["L0_attn_a_W_up_v"])]
    loaded = 16 * len(pairs)

    with nc.Block() as block:
        @block.sync
        def _(sp):
            ph.start(sp)
            load_once(sp, weights, pairs)
            with sp.Fori(0, B) as b:
                for h in range(HB):
                    split.sync(sp, b, h, b * HB + h)
            sp.wait_ge(split.written, 16 + 16 * 2 * PARTS * NG)

        @block.gpsimd
        def _(pool):
            ln.pool_setup()
            pool.wait_ge(ln.rs, START + 1)
            nc.gpsimd.memset(V[:, :, :, :, HD], 1.0)
            ln.pool(pool, 0)
            with pool.Fori(0, NG - 1) as g:
                ln.pool(pool, g + 1)
                split.pool(pool, g)
            split.pool(pool, NG - 1)

        @block.vector
        def _(dve):
            dve.wait_ge(weights, loaded)
            nc.vector.tensor_tensor(wkT[:, :, :], wkT[:, :, :], wvT[:, :, :], ALU.add).then_inc(consts, 1)
            ln.vector(dve, 0)
            dve.wait_ge(wl_mm, START + 1)
            nc.vector.tensor_copy(wlat[:, :, :], ps_q[:, 0, 0:DC * DL].rearrange("p (c n) -> p c n", c=DC)
                                  ).then_inc(consts, 1)

            def turn(b, h, last):
                g = b * HB + h
                if not last:
                    ln.vector(dve, g + 1)
                for k in range(G // 2):
                    dve.wait_ge(v_mm, START + g * (G // 2) + k + 1)
                    for j in range(2):
                        nc.vector.tensor_copy(V[:, ds(b, 1), :, h * G + 2 * k + j, 0:HD],
                                              ps_v[:, j, :].rearrange("p (a h d) -> p a h d", h=H, a=1)
                                              ).then_inc(v_ok, 1)
                split.vector(dve, g)
            with dve.Fori(0, B - 1) as b:
                for h in range(HB):
                    turn(b, h, False)
            for h in range(HB):
                turn(B - 1, h, h == HB - 1)

        @block.scalar
        def _(act):
            def turn(g, last):
                act.wait_ge(l_mm, START + g + 1)
                act.wait_ge(v_mm, START + g * (G // 2))
                nc.scalar.copy(latT[:, :], ps_l[0:DL, :]).then_inc(l_ok, 1)
                act.wait_ge(split.third, START + g)
                act.wait_ge(q_mm, START + g + 1)
                nc.scalar.copy(split.F[:, 0, :, :], ps_q[:, :, :]).then_inc(split.f_ok, 1)
                act.wait_ge(k_mm, START + g + 1)
                nc.scalar.copy(split.F[:, 1, :, :], ps_k[:, :, :]).then_inc(split.f_ok, 1)
                if not last:
                    ln.scalar(act, g + 1)
                split.scalar(act, g)
            ln.scalar(act, 0)
            with act.Fori(0, NG - 1) as g:
                turn(g, False)
            turn(NG - 1, True)

        @block.tensor
        def _(pe):
            pe.wait_ge(weights, loaded)
            pe.wait_ge(consts, START + 1)
            for c in range(DC):
                for k in range(DC):
                    i = nc.tensor.matmul(ps_q[:, 0, c * DL:(c + 1) * DL], wkT[:, k, c * P:(c + 1) * P],
                                         wd[:, k, :], start=(k == 0), stop=(k == DC - 1))
            i.then_inc(wl_mm, 1)
            pe.wait_ge(consts, START + 2)

            def turn(g, last):
                pe.wait_ge(ln.hTok, START + (g + 1) * DC)
                pe.wait_ge(l_ok, START + g)
                for k in range(DC):
                    i = nc.tensor.matmul(ps_l[0:DL, :], wlat[:, k, :], hT[:, k, ds(g * GT, GT)],
                                         start=(k == 0), stop=(k == DC - 1))
                i.then_inc(l_mm, 1)
                pe.wait_ge(split.f_ok, START + 2 * g)
                for c in range(DC):
                    for k in range(DC):
                        i = nc.tensor.matmul(ps_q[:, c, :], wq[:, k, c * P:(c + 1) * P], hT[:, k, ds(g * GT, GT)],
                                             start=(k == 0), stop=(k == DC - 1))
                i.then_inc(q_mm, 1)
                pe.wait_ge(l_ok, START + g + 1)
                for c in range(DC):
                    i = nc.tensor.matmul(ps_k[:, c, :], wuk[:, c * P:(c + 1) * P], latT[:, :], start=True, stop=True)
                i.then_inc(k_mm, 1)
                for k in range(G // 2):
                    pe.wait_ge(v_ok, START + g * G + 2 * k)
                    for j in range(2):
                        t = (2 * k + j) * P
                        i = nc.tensor.matmul(ps_v[:, j, :], latT[:, t:t + P], wuv[:, :], start=True, stop=True)
                    i.then_inc(v_mm, 1)
                if not last:
                    ln.tensor(pe, g + 1)
            ln.tensor(pe, 0)
            with pe.Fori(0, NG - 1) as g:
                turn(g, False)
            turn(NG - 1, True)


def project_rotary(nc, ph, X, ident, a, parts, V):
    HB = T // GT
    hT = ph.sb("hT", [P, 2, DC, GT])
    w = ph.sb("w", [P, DC, 3 * D])
    wr = ph.sb("wr", [P, DC, 2 * D])
    cos, sin = ph.sb("cos", [P, T]), ph.sb("sin", [P, T])
    AB = ph.sb("AB", [P, 2, 2, DC, GT])
    ps_t = ph.ps("ps_t", [P, DC, GT])
    ps_q, ps_r = ph.ps("ps_q", [P, DC, GT]), ph.ps("ps_r", [P, DC, GT])
    ps_v = ph.ps("ps_v", [P, 2, D])
    ln = LayerNorm(ph, X, ident, hT, ps_t)
    split = Split(ph, parts)
    weights = ph.dma_sem("weights")
    consts, r_mm, ab_ok = ph.sem("consts"), ph.sem("r_mm"), ph.sem("ab_ok")
    v_mm, v_ok = ph.sem("v_mm"), ph.sem("v_ok")
    pairs = [(w[:, :, :], a["qkv_wT"].rearrange("(c p) n -> p c n", p=P)), (cos[:, :], a["cos"]), (sin[:, :], a["sin"])]
    loaded = 16 * len(pairs)

    with nc.Block() as block:
        @block.sync
        def _(sp):
            ph.start(sp)
            load_once(sp, weights, pairs)
            with sp.Fori(0, B) as b:
                for h in range(HB):
                    split.sync(sp, b, h, b * HB + h)
            sp.wait_ge(split.written, 16 + 16 * 2 * PARTS * NG)

        @block.gpsimd
        def _(pool):
            ln.pool_setup()
            pool.wait_ge(ln.rs, START + 1)
            nc.gpsimd.memset(V[:, :, :, :, HD], 1.0)
            ln.pool(pool, 0)

            def turn(g, last):
                pool.wait_ge(split.third, START + g)
                for s in range(2):
                    pool.wait_ge(ab_ok, START + 2 * g + s + 1)
                    nc.gpsimd.tensor_tensor(split.F[:, s, :, :], AB[:, s, 0, :, :], AB[:, s, 1, :, :],
                                            ALU.add).then_inc(split.f_ok, 1)
                if not last:
                    ln.pool(pool, g + 1)
                split.pool(pool, g)
            with pool.Fori(0, NG - 1) as g:
                turn(g, False)
            turn(NG - 1, True)

        @block.vector
        def _(dve):
            dve.wait_ge(weights, loaded)
            pair = lambda t: t[:, :, 0:2 * D].rearrange("p c (n two) -> p c n two", two=2)
            nc.vector.tensor_scalar(pair(wr)[:, :, :, 0], pair(w)[:, :, :, 1], -1.0, None, ALU.mult).then_inc(consts, 1)
            nc.vector.tensor_copy(pair(wr)[:, :, :, 1], pair(w)[:, :, :, 0]).then_inc(consts, 1)
            ln.vector(dve, 0)

            def turn(b, h, last):
                g = b * HB + h
                both = lambda t: t[:, h * GT:(h + 1) * GT].unsqueeze(1).to_broadcast([P, DC, GT])
                for s in range(2):
                    dve.wait_ge(split.f_ok, START + 2 * g + s - 1)
                    dve.wait_ge(r_mm, START + 2 * g + s + 1)
                    nc.vector.tensor_tensor(AB[:, s, 0, :, :], ps_q[:, :, :], both(cos), ALU.mult)
                    nc.vector.tensor_tensor(AB[:, s, 1, :, :], ps_r[:, :, :], both(sin), ALU.mult).then_inc(ab_ok, 1)
                if not last:
                    ln.vector(dve, g + 1)
                for k in range(G // 2):
                    dve.wait_ge(v_mm, START + g * (G // 2) + k + 1)
                    for j in range(2):
                        nc.vector.tensor_copy(V[:, ds(b, 1), :, h * G + 2 * k + j, 0:HD],
                                              ps_v[:, j, :].rearrange("p (a h d) -> p a h d", h=H, a=1)
                                              ).then_inc(v_ok, 1)
                split.vector(dve, g)
            with dve.Fori(0, B - 1) as b:
                for h in range(HB):
                    turn(b, h, False)
            for h in range(HB):
                turn(B - 1, h, h == HB - 1)

        @block.scalar
        def _(act):
            def turn(g, h, last):
                if not last:
                    ln.scalar(act, g + 1, (h + 1) % 2)
                split.scalar(act, g)
            ln.scalar(act, 0, 0)
            with act.Fori(0, B - 1) as b:
                for h in range(HB):
                    turn(b * HB + h, h, False)
            for h in range(HB):
                turn((B - 1) * HB + h, h, h == HB - 1)

        @block.tensor
        def _(pe):
            pe.wait_ge(weights, loaded)
            pe.wait_ge(consts, START + 2)

            def turn(g, h, last):
                pe.wait_ge(ln.hTok, START + (g + 1) * DC)
                for s in range(2):
                    pe.wait_ge(ab_ok, START + 2 * g + s)
                    for out, weight in ((ps_q, w), (ps_r, wr)):
                        for c in range(DC):
                            for k in range(DC):
                                n = s * D + c * P
                                i = nc.tensor.matmul(out[:, c, :], weight[:, k, n:n + P], hT[:, h, k, :],
                                                     start=(k == 0), stop=(k == DC - 1))
                    i.then_inc(r_mm, 1)
                for k in range(G // 2):
                    pe.wait_ge(v_ok, START + g * G + 2 * k)
                    for j in range(2):
                        t = (2 * k + j) * P
                        for c in range(DC):
                            i = nc.tensor.matmul(ps_v[:, j, :], hT[:, h, c, t:t + P], w[:, c, 2 * D:3 * D],
                                                 start=(c == 0), stop=(c == DC - 1))
                    i.then_inc(v_mm, 1)
                if not last:
                    ln.tensor(pe, g + 1)
            ln.tensor(pe, 0)
            with pe.Fori(0, B - 1) as b:
                for h in range(HB):
                    turn(b * HB + h, h, False)
            for h in range(HB):
                turn((B - 1) * HB + h, h, h == HB - 1)


def heads_decay(nc, ph, ident, a, parts, V, AO):
    qs = [ph.sb(f"qs{i}", [STACK, T], BF16) for i in range(2)]
    ks = [ph.sb(f"ks{i}", [STACK, T], BF16) for i in range(2)]
    table = ph.sb("table", [P, 2 * T - P])
    gather = ph.sb("gather", [P, HD + 1])
    NBUF = 4
    SD = [ph.sb(f"SD{i}", [P, T]) for i in range(NBUF)]
    PM = [ph.sb(f"PM{i}", [P, T]) for i in range(NBUF)]
    PT = [ph.sb(f"PT{i}", [P, TB, GT]) for i in range(2)]
    W = 32
    Vs = [ph.sb(f"Vs{i}", [P, TB, W]) for i in range(2)]
    OT = ph.sb("OT", [P, GT])
    U = 2 * TB
    mx, nb = ph.sb("mx", [P, U]), ph.sb("nb", [P, U])
    minus, rc = ph.sb("minus", [P, 1]), ph.sb("rc", [P, G])
    ps_s = [ph.ps(f"ps_s{i}", [P, 2, GT]) for i in range(2)]
    ps_t = ph.ps("ps_t", [P, 2, GT])
    ps_v, ps_o = ph.ps("ps_v", [P, GT]), ph.ps("ps_o", [P, GT])
    tabled = ph.dma_sem("tabled")
    loads = [ph.dma_sem(f"loads{i}") for i in range(2)]
    s_mm, m_ok, nb_ok, e_ok = ph.sem("s_mm"), ph.sem("m_ok"), ph.sem("nb_ok"), ph.sem("e_ok")
    ta_mm, tb_mm, ta_ok, tb_ok = ph.sem("ta_mm"), ph.sem("tb_mm"), ph.sem("ta_ok"), ph.sem("tb_ok")
    pv_mm, ot_ok, o_mm, n_ok = ph.sem("pv_mm"), ph.sem("ot_ok"), ph.sem("o_mm"), ph.sem("n_ok")
    passed, minus_ok, vs_ok = ph.sem("passed"), ph.sem("minus_ok"), ph.sem("vs_ok")
    NP = B * H // 2
    ND = 2 * len(PAIRS)
    UH = U // G

    with nc.Block() as block:
        @block.sync
        def _(sp):
            ph.start(sp)
            sp.dma_start(table[:, :], a["decay"]).then_inc(tabled, 16)
            sp.dma_start(gather[:, :], a["gather"]).then_inc(tabled, 16)

            def load(n, s):
                rows = ds(n * HD, HD)
                for r, both in enumerate(PAIRS):
                    for which, (st, part) in enumerate(zip((qs[s], ks[s]), both)):
                        sp.dma_start(st[r * HD:(r + 1) * HD, :], parts[which, part, rows, :]).then_inc(loads[s], 16)
            load(0, 0)
            load(1, 1)
            with sp.Fori(1, NP) as pr:
                for s in range(2):
                    sp.wait_ge(s_mm, START + (pr * 2 + s - 1) * TB)
                    load(pr * 2 + s, s)

        @block.gpsimd
        def _(pool):
            Vn = V[:, :, :, :, :].rearrange("p b h t d -> p (b h) t d")
            for s in range(2):
                nc.gpsimd.memset(Vs[s][:, :, :], 0.0).then_inc(minus_ok, 1)
            nc.gpsimd.memset(minus[:, :], -1.0).then_inc(minus_ok, 1)
            pool.wait_ge(minus_ok, START + 3)
            with pool.Fori(0, NP) as pr:
                for u in range(U):
                    if u % TB == 1:
                        s = u // TB
                        pool.wait_ge(pv_mm, START + (pr * 2 + s) * 2 - 2)
                        pool.sem_inc(passed, 1)
                        nc.gpsimd.tensor_copy(Vs[s][:, :, 0:HD + 1],
                                              Vn[:, ds(pr * 2 + s, 1), :, :].rearrange("p a t d -> p (a t) d")
                                              ).then_inc(vs_ok, 1)
                    pool.wait_ge(m_ok, START + pr * U + u + 1)
                    nc.gpsimd.tensor_tensor(nb[:, u:u + 1], mx[:, u:u + 1], minus[:, :], ALU.mult).then_inc(nb_ok, 1)

        @block.vector
        def _(dve):
            dve.wait_ge(tabled, 32)

            def most(i, u):
                dve.wait_ge(s_mm, START + i + 1)
                dve.wait_ge(e_ok, START + i + 1 - NBUF)
                dve.sem_inc(passed, 1)
                t = u % TB
                nc.vector.tensor_tensor_reduce(SD[u % NBUF][:, :],
                                               ps_s[u % 2][:, :, :].rearrange("p a n -> p (a n)"),
                                               table[:, (TB - 1 - t) * P:(TB - 1 - t) * P + T], 1.0, -3e38,
                                               ALU.mult, ALU.max, accum_out=mx[:, u:u + 1]).then_inc(m_ok, 1)

            def copy(i, u):
                dve.wait_ge(ta_mm, START + i + 1)
                q = u % G * P
                nc.vector.tensor_copy(PT[u // G % 2][:, 0:G, q:q + P],
                                      ps_t[:, 0, :].rearrange("p (k q) -> p k q", k=G)).then_inc(ta_ok, 1)

            def norm(n, half, hh):
                dve.wait_ge(o_mm, START + hh + 1)
                o = ps_o[:, 0:G * (HD + 1)].rearrange("p (t d) -> p t d", t=G)
                nc.vector.reciprocal(rc[:, :], o[:, :, HD])
                dve.drain()
                to = AO[:, ds(n // H, 1), half * G:(half + 1) * G, ds(n % H, 1), :].rearrange("p b t h d -> p (b t h) d")
                nc.vector.tensor_tensor(to, o[:, :, 0:HD],
                                        rc[:, :].unsqueeze(2).to_broadcast([P, G, HD]), ALU.mult).then_inc(n_ok, 1)

            def turn(pr, first, last):
                for u in range(U):
                    i = pr * U + u
                    if not (last and u >= U - 2):
                        most(i + 2, (u + 2) % U)
                    copy(i, u)
                    if u % G == 0 and not (first and u < 2 * G):
                        v = u // G - 2
                        norm(pr * 2 + v // 2, v % 2, pr * UH + v)
            most(0, 0)
            most(1, 1)
            turn(0, True, False)
            with dve.Fori(1, NP - 1) as pr:
                turn(pr, False, False)
            turn(NP - 1, False, True)
            norm(NP * 2 - 1, 0, NP * UH - 2)
            norm(NP * 2 - 1, 1, NP * UH - 1)

        @block.scalar
        def _(act):
            def exp(i, u):
                act.wait_ge(nb_ok, START + i + 1)
                act.wait_ge(tb_mm, START + i + 1 - NBUF)
                nc.scalar.activation(PM[u % NBUF][:, :], SD[u % NBUF][:, :], ACT.Exp, bias=nb[:, u:u + 1]
                                     ).then_inc(e_ok, 1)

            def copy(i, u):
                act.wait_ge(tb_mm, START + i + 1)
                q = u % G * P
                nc.scalar.copy(PT[u // G % 2][:, G:, q:q + P],
                               ps_t[:, 1, :].rearrange("p (k q) -> p k q", k=G)).then_inc(tb_ok, 1)

            def collect(hh):
                act.wait_ge(pv_mm, START + hh + 1)
                nc.scalar.copy(OT[:, :], ps_v[:, :]).then_inc(ot_ok, 1)

            def turn(pr, first, last):
                for u in range(U):
                    i = pr * U + u
                    if not (last and u == U - 1):
                        exp(i + 1, (u + 1) % U)
                    copy(i, u)
                    if u % G == 2 and not (first and u < G):
                        collect(pr * UH + u // G - 1)
            exp(0, 0)
            turn(0, True, False)
            with act.Fori(1, NP - 1) as pr:
                turn(pr, False, False)
            turn(NP - 1, False, True)
            collect(NP * UH - 1)

        @block.tensor
        def _(pe):
            pe.wait_ge(tabled, 32)

            def scores(i, u):
                s, t = u // TB, u % TB
                pe.wait_ge(m_ok, START + i - 1)
                for k in range(2):
                    x = nc.tensor.matmul(ps_s[u % 2][:, k, :], qs[s][:, t * P:(t + 1) * P],
                                         ks[s][:, k * GT:(k + 1) * GT], start=True, stop=True)
                x.then_inc(s_mm, 1)

            def transposes(i, u):
                pe.wait_ge(e_ok, START + i + 1)
                for bank, out, done in ((0, ta_ok, ta_mm), (1, tb_ok, tb_mm)):
                    pe.wait_ge(out, START + i)
                    for k in range(G):
                        at = (bank * G + k) * P
                        x = nc.tensor.transpose(ps_t[:, bank, k * P:(k + 1) * P], PM[u % NBUF][:, at:at + P],
                                                ident[:, :])
                    x.then_inc(done, 1)

            def values(n, hh, v, r, i):
                if r == 0:
                    pe.wait_ge(ta_ok, START + i)
                    pe.wait_ge(tb_ok, START + i)
                    pe.wait_ge(ot_ok, START + hh)
                    if v % 2 == 0:
                        pe.wait_ge(vs_ok, START + n + 1)
                for j in range(G):
                    x = nc.tensor.matmul(ps_v[j * W:(j + 1) * W, :], Vs[v // 2][:, 2 * j + r, :],
                                         PT[v % 2][:, 2 * j + r, :], start=(r == 0), stop=(r == 1),
                                         tile_position=(0, j * W))
                if r == 1:
                    x.then_inc(pv_mm, 1)

            def gathered(hh):
                pe.wait_ge(ot_ok, START + hh + 1)
                pe.wait_ge(n_ok, START + hh)
                for t in range(G):
                    x = nc.tensor.matmul(ps_o[:, t * (HD + 1):(t + 1) * (HD + 1)], OT[:, t * P:(t + 1) * P],
                                         gather[:, :], start=True, stop=True)
                x.then_inc(o_mm, 1)

            def turn(pr, first, last):
                for u in range(U):
                    i = pr * U + u
                    if not (last and u >= U - 3):
                        if u == U - 3:
                            pe.wait_ge(loads[0], 16 * ND * (pr + 2))
                        if u == TB - 3:
                            pe.wait_ge(loads[1], 16 * ND * (pr + 1))
                        scores(i + 3, (u + 3) % U)
                    transposes(i, u)
                    if first and u < G:
                        continue
                    v, r = u // G - 1, u % G
                    if r < 2:
                        values(pr * 2 + v // 2, pr * UH + v, v % UH, r, pr * U + u - r)
                    if r == 3:
                        gathered(pr * UH + v)
            pe.wait_ge(loads[0], 16 * ND)
            scores(0, 0)
            scores(1, 1)
            scores(2, 2)
            turn(0, True, False)
            with pe.Fori(1, NP - 1) as pr:
                turn(pr, False, False)
            turn(NP - 1, False, True)
            for r in range(2):
                values(NP * 2 - 1, NP * UH - 1, UH - 1, r, NP * U)
            gathered(NP * UH - 1)


def heads(nc, ph, ident, a, parts, V, AO, kind):
    decay = kind == "decay"
    WK = T if decay else 2 * P + 4
    WT = 2 * T - P if decay else 3 * WK
    table = ph.sb("table", [P, WT])
    qs = [ph.sb(f"qs{i}", [STACK, T], BF16) for i in range(2)]
    ks = [ph.sb(f"ks{i}", [STACK, T], BF16) for i in range(2)]
    NBUF = 4
    SD = [ph.sb(f"SD{i}", [P, WK]) for i in range(NBUF)]
    PM = [ph.sb(f"PM{i}", [P, WK]) for i in range(NBUF)]
    HALF = G * P if decay else P
    PT = [ph.sb(f"PT{i}", [P, TB if decay else 3, P]) for i in range(2)]
    U = 2 * TB
    mx, nb = ph.sb("mx", [P, U]), ph.sb("nb", [P, U])
    minus, rc = ph.sb("minus", [P, 1]), ph.sb("rc", [P, TB])
    ps_s = [ph.ps(f"ps_s{i}", [P, 2, GT]) for i in range(2)]
    ps_t = ph.ps("ps_t", [P, 2, GT])
    ps_o = [ph.ps(f"ps_o{i}", [P, GT]) for i in range(2)]
    tabled = ph.dma_sem("tabled")
    loads = [ph.dma_sem(f"loads{i}") for i in range(2)]
    s_mm, m_ok, nb_ok, e_ok = ph.sem("s_mm"), ph.sem("m_ok"), ph.sem("nb_ok"), ph.sem("e_ok")
    ta_mm, tb_mm, ta_ok, tb_ok = ph.sem("ta_mm"), ph.sem("tb_mm"), ph.sem("ta_ok"), ph.sem("tb_ok")
    pv_mm, n_ok, passed = ph.sem("pv_mm"), ph.sem("n_ok"), ph.sem("passed")
    minus_ok = ph.sem("minus_ok")
    NP = B * H // 2
    ND = 2 * len(PAIRS)

    def keys(t):
        if decay:
            return [(0, GT), (GT, GT)]
        if t == 0:
            return [(0, P)]
        return [((t - 1) * P, 2 * P)] + ([(0, 4)] if t >= 2 else [])

    def width(t):
        return sum(n for _, n in keys(t))

    def factor(t):
        if decay:
            return table[:, (TB - 1 - t) * P:(TB - 1 - t) * P + T]
        return table[:, min(t, 2) * WK:min(t, 2) * WK + width(t)]

    def scores_of(i):
        flat = ps_s[i % 2][:, :, :].rearrange("p a n -> p (a n)")
        return flat[:, 0:width(i % TB)]

    def blocks(t):
        if decay:
            return [(k * P, P, k) for k in range(TB)]
        if t == 0:
            return [(0, P, 0)]
        return [(0, P, t - 1), (P, P, t)] + ([(2 * P, 4, 0)] if t >= 2 else [])

    with nc.Block() as block:
        @block.sync
        def _(sp):
            ph.start(sp)
            sp.dma_start(table[:, :], a["decay"] if decay else a["masks"]).then_inc(tabled, 16)

            def load(n, s):
                rows = ds(n * HD, HD)
                for r, both in enumerate(PAIRS):
                    for which, (st, part) in enumerate(zip((qs[s], ks[s]), both)):
                        sp.dma_start(st[r * HD:(r + 1) * HD, :], parts[which, part, rows, :]).then_inc(loads[s], 16)
            load(0, 0)
            load(1, 1)
            with sp.Fori(1, NP) as pr:
                for s in range(2):
                    sp.wait_ge(s_mm, START + (pr * 2 + s - 1) * TB)
                    load(pr * 2 + s, s)

        @block.gpsimd
        def _(pool):
            nc.gpsimd.memset(minus[:, :], -1.0).then_inc(minus_ok, 1)
            pool.wait_ge(minus_ok, START + 1)
            with pool.Fori(0, NP) as pr:
                for u in range(U):
                    pool.wait_ge(m_ok, START + pr * U + u + 1)
                    nc.gpsimd.tensor_tensor(nb[:, u:u + 1], mx[:, u:u + 1], minus[:, :], ALU.mult).then_inc(nb_ok, 1)

        @block.vector
        def _(dve):
            dve.wait_ge(tabled, 16)

            def most(i, u):
                dve.wait_ge(s_mm, START + i + 1)
                dve.wait_ge(e_ok, START + i + 1 - NBUF)
                dve.sem_inc(passed, 1)
                t = u % TB
                nc.vector.tensor_tensor_reduce(SD[u % NBUF][:, 0:width(t)], scores_of(u), factor(t),
                                               1.0 if decay else HD ** -0.5, -3e38,
                                               ALU.mult if decay else ALU.add, ALU.max,
                                               accum_out=mx[:, u:u + 1]).then_inc(m_ok, 1)

            def copy(i, u):
                dve.wait_ge(ta_mm, START + i + 1)
                n = G if decay else 1
                nc.vector.tensor_copy(PT[u % 2][:, 0:n, :], ps_t[:, 0, 0:n * P].rearrange("p (k q) -> p k q", k=n)
                                      ).then_inc(ta_ok, 1)

            def norm(n, s):
                dve.wait_ge(pv_mm, START + n + 1)
                o = ps_o[s][:, 0:TB * (HD + 1)].rearrange("p (t d) -> p t d", t=TB)
                nc.vector.reciprocal(rc[:, :], o[:, :, HD])
                dve.drain()
                to = AO[:, ds(n // H, 1), :, ds(n % H, 1), :].rearrange("p b t h d -> p (b t h) d")
                nc.vector.tensor_tensor(to, o[:, :, 0:HD],
                                        rc[:, :].unsqueeze(2).to_broadcast([P, TB, HD]), ALU.mult).then_inc(n_ok, 1)

            def turn(pr, first, last):
                for u in range(U):
                    i = pr * U + u
                    if not (last and u >= U - 2):
                        most(i + 2, (u + 2) % U)
                    copy(i, u)
                    if u == 1 and not first:
                        norm(pr * 2 - 1, 1)
                    if u == TB + 1:
                        norm(pr * 2, 0)
                if last:
                    norm(pr * 2 + 1, 1)
            most(0, 0)
            most(1, 1)
            turn(0, True, False)
            with dve.Fori(1, NP - 1) as pr:
                turn(pr, False, False)
            turn(NP - 1, False, True)

        @block.scalar
        def _(act):
            def exp(i, u):
                act.wait_ge(nb_ok, START + i + 1)
                act.wait_ge(tb_mm, START + i + 1 - NBUF)
                n = width(u % TB)
                nc.scalar.activation(PM[u % NBUF][:, 0:n], SD[u % NBUF][:, 0:n], ACT.Exp, bias=nb[:, u:u + 1]
                                     ).then_inc(e_ok, 1)

            def copy(i, u):
                act.wait_ge(tb_mm, START + i + 1)
                t = u % TB
                if decay:
                    nc.scalar.copy(PT[u % 2][:, G:, :], ps_t[:, 1, :].rearrange("p (k q) -> p k q", k=G)
                                   ).then_inc(tb_ok, 1)
                elif t == 0:
                    act.sem_inc(tb_ok, 1)
                else:
                    if t >= 2:
                        nc.scalar.copy(PT[u % 2][0:4, 2, :], ps_t[0:4, 1, P:2 * P])
                    nc.scalar.copy(PT[u % 2][:, 1, :], ps_t[:, 1, 0:P]).then_inc(tb_ok, 1)

            def turn(pr, last):
                for u in range(U):
                    i = pr * U + u
                    if not (last and u == U - 1):
                        exp(i + 1, (u + 1) % U)
                    copy(i, u)
            exp(0, 0)
            with act.Fori(0, NP - 1) as pr:
                turn(pr, False)
            turn(NP - 1, True)

        @block.tensor
        def _(pe):
            def scores(i, u):
                s, t = u // TB, u % TB
                pe.wait_ge(m_ok, START + i - 1)
                at = 0
                flat = ps_s[u % 2][:, :, :].rearrange("p a n -> p (a n)")
                for k0, n in keys(t):
                    x = nc.tensor.matmul(flat[:, at:at + n], qs[s][:, t * P:(t + 1) * P], ks[s][:, k0:k0 + n],
                                         start=True, stop=True)
                    at += n
                x.then_inc(s_mm, 1)

            def transposes(i, u):
                t = u % TB
                pe.wait_ge(e_ok, START + i + 1)
                pe.wait_ge(ta_ok, START + i)
                for at, n, _ in blocks(t):
                    bank = at // HALF if decay else min(at // HALF, 1)
                    if at == HALF:
                        x.then_inc(ta_mm, 1)
                        pe.wait_ge(tb_ok, START + i)
                    to = at - bank * HALF
                    x = nc.tensor.transpose(ps_t[0:n, bank, to:to + P], PM[u % NBUF][:, at:at + n], ident[:, :])
                if len(blocks(t)) == 1:
                    x.then_inc(ta_mm, 1)
                    pe.wait_ge(tb_ok, START + i)
                    x = nc.tensor.transpose(ps_t[0:4, 1, 0:P], PM[u % NBUF][:, 0:4], ident[:, :])
                x.then_inc(tb_mm, 1)

            def values(i, u, n):
                s, t = u // TB, u % TB
                if t == 0:
                    pe.wait_ge(n_ok, START + n - 1)
                pe.wait_ge(ta_ok, START + i + 1)
                pe.wait_ge(tb_ok, START + i + 1)
                todo = blocks(t)
                for j, (at, rows, kt) in enumerate(todo):
                    x = nc.tensor.matmul(ps_o[s][:, t * (HD + 1):(t + 1) * (HD + 1)], PT[u % 2][0:rows, j, :],
                                         Vn[0:rows, ds(n, 1), kt, :].rearrange("p a d -> p (a d)"),
                                         start=(j == 0), stop=(j == len(todo) - 1))
                if t == TB - 1:
                    x.then_inc(pv_mm, 1)
            Vn = V[:, :, :, :, :].rearrange("p b h t d -> p (b h) t d")

            def turn(pr, first, last):
                for u in range(U):
                    i = pr * U + u
                    if not (last and u >= U - 3):
                        if u == U - 3:
                            pe.wait_ge(loads[0], 16 * ND * (pr + 2))
                        if u == TB - 3:
                            pe.wait_ge(loads[1], 16 * ND * (pr + 1))
                        scores(i + 3, (u + 3) % U)
                    transposes(i, u)
                    if u or not first:
                        values(i - 1, (u - 1) % U, pr * 2 + (u - 1) // TB if u else pr * 2 - 1)
            pe.wait_ge(loads[0], 16 * ND)
            scores(0, 0)
            scores(1, 1)
            scores(2, 2)
            turn(0, True, False)
            with pe.Fori(1, NP - 1) as pr:
                turn(pr, False, False)
            turn(NP - 1, False, True)
            values(NP * U - 1, U - 1, 2 * NP - 1)


def project_out(nc, ph, X, ident, w, AO):
    wo = ph.sb("wo", [P, DC, D])
    AT = ph.sb("AT", [P, 2, DC, GT])
    ps_t = ph.ps("ps_t", [P, DC, GT])
    ps_o = ph.ps("ps_o", [P, 2, GT])
    weights = ph.dma_sem("weights")
    tr, at_ok, o_mm, o_add = ph.sem("tr"), ph.sem("at_ok"), ph.sem("o_mm"), ph.sem("o_add")
    HC = H // DC
    with nc.Block() as block:
        @block.sync
        def _(sp):
            ph.start(sp)
            sp.dma_start(wo[:, :, :], w.rearrange("(c p) n -> p c n", p=P)).then_inc(weights, 16)

        @block.scalar
        def _(act):
            for g in range(NG):
                act.wait_ge(o_mm, START + 2 * g - 2)
                for c in range(DC):
                    act.wait_ge(tr, START + g * DC + c + 1)
                    nc.scalar.copy(AT[:, g % 2, c, :], ps_t[:, c, :]).then_inc(at_ok, 1)

        @block.vector
        def _(dve):
            for g in range(NG):
                for k in range(G // 2):
                    dve.wait_ge(o_mm, START + 2 * g + k + 1)
                    x2 = X[:, g * G + 2 * k:g * G + 2 * k + 2, :]
                    nc.vector.tensor_tensor(x2, ps_o[:, k, :].rearrange("p (j d) -> p j d", j=2), x2,
                                            ALU.add).then_inc(o_add, 1)

        @block.tensor
        def _(pe):
            pe.wait_ge(weights, 16)

            def transposes(g):
                for c in range(DC):
                    pe.wait_ge(at_ok, START + (g - 1) * DC + c + 1)
                    for j in range(G):
                        tile = g * G + j
                        x = nc.tensor.transpose(ps_t[:, c, j * P:(j + 1) * P],
                                                AO[:, tile // TB, tile % TB, c * HC:(c + 1) * HC, :].rearrange(
                                                    "p h d -> p (h d)"), ident[:, :])
                    x.then_inc(tr, 1)
            transposes(0)
            for g in range(NG):
                if g < NG - 1:
                    transposes(g + 1)
                pe.wait_ge(at_ok, START + (g + 1) * DC)
                pe.wait_ge(o_add, START + 2 * g)
                for k in range(G // 2):
                    for j in (2 * k, 2 * k + 1):
                        for c in range(DC):
                            x = nc.tensor.matmul(ps_o[:, k, (j % 2) * D:(j % 2 + 1) * D],
                                                 AT[:, g % 2, c, j * P:(j + 1) * P], wo[:, c, :],
                                                 start=(c == 0), stop=(c == DC - 1))
                    x.then_inc(o_mm, 1)


STAGES = "AMBMCFDF"


def network(nc, a):
    ctx = ExitStack()
    with ctx:
        top = Phase(nc, ctx, "top")
        X = top.sb("X", [P, NT, D])
        ident = top.sb("ident", [P, P])
        loaded, stored = top.sem("loaded"), top.sem("stored")
        with nc.Block() as block:
            @block.sync
            def _(sp):
                sp.dma_start(X[:, :, :], a["L0_attn_a_x"].rearrange("b (j p) d -> p (b j) d", p=P)).then_inc(loaded, 16)
                sp.dma_start(ident[:, :], a["ident"]).then_inc(loaded, 16)
                sp.wait_ge(loaded, 32)
        for n, stage in enumerate(STAGES):
            with ExitStack() as own:
                ph = Phase(nc, own, f"s{n}{stage}")
                if stage == "A":
                    attention(nc, ph, X, ident, a, "decay")
                if stage == "M":
                    expert_ffn(nc, ph, X, ident, a)
                if stage == "B":
                    retention(nc, ph, X, ident, a)
                if stage == "C":
                    attention(nc, ph, X, ident, a, "window")
                if stage == "D":
                    gated_recurrence(nc, ph, X, ident, a)
                if stage == "F":
                    low_rank_ffn(nc, ph, X, ident, a["L1_ffn_U1"], a["L1_ffn_V1"], a["L1_ffn_b1"],
                                 a["L1_ffn_U2"], a["L1_ffn_V2"], a["L1_ffn_b2"], a["ones"])
        with nc.Block() as block:
            @block.sync
            def _(sp):
                sp.dma_start(a["out"].rearrange("b (j p) d -> p (b j) d", p=P), X[:, :, :]).then_inc(stored, 16)
                sp.wait_ge(stored, 16)


def shape_constants():
    f = np.float32
    distance = np.abs(np.arange(2 * T - P)[None, :] - (T - P) - np.arange(P)[:, None]).astype(f)
    decay = np.exp(f(-0.01) * distance) * f(D ** -0.5)
    inv_freq = (f(1.0) / f(10000.0) ** (np.arange(0, HD, 2, dtype=f) / f(HD))).astype(f)
    freqs = np.arange(T, dtype=f)[:, None] * inv_freq[None, :]
    emb = np.tile(np.concatenate([freqs, freqs], 1).T, (P // HD, 1)).astype(f)
    q, k = np.arange(P)[:, None], np.arange(2 * P)[None, :]
    seen = (k <= q + P) & ((q + P - k <= 128) | (k // 64 == (q + P) // 64))
    masks = np.zeros((P, 3, 2 * P + 4), f)
    masks[:, 0, 0:P] = np.where(k[:, 0:P] <= q, 0.0, -3e38)
    masks[:, 1, 0:2 * P] = np.where(seen | ((k < 4) & (k <= q + P)), 0.0, -3e38)
    masks[:, 2, 0:2 * P] = np.where(seen, 0.0, -3e38)
    return {"decay": decay, "cos": np.cos(emb), "sin": np.sin(emb), "masks": masks.reshape(P, -1), "ident": np.eye(P, dtype=np.float32), "ones": np.ones((P, T), np.float32),
            "gather": np.tile(np.eye(32, dtype=f)[:, 0:HD + 1], (4, 1)), "batch_base": np.repeat(np.arange(B, dtype=np.float32) * T, 8).reshape(-1, 1)}


def laid_out(inputs):
    arrays = {k: np.ascontiguousarray(v) for k, v in inputs.items()}
    for name in ("Wq", "Wv", "Wg", "Wo"):
        arrays[name + "T"] = np.ascontiguousarray(arrays.pop("L0_attn_b_" + name).T)
    arrays["qkv_wT"] = np.ascontiguousarray(arrays.pop("L1_attn_a_qkv_w").T)
    arrays["out_wT"] = np.ascontiguousarray(arrays.pop("L1_attn_a_out_w").T)
    arrays["WkT"] = np.ascontiguousarray(arrays.pop("L0_attn_a_W_k").T)
    arrays["WvT_a"] = np.ascontiguousarray(arrays.pop("L0_attn_a_W_v").T)
    arrays["beta_rows"] = np.repeat(arrays.pop("L0_attn_b_beta"), HD)
    return arrays


def kernel(**inputs):
    import concourse.bacc as bacc
    from concourse.bass_utils import run_bass_kernel_spmd

    nc = bacc.Bacc("TRN2", target_bir_lowering=False, num_devices=1)
    arrays = {**laid_out(inputs), **shape_constants()}
    a = {k: nc.dram_tensor(f"in_{k}", v.shape, mybir.dt.from_np(v.dtype), kind="ExternalInput").ap()
         for k, v in arrays.items()}
    a["out"] = nc.dram_tensor("out", (B, T, D), F32, kind="ExternalOutput").ap()
    network(nc, a)
    r = run_bass_kernel_spmd(nc, [{f"in_{k}": v for k, v in arrays.items()}], core_ids=[0])
    return r.results[0]["out"]
```

```python
import numpy as np
from contextlib import ExitStack

import concourse.bass as bass
from concourse import mybir

F32 = mybir.dt.float32
F32R = mybir.dt.float32r
BF16 = mybir.dt.bfloat16
U32 = mybir.dt.uint32
ALU = mybir.AluOpType
ACT = mybir.ActivationFunctionType
AXX = mybir.AxisListType.X
ds = bass.ds

P = 128
B, T, D = 4, 1024, 256
NT = B * T // P
TB = T // P
DC = D // P
G = 4
GT = G * P
NG = NT // G
H, HD = 16, 16
EPS = 1e-5
START = 4


class Phase:

    def __init__(self, nc, ctx, name):
        self.nc, self.ctx, self.name = nc, ctx, name
        self.sems, self.dma_sems, self.all_sems = [], [], []
        ctx.callback(self.finish)

    def sb(self, name, shape, dt=F32):
        return self.ctx.enter_context(self.nc.sbuf_tensor(f"{self.name}_{name}", shape, dt))

    def ps(self, name, shape, dt=F32):
        return self.ctx.enter_context(self.nc.psum_tensor(f"{self.name}_{name}", shape, dt))

    def sem(self, name):
        s = self.nc.alloc_semaphore(f"{self.name}_{name}")
        self.sems.append(s)
        self.all_sems.append(s)
        return s

    def dma_sem(self, name, start=0):
        s = self.nc.alloc_semaphore(f"{self.name}_{name}")
        self.all_sems.append(s)
        if start:
            self.dma_sems.append((s, start))
        return s

    def finish(self):
        if self.all_sems:
            self.nc.clear_and_free_semaphores(self.all_sems)
            self.nc.all_engine_barrier()

    def start(self, eng):
        for s in self.sems:
            eng.sem_inc(s, START)
        for s, n in self.dma_sems:
            eng.sem_inc(s, n)


class LayerNorm:

    def __init__(self, ph, X, ident, hT, ps_t, h_out=None):
        self.nc, self.X, self.ident, self.hT, self.ps_t, self.h_out = ph.nc, X, ident, hT, ps_t, h_out
        self.st = ph.sb("ln_st", [P, G, 6])
        self.mv = ph.sb("ln_mv", [P, G, 2])
        self.ve = ph.sb("ln_ve", [P, G])
        self.mhalf = ph.sb("ln_mhalf", [P, G])
        self.eps = ph.sb("ln_eps", [P, G])
        self.rstd = ph.sb("ln_rstd", [P, G])
        self.h = ph.sb("ln_h", [P, G, D])
        self.moments = ph.sem("ln_moments")
        self.veps = ph.sem("ln_veps")
        self.rs = ph.sem("ln_rs")
        self.hrow = ph.sem("ln_hrow")
        self.trans = ph.sem("ln_trans")
        self.hTok = ph.sem("ln_hT")

    def pool_setup(self):
        self.nc.gpsimd.memset(self.eps[:, :], EPS)
        self.nc.gpsimd.memset(self.mhalf[:, :], -0.5).then_inc(self.rs, 1)

    def vector(self, v, g):
        for j in range(G):
            self.nc.vector.bn_stats(self.st[:, j, :], self.X[:, ds(g * G + j, 1), :])
        v.drain()
        for j in range(G):
            self.nc.vector.bn_aggr(self.mv[:, j, :], self.st[:, j, :]).then_inc(self.moments, 1)
        v.wait_ge(self.rs, START + g + 2)
        v.wait_ge(self.trans, START + g * DC)
        for j in range(G):
            self.nc.vector.tensor_scalar(self.h[:, j, :], self.X[:, ds(g * G + j, 1), :], self.mv[:, j, 0:1],
                                         self.rstd[:, j:j + 1], ALU.subtract, ALU.mult).then_inc(self.hrow, 1)

    def pool(self, p, g):
        p.wait_ge(self.moments, START + (g + 1) * G)
        self.nc.gpsimd.tensor_tensor(self.ve[:, :], self.mv[:, :, 1], self.eps[:, :], ALU.add).then_inc(self.veps, 1)
        p.wait_ge(self.veps, START + g + 1)
        p.wait_ge(self.hrow, START + g * G)
        self.nc.gpsimd.tensor_tensor(self.rstd[:, :], self.ve[:, :], self.mhalf[:, :], ALU.pow).then_inc(self.rs, 1)

    def tensor(self, t, g):
        t.wait_ge(self.hrow, START + (g + 1) * G)
        t.wait_ge(self.hTok, START + g * DC)
        for c in range(DC):
            for j in range(G):
                last = self.nc.tensor.transpose(self.ps_t[:, c, j * P:(j + 1) * P],
                                                self.h[:, j, c * P:(c + 1) * P], self.ident[:, :])
            last.then_inc(self.trans, 1)

    def scalar(self, s, g, slot=None):
        for c in range(DC):
            s.wait_ge(self.trans, START + g * DC + c + 1)
            to = self.hT[:, c, ds(g * GT, GT)] if slot is None else self.hT[:, slot, c, :]
            self.nc.scalar.copy(to, self.ps_t[:, c, :]).then_inc(self.hTok, 1)


def load_once(eng, sem, pairs):
    for dst, src in pairs:
        eng.dma_start(dst, src).then_inc(sem, 16)
    return 16 * len(pairs)


def low_rank_ffn(nc, ph, X, ident, U1, V1, b1, U2, V2, b2, ones):
    R, FF = U1.shape[1], V1.shape[1]
    M = FF // P
    hT = ph.sb("hT", [P, DC, B * T])
    u1 = ph.sb("u1", [P, DC, R])
    v1 = ph.sb("v1", [R, FF])
    bias1 = ph.sb("bias1", [P, M])
    u2 = ph.sb("u2", [P, M, R])
    v2 = ph.sb("v2", [R + 1, D])
    PT = ph.sb("PT", [R, GT])
    HT = ph.sb("HT", [P, M, GT])
    QT = ph.sb("QT", [R + 1, GT])
    ps_t = ph.ps("ps_t", [P, DC, GT])
    ps_p = ph.ps("ps_p", [P, GT])
    ps_h = ph.ps("ps_h", [P, 2, GT])
    ps_q = ph.ps("ps_q", [P, GT])
    ps_o = ph.ps("ps_o", [P, 2, GT])
    ln = LayerNorm(ph, X, ident, hT, ps_t)
    weights = ph.dma_sem("weights")
    p_mm, p_sb = ph.sem("p_mm"), ph.sem("p_sb")
    h_mm, h_sb = ph.sem("h_mm"), ph.sem("h_sb")
    q_mm, q_sb = ph.sem("q_mm"), ph.sem("q_sb")
    o_mm, o_add = ph.sem("o_mm"), ph.sem("o_add")
    pairs = [(u1[:, :, :], U1.rearrange("(c p) r -> p c r", p=P)), (v1[:, :], V1),
             (bias1[:, :], b1.rearrange("(m p) -> p m", p=P)),
             (u2[:, :, :], U2.rearrange("(m p) r -> p m r", p=P)), (v2[0:R, :], V2),
             (v2[R:R + 1, :], b2.rearrange("(a d) -> a d", a=1)), (QT[R:R + 1, :], ones[0:1, 0:GT])]
    loaded = 16 * len(pairs)

    with nc.Block() as block:
        @block.sync
        def _(sp):
            ph.start(sp)
            with nc.allow_non_contiguous_dma(reason="a bias laid out over partitions"):
                load_once(sp, weights, pairs)
            sp.wait_ge(weights, loaded)

        @block.gpsimd
        def _(pool):
            ln.pool_setup()
            pool.wait_ge(ln.rs, START + 1)
            with pool.Fori(0, NG) as g:
                ln.pool(pool, g)

        @block.vector
        def _(dve):
            def add(g):
                for k in range(G // 2):
                    dve.wait_ge(o_mm, START + g * (G // 2) + k + 1)
                    x2 = X[:, ds(g * G + 2 * k, 2), :]
                    nc.vector.tensor_tensor(x2, ps_o[:, k, :].rearrange("p (j d) -> p j d", j=2), x2,
                                            ALU.add).then_inc(o_add, 1)
            ln.vector(dve, 0)
            with dve.Fori(0, NG - 1) as g:
                ln.vector(dve, g + 1)
                add(g)
            add(NG - 1)

        @block.scalar
        def _(act):
            act.wait_ge(weights, loaded)

            def turn(g, last):
                act.wait_ge(p_mm, START + g + 1)
                nc.scalar.copy(PT[:, :], ps_p[0:R, :]).then_inc(p_sb, 1)
                if not last:
                    ln.scalar(act, g + 1)
                for m in range(M):
                    act.wait_ge(h_mm, START + g * M + m + 1)
                    if m == 0:
                        act.wait_ge(q_mm, START + g)
                    nc.scalar.activation(HT[:, m, :], ps_h[:, m % 2, :], ACT.Gelu_apprx_tanh,
                                         bias=bias1[:, m:m + 1]).then_inc(h_sb, 1)
                act.wait_ge(q_mm, START + g + 1)
                act.wait_ge(o_mm, START + g * (G // 2))
                nc.scalar.copy(QT[0:R, :], ps_q[0:R, :]).then_inc(q_sb, 1)
            ln.scalar(act, 0)
            with act.Fori(0, NG - 1) as g:
                turn(g, False)
            turn(NG - 1, True)

        @block.tensor
        def _(pe):
            pe.wait_ge(weights, loaded)

            def down(g, m):
                pe.wait_ge(h_sb, START + g * M + m + 1)
                i = nc.tensor.matmul(ps_q[0:R, :], u2[:, m, :], HT[:, m, :], start=(m == 0), stop=(m == M - 1))
                if m == M - 1:
                    i.then_inc(q_mm, 1)

            def turn(g, last):
                pe.wait_ge(ln.hTok, START + (g + 1) * DC)
                for c in range(DC):
                    i = nc.tensor.matmul(ps_p[0:R, :], u1[:, c, :], hT[:, c, ds(g * GT, GT)],
                                         start=(c == 0), stop=(c == DC - 1))
                i.then_inc(p_mm, 1)
                if not last:
                    ln.tensor(pe, g + 1)
                pe.wait_ge(p_sb, START + g + 1)
                pe.wait_ge(q_sb, START + g)
                for m in range(M + 1):
                    if m < M:
                        if m >= 2:
                            pe.wait_ge(h_sb, START + g * M + m - 1)
                        nc.tensor.matmul(ps_h[:, m % 2, :], v1[:, m * P:(m + 1) * P], PT[:, :],
                                         start=True, stop=True).then_inc(h_mm, 1)
                    if m:
                        down(g, m - 1)
                pe.wait_ge(q_sb, START + g + 1)
                pe.wait_ge(o_add, START + g * (G // 2))
                for k in range(G // 2):
                    for j in (2 * k, 2 * k + 1):
                        i = nc.tensor.matmul(ps_o[:, k, (j % 2) * D:(j % 2 + 1) * D], QT[:, j * P:(j + 1) * P],
                                             v2[:, :], start=True, stop=True)
                    i.then_inc(o_mm, 1)
            ln.tensor(pe, 0)
            with pe.Fori(0, NG - 1) as g:
                turn(g, False)
            turn(NG - 1, True)


def retention(nc, ph, X, ident, a):
    hT = ph.sb("hT", [P, DC, B * T])
    wq, wv, wg, wo = (ph.sb(n, [P, DC, D]) for n in ("wq", "wv", "wg", "wo"))
    mean_w = ph.sb("mean_w", [P, P])
    beta_in, lam = ph.sb("beta_in", [P, DC]), ph.sb("lam", [P, DC])
    gamma, shift = ph.sb("gamma", [P, DC]), ph.sb("shift", [P, DC])
    eps = ph.sb("eps", [P, 1])
    S = ph.sb("S", [P, DC, GT])
    carry = ph.sb("carry", [P, DC])
    Y, SQ = ph.sb("Y", [P, DC, GT]), ph.sb("SQ", [P, DC, GT])
    gate = ph.sb("gate", [P, DC, GT])
    Z = ph.sb("Z", [P, DC, GT])
    sd, rstd = ph.sb("sd", [P, GT]), ph.sb("rstd", [P, GT])
    ps_t = ph.ps("ps_t", [P, DC, GT])
    ps_v = ph.ps("ps_v", [P, DC, GT])
    ps_q = ph.ps("ps_q", [P, DC, GT])
    ps_m, ps_r = ph.ps("ps_m", [P, GT]), ph.ps("ps_r", [P, GT])
    ln = LayerNorm(ph, X, ident, hT, ps_t)
    weights = ph.dma_sem("weights")
    consts = ph.sem("consts")
    v_mm, scan = ph.sem("v_mm"), ph.sem("scan")
    q_mm, y_ok = ph.sem("q_mm"), ph.sem("y_ok")
    g_mm, gate_ok = ph.sem("g_mm"), ph.sem("gate_ok")
    m_mm, d_ok = ph.sem("m_mm"), ph.sem("d_ok")
    sq_ok, r_mm = ph.sem("sq_ok"), ph.sem("r_mm")
    sd_ok, z_ok = ph.sem("sd_ok"), ph.sem("z_ok")
    o_mm, o_add = ph.sem("o_mm"), ph.sem("o_add")
    part = lambda w: w.rearrange("(c p) n -> p c n", p=P)
    col = lambda w: w.rearrange("(c p) -> p c", p=P)
    pairs = [(wv[:, :, :], part(a["WvT"])), (wq[:, :, :], part(a["WqT"])), (wg[:, :, :], part(a["WgT"])),
             (wo[:, :, :], part(a["WoT"])), (beta_in[:, :], col(a["beta_rows"])),
             (gamma[:, :], col(a["L0_attn_b_ln_gamma"])), (shift[:, :], col(a["L0_attn_b_ln_beta"]))]
    loaded = 16 * len(pairs)
    HB = T // GT

    with nc.Block() as block:
        @block.sync
        def _(sp):
            ph.start(sp)
            with nc.allow_non_contiguous_dma(reason="vectors laid out over partitions"):
                load_once(sp, weights, pairs)
            sp.wait_ge(weights, loaded)

        @block.gpsimd
        def _(pool):
            ln.pool_setup()
            pool.wait_ge(ln.rs, START + 1)
            with pool.Fori(0, NG) as g:
                ln.pool(pool, g)

        @block.vector
        def _(dve):
            nc.vector.memset(eps[:, :], EPS)
            nc.vector.memset(mean_w[:, :], 1.0 / D).then_inc(consts, 1)
            ln.vector(dve, 0)
            dve.wait_ge(consts, START + 2)

            def turn(b, h, last):
                g = b * HB + h
                dve.wait_ge(z_ok, START + g * DC)
                for c in range(DC):
                    dve.wait_ge(v_mm, START + g * DC + c + 1)
                    nc.vector.tensor_tensor_scan(S[:, c, :], lam[:, c:c + 1].to_broadcast([P, GT]), ps_v[:, c, :],
                                                 0.0 if h == 0 else carry[:, c:c + 1],
                                                 ALU.mult, ALU.add).then_inc(scan, 1)
                for c in range(DC):
                    dve.wait_ge(q_mm, START + g * DC + c + 1)
                    dve.wait_ge(scan, START + g * DC + c + 1)
                    nc.vector.tensor_tensor(Y[:, c, :], ps_q[:, c, :], S[:, c, :], ALU.mult).then_inc(y_ok, 1)
                nc.vector.tensor_copy(carry[:, :], S[:, :, GT - 1])
                if not last:
                    ln.vector(dve, g + 1)
                dve.wait_ge(m_mm, START + g + 1)
                for c in range(DC):
                    nc.vector.tensor_tensor(Y[:, c, :], Y[:, c, :], ps_m[:, :], ALU.subtract).then_inc(d_ok, 1)
                dve.wait_ge(sd_ok, START + g + 1)
                nc.vector.reciprocal(rstd[:, :], sd[:, :])
                dve.drain()
                for c in range(DC):
                    nc.vector.scalar_tensor_tensor(Z[:, c, :], Y[:, c, :], gamma[:, c:c + 1], rstd[:, :],
                                                   ALU.mult, ALU.mult)
                dve.drain()
                dve.wait_ge(gate_ok, START + (g + 1) * DC)
                for c in range(DC):
                    nc.vector.scalar_tensor_tensor(Z[:, c, :], Z[:, c, :], shift[:, c:c + 1], gate[:, c, :],
                                                   ALU.add, ALU.mult).then_inc(z_ok, 1)
                for k in range(G // 2):
                    dve.wait_ge(o_mm, START + g * (G // 2) + k + 1)
                    x2 = X[:, ds(g * G + 2 * k, 2), :]
                    nc.vector.tensor_tensor(x2, ps_q[:, k, :].rearrange("p (j d) -> p j d", j=2), x2,
                                            ALU.add).then_inc(o_add, 1)
            with dve.Fori(0, B - 1) as b:
                for h in range(HB):
                    turn(b, h, False)
            for h in range(HB):
                turn(B - 1, h, h == HB - 1)

        @block.scalar
        def _(act):
            act.wait_ge(weights, loaded)
            act.wait_ge(consts, START + 1)
            nc.scalar.activation(lam[:, :], beta_in[:, :], ACT.Sigmoid).then_inc(consts, 1)
            ln.scalar(act, 0)

            def turn(g, last):
                if not last:
                    ln.scalar(act, g + 1)
                act.wait_ge(g_mm, START + g * DC + 1)
                act.wait_ge(z_ok, START + g * DC)
                for c in range(DC):
                    act.wait_ge(g_mm, START + g * DC + c + 1)
                    nc.scalar.activation(gate[:, c, :], ps_v[:, c, :], ACT.Silu).then_inc(gate_ok, 1)
                for c in range(DC):
                    act.wait_ge(d_ok, START + g * DC + c + 1)
                    nc.scalar.activation(SQ[:, c, :], Y[:, c, :], ACT.Square).then_inc(sq_ok, 1)
                act.wait_ge(r_mm, START + g + 1)
                nc.scalar.activation(sd[:, :], ps_r[:, :], ACT.Sqrt, bias=eps[:, 0:1]).then_inc(sd_ok, 1)
            with act.Fori(0, NG - 1) as g:
                turn(g, False)
            turn(NG - 1, True)

        @block.tensor
        def _(pe):
            pe.wait_ge(weights, loaded)
            pe.wait_ge(consts, START + 1)

            def project(out, w, g, done):
                for c in range(DC):
                    for k in range(DC):
                        i = nc.tensor.matmul(out[:, c, :], w[:, k, c * P:(c + 1) * P], hT[:, k, ds(g * GT, GT)],
                                             start=(k == 0), stop=(k == DC - 1))
                    i.then_inc(done, 1)

            def mean(out, src, done):
                for c in range(DC):
                    i = nc.tensor.matmul(out[:, :], mean_w[:, :], src[:, c, :], start=(c == 0), stop=(c == DC - 1))
                i.then_inc(done, 1)

            def turn(g, last):
                pe.wait_ge(ln.hTok, START + (g + 1) * DC)
                pe.wait_ge(gate_ok, START + g * DC)
                project(ps_v, wv, g, v_mm)
                pe.wait_ge(o_add, START + g * (G // 2))
                project(ps_q, wq, g, q_mm)
                pe.wait_ge(scan, START + (g + 1) * DC)
                project(ps_v, wg, g, g_mm)
                if not last:
                    ln.tensor(pe, g + 1)
                pe.wait_ge(y_ok, START + (g + 1) * DC)
                mean(ps_m, Y, m_mm)
                pe.wait_ge(sq_ok, START + (g + 1) * DC)
                mean(ps_r, SQ, r_mm)
                pe.wait_ge(z_ok, START + (g + 1) * DC)
                for k in range(G // 2):
                    for j in (2 * k, 2 * k + 1):
                        for c in range(DC):
                            i = nc.tensor.matmul(ps_q[:, k, (j % 2) * D:(j % 2 + 1) * D],
                                                 Z[:, c, j * P:(j + 1) * P], wo[:, c, :],
                                                 start=(c == 0), stop=(c == DC - 1))
                    i.then_inc(o_mm, 1)
            ln.tensor(pe, 0)
            with pe.Fori(0, NG - 1) as g:
                turn(g, False)
            turn(NG - 1, True)


def gated_recurrence(nc, ph, X, ident, a):
    K = 4
    hT = ph.sb("hT", [P, DC, B * T])
    wi, wf, wg, wo = (ph.sb(n, [P, DC, D]) for n in ("wi", "wf", "wg", "wo"))
    conv_i, conv_f = ph.sb("conv_i", [P, DC, K]), ph.sb("conv_f", [P, DC, K])
    gnorm = ph.sb("gnorm", [P, DC])
    mean_w = ph.sb("mean_w", [P, P])
    eps = ph.sb("eps", [P, 1])
    RAW = ph.sb("RAW", [P, 2, DC, K - 1 + GT])
    CV = ph.sb("CV", [P, 2, DC, GT])
    FG, OM = ph.sb("FG", [P, DC, GT]), ph.sb("OM", [P, DC, GT])
    SI = ph.sb("SI", [P, DC, GT])
    O = ph.sb("O", [P, DC, GT])
    carry = ph.sb("carry", [P, DC])
    SQ, gate, Z = (ph.sb(n, [P, DC, GT]) for n in ("SQ", "gate", "Z"))
    sd, rms = ph.sb("sd", [P, GT]), ph.sb("rms", [P, GT])
    ps_t = ph.ps("ps_t", [P, DC, GT])
    ps_i = ph.ps("ps_i", [P, DC, GT])
    ps_f = ph.ps("ps_f", [P, DC, GT])
    ps_r = ph.ps("ps_r", [P, GT])
    ln = LayerNorm(ph, X, ident, hT, ps_t)
    weights = ph.dma_sem("weights")
    consts = ph.sem("consts")
    raw_mm, raw_ok = ph.sem("raw_mm"), ph.sem("raw_ok")
    conv_ok, act_ok = ph.sem("conv_ok"), ph.sem("act_ok")
    i_ok, o_ok = ph.sem("i_ok"), ph.sem("o_ok")
    g_mm, gate_ok = ph.sem("g_mm"), ph.sem("gate_ok")
    sq_ok, r_mm, sd_ok = ph.sem("sq_ok"), ph.sem("r_mm"), ph.sem("sd_ok")
    z_ok, o_mm, o_add = ph.sem("z_ok"), ph.sem("o_mm"), ph.sem("o_add")
    part = lambda w: w.rearrange("(c p) n -> p c n", p=P)
    pairs = [(wi[:, :, :], part(a["L1_attn_b_Wi"])), (wf[:, :, :], part(a["L1_attn_b_Wf"])),
             (wg[:, :, :], part(a["L1_attn_b_Wg"])), (wo[:, :, :], part(a["L1_attn_b_Wo"])),
             (conv_i[:, :, :], part(a["L1_attn_b_conv_i"])), (conv_f[:, :, :], part(a["L1_attn_b_conv_f"])),
             (gnorm[:, :], a["L1_attn_b_g_norm_weight"].rearrange("(c p) -> p c", p=P))]
    loaded = 16 * len(pairs)
    HB = T // GT

    with nc.Block() as block:
        @block.sync
        def _(sp):
            ph.start(sp)
            with nc.allow_non_contiguous_dma(reason="vectors laid out over partitions"):
                load_once(sp, weights, pairs)
            sp.wait_ge(weights, loaded)

        @block.gpsimd
        def _(pool):
            ln.pool_setup()
            pool.wait_ge(ln.rs, START + 1)
            with pool.Fori(0, NG) as g:
                ln.pool(pool, g)

        @block.vector
        def _(dve):
            nc.vector.memset(eps[:, :], EPS)
            nc.vector.memset(mean_w[:, :], 1.0 / D).then_inc(consts, 1)
            ln.vector(dve, 0)
            dve.wait_ge(weights, loaded)

            def turn(b, h, last):
                g = b * HB + h
                dve.wait_ge(act_ok, START + g * 3 * DC)
                for s, w in ((0, conv_i), (1, conv_f)):
                    for c in range(DC):
                        dve.wait_ge(raw_ok, START + g * 2 * DC + s * DC + c + 1)
                        nc.vector.tensor_scalar(CV[:, s, c, :], RAW[:, s, c, 0:GT], w[:, c, 0:1], None, ALU.mult)
                for k in range(1, K):
                    dve.drain()
                    for s, w in ((0, conv_i), (1, conv_f)):
                        for c in range(DC):
                            i = nc.vector.scalar_tensor_tensor(CV[:, s, c, :], RAW[:, s, c, k:k + GT],
                                                               w[:, c, k:k + 1], CV[:, s, c, :], ALU.mult, ALU.add)
                            if k == K - 1:
                                i.then_inc(conv_ok, 1)
                if not last:
                    ln.vector(dve, g + 1)
                dve.wait_ge(act_ok, START + (g + 1) * 3 * DC)
                for c in range(DC):
                    nc.vector.tensor_tensor(SI[:, c, :], SI[:, c, :], OM[:, c, :], ALU.mult).then_inc(i_ok, 1)
                for c in range(DC):
                    dve.wait_ge(i_ok, START + g * DC + c + 1)
                    nc.vector.tensor_tensor_scan(O[:, c, :], FG[:, c, :], SI[:, c, :],
                                                 0.0 if h == 0 else carry[:, c:c + 1],
                                                 ALU.mult, ALU.add).then_inc(o_ok, 1)
                dve.drain()
                nc.vector.tensor_copy(carry[:, :], O[:, :, GT - 1])
                dve.wait_ge(sd_ok, START + g + 1)
                nc.vector.reciprocal(rms[:, :], sd[:, :])
                dve.drain()
                for c in range(DC):
                    nc.vector.scalar_tensor_tensor(Z[:, c, :], O[:, c, :], gnorm[:, c:c + 1], rms[:, :],
                                                   ALU.mult, ALU.mult)
                dve.drain()
                dve.wait_ge(gate_ok, START + (g + 1) * DC)
                for c in range(DC):
                    nc.vector.tensor_tensor(Z[:, c, :], Z[:, c, :], gate[:, c, :], ALU.mult).then_inc(z_ok, 1)
                for k in range(G // 2):
                    dve.wait_ge(o_mm, START + g * (G // 2) + k + 1)
                    x2 = X[:, ds(g * G + 2 * k, 2), :]
                    nc.vector.tensor_tensor(x2, ps_f[:, k, :].rearrange("p (j d) -> p j d", j=2), x2,
                                            ALU.add).then_inc(o_add, 1)
            with dve.Fori(0, B - 1) as b:
                for h in range(HB):
                    turn(b, h, False)
            for h in range(HB):
                turn(B - 1, h, h == HB - 1)

        @block.scalar
        def _(act):
            act.wait_ge(weights, loaded)
            act.wait_ge(consts, START + 1)
            ln.scalar(act, 0)

            def turn(b, h, last):
                g = b * HB + h
                act.wait_ge(conv_ok, START + g * 2 * DC)
                for s, ps in ((0, ps_i), (1, ps_f)):
                    for c in range(DC):
                        if h == 0:
                            nc.scalar.memzero(RAW[:, s, c, 0:K - 1])
                        else:
                            nc.scalar.copy(RAW[:, s, c, 0:K - 1], RAW[:, s, c, GT:GT + K - 1])
                act.drain()
                for s, ps in ((0, ps_i), (1, ps_f)):
                    for c in range(DC):
                        act.wait_ge(raw_mm, START + g * 2 * DC + s * DC + c + 1)
                        nc.scalar.copy(RAW[:, s, c, K - 1:], ps[:, c, :]).then_inc(raw_ok, 1)
                if not last:
                    ln.scalar(act, g + 1)
                act.wait_ge(z_ok, START + g * DC)
                for c in range(DC):
                    act.wait_ge(g_mm, START + g * DC + c + 1)
                    nc.scalar.activation(gate[:, c, :], ps_i[:, c, :], ACT.Silu).then_inc(gate_ok, 1)
                act.wait_ge(conv_ok, START + (g + 1) * 2 * DC)
                for c in range(DC):
                    nc.scalar.activation(SI[:, c, :], CV[:, 0, c, :], ACT.Silu).then_inc(act_ok, 1)
                for c in range(DC):
                    nc.scalar.activation(FG[:, c, :], CV[:, 1, c, :], ACT.Sigmoid).then_inc(act_ok, 1)
                act.wait_ge(act_ok, START + (g + 1) * 3 * DC - DC)
                for c in range(DC):
                    nc.scalar.activation(OM[:, c, :], FG[:, c, :], ACT.Copy, bias=1.0, scale=-1.0).then_inc(act_ok, 1)
                for c in range(DC):
                    act.wait_ge(o_ok, START + g * DC + c + 1)
                    nc.scalar.activation(SQ[:, c, :], O[:, c, :], ACT.Square).then_inc(sq_ok, 1)
                act.wait_ge(r_mm, START + g + 1)
                nc.scalar.activation(sd[:, :], ps_r[:, :], ACT.Sqrt, bias=eps[:, 0:1]).then_inc(sd_ok, 1)
            with act.Fori(0, B - 1) as b:
                for h in range(HB):
                    turn(b, h, False)
            for h in range(HB):
                turn(B - 1, h, h == HB - 1)

        @block.tensor
        def _(pe):
            pe.wait_ge(weights, loaded)
            pe.wait_ge(consts, START + 1)

            def project(out, w, g, done):
                for c in range(DC):
                    for k in range(DC):
                        i = nc.tensor.matmul(out[:, c, :], w[:, k, c * P:(c + 1) * P], hT[:, k, ds(g * GT, GT)],
                                             start=(k == 0), stop=(k == DC - 1))
                    i.then_inc(done, 1)

            def turn(g, last):
                pe.wait_ge(ln.hTok, START + (g + 1) * DC)
                pe.wait_ge(gate_ok, START + g * DC)
                project(ps_i, wi, g, raw_mm)
                pe.wait_ge(o_add, START + g * (G // 2))
                project(ps_f, wf, g, raw_mm)
                pe.wait_ge(raw_ok, START + g * 2 * DC + DC)
                project(ps_i, wg, g, g_mm)
                if not last:
                    ln.tensor(pe, g + 1)
                pe.wait_ge(sq_ok, START + (g + 1) * DC)
                for c in range(DC):
                    i = nc.tensor.matmul(ps_r[:, :], mean_w[:, :], SQ[:, c, :], start=(c == 0), stop=(c == DC - 1))
                i.then_inc(r_mm, 1)
                pe.wait_ge(z_ok, START + (g + 1) * DC)
                for k in range(G // 2):
                    for j in (2 * k, 2 * k + 1):
                        for c in range(DC):
                            i = nc.tensor.matmul(ps_f[:, k, (j % 2) * D:(j % 2 + 1) * D],
                                                 Z[:, c, j * P:(j + 1) * P], wo[:, c, :],
                                                 start=(c == 0), stop=(c == DC - 1))
                    i.then_inc(o_mm, 1)
            ln.tensor(pe, 0)
            with pe.Fori(0, NG - 1) as g:
                turn(g, False)
            turn(NG - 1, True)


def expert_ffn(nc, ph, X, ident, a):
    E, FF = a["L0_ffn_w1"].shape[0], a["L0_ffn_w1"].shape[2]
    KT = 2 * T // E
    C = KT // P
    R = B * E
    M = FF // P
    h_rows = nc.dram_tensor(f"{ph.name}_h_rows", (B * T, D), F32, kind="Internal").ap()
    acc = nc.dram_tensor(f"{ph.name}_acc", (B * T, D), F32, kind="Internal").ap()
    idxT = ph.sb("idxT", [P, C, R], U32)
    gT = ph.sb("gT", [P, C, R])
    raw = Raw(ph, a, M)
    with ExitStack() as own:
        route(nc, Phase(nc, own, ph.name + "r"), X, ident, a, E, R, C, KT, h_rows, acc, idxT, gT, raw)
    with ExitStack() as own:
        experts(nc, Phase(nc, own, ph.name + "e"), ident, E, C, M, h_rows, acc, idxT, gT, raw)
    with ExitStack() as own:
        add_rounded(nc, Phase(nc, own, ph.name + "a"), X, acc)


class Raw:

    def __init__(self, ph, a, M):
        self.w1 = ph.sb("raw_w1", [P, DC, M * P])
        self.w2 = ph.sb("raw_w2", [P, M, D])
        self.w1_in, self.w2_in = ph.dma_sem("raw_w1_in"), ph.dma_sem("raw_w2_in")
        self.a = a

    def load_w1(self, sp, e):
        sp.dma_start(self.w1[:, :, :], self.a["L0_ffn_w1"][ds(e, 1), :, :].rearrange(
            "a (c p) f -> p (a c) f", p=P)).then_inc(self.w1_in, 16)

    def load_w2(self, sp, e):
        sp.dma_start(self.w2[:, :, :], self.a["L0_ffn_w2"][ds(e, 1), :, :].rearrange(
            "a (m p) d -> p (a m) d", p=P)).then_inc(self.w2_in, 16)


def route(nc, ph, X, ident, a, E, R, C, KT, h_rows, acc, idxT, gT, raw):
    TH = T // 2
    hT = ph.sb("hT", [P, DC, B * T])
    gate_w = ph.sb("gate_w", [P, DC, E])
    base = ph.sb("base", [2 * R, 1])
    reverse = ph.sb("reverse", [P, P])
    zeros = ph.sb("zeros", [P, G, D])
    scT = ph.sb("scT", [E, B * T])
    sc, ex, pr = (ph.sb(n, [P, TB, B, E]) for n in ("sc", "ex", "pr"))
    mx, sm, rc = (ph.sb(n, [P, TB, B]) for n in ("mx", "sm", "rc"))
    PR = [ph.sb(f"PR{i}", [2 * R, TH]) for i in range(2)]
    vals, idx = ph.sb("vals", [2 * R, KT]), ph.sb("idx", [2 * R, KT], U32)
    rowf = ph.sb("rowf", [2 * R, KT])
    both = ph.sb("both", [P, 2, C, 2 * R])
    first, step = ph.sb("first", [P, C, R]), ph.sb("step", [P, C, R])
    ps_t = ph.ps("ps_t", [P, DC, GT])
    ps_s = ph.ps("ps_s", [P, GT])
    ps_x = ph.ps("ps_x", [P, TB, B, E])
    ps_p = ph.ps("ps_p", [P, TH])
    ps_i = ph.ps("ps_i", [P, 2, C, 2 * R])
    ps_r = ph.ps("ps_r", [P, 2, C, R])
    ln = LayerNorm(ph, X, ident, hT, ps_t)
    weights, rows_out, zeroed = ph.dma_sem("weights"), ph.dma_sem("rows_out"), ph.dma_sem("zeroed")
    zeros_ok = ph.sem("zeros_ok")
    s_mm, s_sb = ph.sem("s_mm"), ph.sem("s_sb")
    x_tr, x_ok, e_ok, p_ok = ph.sem("x_tr"), ph.sem("x_ok"), ph.sem("e_ok"), ph.sem("p_ok")
    p_tr, p_sb, top_ok = ph.sem("p_tr"), ph.sem("p_sb"), ph.sem("top_ok")
    i_tr, i_ok, r_mm = ph.sem("i_tr"), ph.sem("i_ok"), ph.sem("r_mm")

    with nc.Block() as block:
        @block.sync
        def _(sp):
            ph.start(sp)
            sp.dma_start(gate_w[:, :, :], a["L0_ffn_gate_w"].rearrange("(c p) e -> p c e", p=P)).then_inc(weights, 16)
            sp.dma_start(base[:, :], a["batch_base"]).then_inc(weights, 16)
            sp.dma_start(reverse[:, :], a["reverse"]).then_inc(weights, 16)
            sp.wait_ge(zeros_ok, START + 1)
            for g in range(NG):
                sp.dma_start(acc[g * GT:(g + 1) * GT, :].rearrange("(j p) d -> p j d", p=P),
                             zeros[:, :, :]).then_inc(zeroed, 16)
            with sp.Fori(0, NG) as g:
                sp.wait_ge(ln.hrow, START + (g + 1) * G)
                sp.dma_start(h_rows[ds(g * GT, GT), :].rearrange("(j p) d -> p j d", p=P),
                             ln.h[:, :, :]).then_inc(rows_out, 16)
            raw.load_w1(sp, 0)
            raw.load_w2(sp, 0)
            sp.wait_ge(rows_out, 16 * NG)
            sp.wait_ge(zeroed, 16 * NG)

        @block.gpsimd
        def _(pool):
            ln.pool_setup()
            pool.wait_ge(ln.rs, START + 1)
            with pool.Fori(0, NG) as g:
                ln.pool(pool, g)

        @block.vector
        def _(dve):
            nc.vector.memset(zeros[:, :, :], 0.0).then_inc(zeros_ok, 1)
            ln.vector(dve, 0)
            with dve.Fori(1, NG) as g:
                dve.wait_ge(rows_out, 16 * g)
                ln.vector(dve, g)
            wide = lambda m: m[:, :, :].rearrange("p j b -> p (j b)").unsqueeze(2).to_broadcast([P, TB * B, E])
            flat = lambda m: m[:, :, :, :].rearrange("p j b e -> p (j b) e")
            dve.wait_ge(x_tr, START + 1)
            nc.vector.tensor_copy(flat(sc), flat(ps_x))
            dve.drain()
            nc.vector.tensor_reduce(mx[:, :, :].rearrange("p j b -> p (j b)"), flat(sc), AXX, ALU.max)
            dve.drain()
            nc.vector.tensor_tensor(flat(sc), flat(sc), wide(mx), ALU.subtract).then_inc(x_ok, 1)
            dve.wait_ge(e_ok, START + 1)
            nc.vector.tensor_reduce(sm[:, :, :].rearrange("p j b -> p (j b)"), flat(ex), AXX, ALU.add)
            dve.drain()
            nc.vector.reciprocal(rc[:, :, :], sm[:, :, :])
            dve.drain()
            nc.vector.tensor_tensor(flat(pr), flat(ex), wide(rc), ALU.mult).then_inc(p_ok, 1)
            dve.wait_ge(p_sb, START + 1)
            dve.wait_ge(weights, 48)
            for r in range(KT // 8):
                now, after, eight = PR[r % 2], PR[(r + 1) % 2], slice(8 * r, 8 * r + 8)
                nc.vector.max(vals[:, eight], now[:, :])
                dve.drain()
                nc.vector.max_index(idx[:, eight], vals[:, eight], now[:, :])
                if r < KT // 8 - 1:
                    nc.vector.match_replace(after[:, :], vals[:, eight], now[:, :], -1.0)
                dve.drain()
            nc.vector.tensor_copy(rowf[:, :], idx[:, :])
            dve.drain()
            nc.vector.tensor_scalar(rowf[:, :], rowf[:, :], base[:, 0:1], None, ALU.add).then_inc(top_ok, 1)
            dve.wait_ge(i_tr, START + 1)
            nc.vector.tensor_copy(both[:, :, :, :], ps_i[:, :, :, :]).then_inc(i_ok, 1)
            dve.wait_ge(r_mm, START + 1)
            row, prob = both[:, 0, :, 0:R], both[:, 1, :, 0:R]
            nc.vector.tensor_tensor(gT[:, :, :], prob, ps_r[:, 1, :, :], ALU.max)
            nc.vector.tensor_tensor(first[:, :, :], prob, ps_r[:, 1, :, :], ALU.is_ge)
            nc.vector.tensor_tensor(step[:, :, :], row, ps_r[:, 0, :, :], ALU.subtract)
            dve.drain()
            nc.vector.tensor_tensor(step[:, :, :], step[:, :, :], first[:, :, :], ALU.mult)
            dve.drain()
            nc.vector.tensor_tensor(step[:, :, :], step[:, :, :], ps_r[:, 0, :, :], ALU.add)
            dve.drain()
            nc.vector.tensor_copy(idxT[:, :, :], step[:, :, :])

        @block.scalar
        def _(act):
            with act.Fori(0, NG) as g:
                ln.scalar(act, g)
                act.wait_ge(s_mm, START + g + 1)
                nc.scalar.copy(scT[:, ds(g * GT, GT)], ps_s[0:E, :]).then_inc(s_sb, 1)
            act.wait_ge(x_ok, START + 1)
            nc.scalar.activation(ex[:, :, :, :], sc[:, :, :, :], ACT.Exp).then_inc(e_ok, 1)
            act.wait_ge(p_tr, START + 1)
            nc.scalar.copy(PR[0][:, :], ps_p[0:2 * R, :]).then_inc(p_sb, 1)

        @block.tensor
        def _(pe):
            pe.wait_ge(weights, 48)
            with pe.Fori(0, NG) as g:
                ln.tensor(pe, g)
                pe.wait_ge(ln.hTok, START + (g + 1) * DC)
                pe.wait_ge(s_sb, START + g)
                for c in range(DC):
                    i = nc.tensor.matmul(ps_s[0:E, :], gate_w[:, c, :], hT[:, c, ds(g * GT, GT)],
                                         start=(c == 0), stop=(c == DC - 1))
                i.then_inc(s_mm, 1)
            pe.wait_ge(s_sb, START + NG)
            for b in range(B):
                for j in range(TB):
                    i = nc.tensor.transpose(ps_x[:, j % G * 2 + j // G, b, :], scT[:, (b * TB + j) * P:(b * TB + j + 1) * P],
                                            ident[0:E, 0:E])
            i.then_inc(x_tr, 1)
            pe.wait_ge(p_ok, START + 1)
            for j in range(G):
                i = nc.tensor.transpose(ps_p[0:2 * R, j * P:(j + 1) * P],
                                        pr[:, 2 * j:2 * j + 2, :, :].rearrange("p h b e -> p (h b e)"), ident[:, :])
            i.then_inc(p_tr, 1)
            pe.wait_ge(top_ok, START + 1)
            for s, src in enumerate((rowf, vals)):
                for c in range(C):
                    i = nc.tensor.transpose(ps_i[:, s, c, :], src[:, c * P:(c + 1) * P], ident[0:2 * R, 0:2 * R])
            i.then_inc(i_tr, 1)
            pe.wait_ge(i_ok, START + 1)
            for s in range(2):
                for c in range(C):
                    i = nc.tensor.matmul(ps_r[:, s, C - 1 - c, :], reverse[:, :], both[:, s, c, R:2 * R],
                                         start=True, stop=True)
            i.then_inc(r_mm, 1)


def experts(nc, ph, ident, E, C, M, h_rows, acc, idxT, gT, raw):
    HV = 2
    BH = B // HV
    NH = 4
    w1p = [[ph.sb(f"w1_{n}{i}", [P, DC, M * P], F32R) for n in ("top", "rest")] for i in range(2)]
    w2p = [[ph.sb(f"w2_{n}{i}", [P, M, D], F32R) for n in ("top", "rest")] for i in range(2)]
    cols = ph.sb("cols", [P, B, C], U32)
    xg = ph.sb("xg", [P, HV, G, D])
    xT = [ph.sb(f"xT_{n}", [P, DC, GT], F32R) for n in ("top", "rest")]
    hid = ph.sb("hid", [P, NH, GT])
    HT = [ph.sb(f"HT_{n}", [P, M, GT], F32R) for n in ("top", "rest")]
    ys = ph.sb("ys", [P, HV, G, D])
    ps_t = ph.ps("ps_t", [P, DC, GT])
    ps_h = ph.ps("ps_h", [P, NH, GT])
    ps_o = ph.ps("ps_o", [P, 2, GT])
    gathered = [ph.dma_sem(f"gathered{v}") for v in range(HV)]
    added = [ph.dma_sem(f"added{v}") for v in range(HV)]
    cols_ok, tr, x_top, x_rest = ph.sem("cols_ok"), ph.sem("tr"), ph.sem("x_top"), ph.sem("x_rest")
    w_top, w_rest = ph.sem("w_top"), ph.sem("w_rest")
    h_mm, h_top, h_rest = ph.sem("h_mm"), ph.sem("h_top"), ph.sem("h_rest")
    o_mm, y_ok = ph.sem("o_mm"), ph.sem("y_ok")
    passed = ph.sem("passed")
    EP = E // 2
    PARTS3 = ((0, 0), (0, 1), (1, 0))

    def quarter(s, k):
        if k < 2:
            return [t[:, k, :] for t in (raw.w1, *w1p[s])]
        half = slice((k - 2) * M // 2, (k - 1) * M // 2)
        return [t[:, half, :] for t in (raw.w2, *w2p[s])]

    def expert_turns(eng, turn):
        for s in range(2):
            turn(s, s, s == 0, False)
        with eng.Fori(1, EP - 1) as ep:
            for s in range(2):
                turn(ep * 2 + s, s, False, False)
        for s in range(2):
            turn(E - 2 + s, s, False, s == 1)
    cells = lambda t, e: t[:, :, :].rearrange("p c (b e) -> p b c e", e=E)[:, :, :, ds(e, 1)]

    with nc.Block() as block:
        @block.sync
        def _(sp):
            ph.start(sp)

            with sp.Fori(1, E) as e:
                sp.wait_ge(w_rest, START + 4 * (e - 1) + 2)
                raw.load_w1(sp, e)
                sp.wait_ge(w_rest, START + 4 * (e - 1) + 4)
                raw.load_w2(sp, e)
            sp.wait_ge(added[0], 16 * G * E)
            sp.wait_ge(added[1], 16 * G * E)

        @block.gpsimd
        def _(pool):
            def gather(e, v):
                pool.wait_ge(tr, START + HV * (e - 1) + v + 1)
                pool.sem_inc(passed, 1)
                rows(v)

            def rows(v):
                for k in range(G):
                    pool.indirect_dma_start(out=xg[:, v, k, :], out_offset=None, in_=h_rows[:, :],
                                            in_offset=bass.IndirectOffsetOnAxis(
                                                ap=cols[:, BH * v + k // C, k % C:k % C + 1], axis=0)
                                            ).then_inc(gathered[v], 16)

            def scatter(e, v, first=False):
                if not first:
                    pool.wait_ge(added[v], 16 * G * e)
                for k in range(G):
                    pool.wait_ge(y_ok, START + (e * HV + v) * G + k + 1)
                    pool.sem_inc(passed, 1)
                    pool.indirect_dma_start(out=acc[:, :], out_offset=bass.IndirectOffsetOnAxis(
                                                ap=keep[:, BH * v + k // C, k % C:k % C + 1], axis=0),
                                            in_=ys[:, v, k, :], in_offset=None,
                                            compute_op=ALU.add).then_inc(added[v], 16)
            keep = ph.sb("keep", [P, B, C], U32)

            nc.gpsimd.tensor_copy(cols[:, :, :].unsqueeze(3), cells(idxT, 0)).then_inc(cols_ok, 1)
            pool.wait_ge(cols_ok, START + 1)
            for v in range(HV):
                rows(v)
            def step(e, first):
                for v in range(HV):
                    pool.wait_ge(gathered[v], 16 * G * (e + 1))
                    if not first:
                        pool.wait_ge(added[v], 16 * G * e)
                pool.sem_inc(passed, 1)
                nc.gpsimd.tensor_copy(keep[:, :, :], cols[:, :, :]).then_inc(cols_ok, 1)
                pool.wait_ge(cols_ok, START + 2 * e + 2)
                pool.sem_inc(passed, 1)
                nc.gpsimd.tensor_copy(cols[:, :, :].unsqueeze(3), cells(idxT, e + 1)).then_inc(cols_ok, 1)
                pool.wait_ge(cols_ok, START + 2 * e + 3)
                pool.sem_inc(passed, 1)
                for v in range(HV):
                    gather(e + 1, v)
                    scatter(e, v, first)
            step(0, True)
            with pool.Fori(1, E - 1) as e:
                step(e, False)
            for v in range(HV):
                pool.wait_ge(gathered[v], 16 * G * E)
                pool.wait_ge(added[v], 16 * G * (E - 1))
            nc.gpsimd.tensor_copy(keep[:, :, :], cols[:, :, :]).then_inc(cols_ok, 1)
            pool.wait_ge(cols_ok, START + 2 * E)
            for v in range(HV):
                scatter(E - 1, v)

        @block.vector
        def _(dve):
            def weights(e, s, ks):
                for k in ks:
                    dve.wait_ge(w_top, START + 4 * e + k + 1)
                    whole, top, rest = quarter(s, k)
                    nc.vector.tensor_tensor(rest, whole, top.bitcast(F32), ALU.subtract).then_inc(w_rest, 1)

            def transposed(i):
                for c in range(DC):
                    dve.wait_ge(x_top, START + i * DC + c + 1)
                    nc.vector.tensor_tensor(xT[1][:, c, :], ps_t[:, c, :], xT[0][:, c, :].bitcast(F32),
                                            ALU.subtract).then_inc(x_rest, 1)

            def hidden(i):
                for m in range(M):
                    dve.wait_ge(h_top, START + i * M + m + 1)
                    nc.vector.tensor_tensor(HT[1][:, m, :], hid[:, m % NH, :], HT[0][:, m, :].bitcast(F32),
                                            ALU.subtract).then_inc(h_rest, 1)

            def weigh(e, v, first):
                if not first:
                    dve.wait_ge(added[v], 16 * G * e)
                for k in range(G):
                    if k % 2 == 0:
                        dve.wait_ge(o_mm, START + (e * HV + v) * 2 + k // 2 + 1)
                    b, c = BH * v + k // C, k % C
                    nc.vector.tensor_scalar(ys[:, v, k, :], ps_o[:, k // 2, (k % 2) * D:(k % 2 + 1) * D],
                                            gT[:, c, ds(b * E + e, 1)], None, ALU.mult).then_inc(y_ok, 1)

            def turn(e, s, first, last):
                for v in range(HV):
                    i = e * HV + v
                    hidden(i)
                    if not (last and v == 1):
                        transposed(i + 1)
                    if not last:
                        weights(e + 1, 1 - s, (2 * v, 2 * v + 1))
                    weigh(e, v, first)
            weights(0, 0, range(2))
            transposed(0)
            weights(0, 0, range(2, 4))
            expert_turns(dve, turn)

        @block.scalar
        def _(act):
            def weights(e, s, ks):
                for k in ks:
                    if k % 2 == 0:
                        act.wait_ge(raw.w2_in if k else raw.w1_in, 16 * (e + 1))
                    whole, top, _ = quarter(s, k)
                    nc.scalar.copy(top, whole).then_inc(w_top, 1)

            def transposed(i):
                act.wait_ge(tr, START + i + 1)
                for c in range(DC):
                    nc.scalar.copy(xT[0][:, c, :], ps_t[:, c, :]).then_inc(x_top, 1)

            def hidden(i):
                for m in range(M):
                    act.wait_ge(h_mm, START + i * M + m + 1)
                    act.wait_ge(h_rest, START + i * M + m + 1 - NH)
                    nc.scalar.activation(hid[:, m % NH, :], ps_h[:, m % NH, :], ACT.Gelu_apprx_tanh)
                    nc.scalar.activation(HT[0][:, m, :], ps_h[:, m % NH, :], ACT.Gelu_apprx_tanh).then_inc(h_top, 1)

            def turn(e, s, first, last):
                for v in range(HV):
                    i = e * HV + v
                    hidden(i)
                    if not (last and v == 1):
                        transposed(i + 1)
                    if not last:
                        weights(e + 1, 1 - s, (2 * v, 2 * v + 1))
            weights(0, 0, range(2))
            transposed(0)
            weights(0, 0, range(2, 4))
            expert_turns(act, turn)

        @block.tensor
        def _(pe):
            def transposes(e, i, v):
                pe.wait_ge(gathered[v], 16 * G * (e + 1))
                pe.wait_ge(x_rest, START + i * DC)
                for c in range(DC):
                    for k in range(G):
                        x = nc.tensor.transpose(ps_t[:, c, k * P:(k + 1) * P], xg[:, v, k, c * P:(c + 1) * P],
                                                ident[:, :])
                x.then_inc(tr, 1)

            def turn(e, s, first, last):
                for v in range(HV):
                    i = e * HV + v
                    if v == 0:
                        pe.wait_ge(w_rest, START + 4 * e + 2)
                    pe.wait_ge(x_rest, START + (i + 1) * DC)
                    for m in range(M):
                        pe.wait_ge(h_top, START + i * M + m + 1 - NH)
                        n = 0
                        for c in range(DC):
                            for wp, xp in PARTS3:
                                x = nc.tensor.matmul(ps_h[:, m % NH, :], w1p[s][wp][:, c, m * P:(m + 1) * P],
                                                     xT[xp][:, c, :], start=(n == 0), stop=(n == 3 * DC - 1))
                                n += 1
                        x.then_inc(h_mm, 1)
                    if not (last and v == 1):
                        transposes(e + v, i + 1, 1 - v)
                    if v == 0:
                        pe.wait_ge(w_rest, START + 4 * e + 4)
                    pe.wait_ge(y_ok, START + i * G)
                    for m in range(M):
                        pe.wait_ge(h_rest, START + i * M + m + 1)
                        for k in range(G):
                            for n, (hp, wp) in enumerate(PARTS3):
                                x = nc.tensor.matmul(ps_o[:, k // 2, (k % 2) * D:(k % 2 + 1) * D],
                                                     HT[hp][:, m, k * P:(k + 1) * P], w2p[s][wp][:, m, :],
                                                     start=(m == 0 and k % 2 == 0 and n == 0),
                                                     stop=(m == M - 1 and k % 2 == 1 and n == 2))
                            if m == M - 1 and k % 2:
                                x.then_inc(o_mm, 1)
            transposes(0, 0, 0)
            expert_turns(pe, turn)


def add_rounded(nc, ph, X, acc):
    A = ph.sb("A", [P, NG, G, D])
    A16 = ph.sb("A16", [P, NG, G, D], BF16)
    loads = [ph.dma_sem(f"loads{g}") for g in range(NG)]
    rounded = ph.sem("rounded")
    with nc.Block() as block:
        @block.sync
        def _(sp):
            ph.start(sp)
            for g in range(NG):
                sp.dma_start(A[:, g, :, :], acc[g * GT:(g + 1) * GT, :].rearrange("(j p) d -> p j d", p=P)
                             ).then_inc(loads[g], 16)

        @block.vector
        def _(dve):
            for g in range(NG):
                dve.wait_ge(loads[g], 16)
                nc.vector.tensor_copy(A16[:, g, :, :], A[:, g, :, :]).then_inc(rounded, 1)
                dve.wait_ge(rounded, START + g + 1)
                nc.vector.tensor_tensor(X[:, g * G:(g + 1) * G, :], X[:, g * G:(g + 1) * G, :], A16[:, g, :, :],
                                        ALU.add)


PARTS = 3
PAIRS = [(0, 0), (1, 0), (2, 0), (0, 1), (1, 1), (0, 2)]
STACK = len(PAIRS) * HD


def attention(nc, ph, X, ident, a, kind):
    parts = nc.dram_tensor(f"{ph.name}_parts", (2, PARTS, B * D, T), BF16, kind="Internal").ap()
    V = ph.sb("V", [P, B, H, TB, HD + 1])
    with ExitStack() as own:
        if kind == "decay":
            project_latent(nc, Phase(nc, own, ph.name + "p"), X, ident, a, parts, V)
        else:
            project_rotary(nc, Phase(nc, own, ph.name + "p"), X, ident, a, parts, V)
    AO = ph.sb("AO", [P, B, TB, H, HD])
    with ExitStack() as own:
        if kind == "decay":
            heads_decay(nc, Phase(nc, own, ph.name + "h"), ident, a, parts, V, AO)
        else:
            heads_window(nc, Phase(nc, own, ph.name + "h"), ident, a, parts, V, AO)
    with ExitStack() as own:
        project_out(nc, Phase(nc, own, ph.name + "o"), X, ident,
                    a["L0_attn_a_W_o"] if kind == "decay" else a["out_wT"], AO)


class Split:

    def __init__(self, ph, parts):
        self.nc, self.parts = ph.nc, parts
        self.F = [ph.sb(f"sp_F{s}", [P, 2, DC, GT]) for s in range(2)]
        self.R = [ph.sb(f"sp_R{s}", [P, 2, DC, GT]) for s in range(2)]
        self.out = [[ph.sb(f"sp_{n}{s}", [P, 2, DC, GT], BF16) for s in range(2)] for n in range(PARTS)]
        self.f_ok = ph.sem("sp_f")
        self.first, self.rest = ph.sem("sp_first"), ph.sem("sp_rest")
        self.second, self.third = ph.sem("sp_second"), ph.sem("sp_third")
        self.GROUP = 16 * 2 * PARTS
        self.written = [ph.dma_sem(f"sp_written{s}", 16) for s in range(2)]

    def scalar_first(self, act, b, s):
        act.wait_ge(self.written[s], 16 + self.GROUP * b)
        act.wait_ge(self.f_ok, START + 2 * (b * 2 + s) + 2)
        self.nc.scalar.copy(self.out[0][s][:, :, :, :], self.F[s][:, :, :, :]).then_inc(self.first, 1)

    def scalar_second(self, act, g, s):
        act.wait_ge(self.rest, START + g + 1)
        self.nc.scalar.copy(self.out[1][s][:, :, :, :], self.R[s][:, :, :, :]).then_inc(self.second, 1)

    def vector(self, dve, g, s):
        dve.wait_ge(self.first, START + g + 1)
        dve.wait_ge(self.third, START + g - 1)
        self.nc.vector.tensor_tensor(self.R[s][:, :, :, :], self.F[s][:, :, :, :], self.out[0][s][:, :, :, :],
                                     ALU.subtract).then_inc(self.rest, 1)

    def pool(self, pool, g, s):
        pool.wait_ge(self.second, START + g + 1)
        self.nc.gpsimd.tensor_tensor(self.out[2][s][:, :, :, :], self.R[s][:, :, :, :], self.out[1][s][:, :, :, :],
                                     ALU.subtract).then_inc(self.third, 1)

    def sync(self, sp, b, h):
        for n, done in enumerate((self.first, self.second, self.third)):
            sp.wait_ge(done, START + b * 2 + h + 1)
            for w in range(2):
                sp.dma_start(self.parts[w, n, ds(b * D, D), h * GT:(h + 1) * GT].rearrange("(c p) t -> p c t", p=P),
                             self.out[n][h][:, w, :, :]).then_inc(self.written[h], 16)

    def all_written(self, sp):
        for s in range(2):
            sp.wait_ge(self.written[s], 16 + self.GROUP * B)


def batch_turns(eng, turn):
    for h in range(2):
        turn(0, h, h == 0, False)
    with eng.Fori(1, B - 1) as b:
        for h in range(2):
            turn(b, h, False, False)
    for h in range(2):
        turn(B - 1, h, False, h == 1)


def project_latent(nc, ph, X, ident, a, parts, V):
    DL = a["L0_attn_a_W_down_kv"].shape[1]
    HB = T // GT
    hT = ph.sb("hT", [P, DC, B * T])
    wq = ph.sb("wq", [P, DC, D])
    wkT, wvT = ph.sb("wkT", [P, DC, D]), ph.sb("wvT", [P, DC, D])
    wd = ph.sb("wd", [P, DC, DL])
    wuk, wuv = ph.sb("wuk", [DL, D]), ph.sb("wuv", [DL, D])
    wlat = ph.sb("wlat", [P, DC, DL])
    latT = ph.sb("latT", [DL, GT])
    ps_t = ph.ps("ps_t", [P, DC, GT])
    ps_q = ph.ps("ps_q", [P, DC, GT])
    ps_k = ph.ps("ps_k", [P, DC, GT])
    ps_l = ph.ps("ps_l", [P, GT])
    ps_v = ph.ps("ps_v", [P, 2, D])
    ln = LayerNorm(ph, X, ident, hT, ps_t)
    split = Split(ph, parts)
    weights = ph.dma_sem("weights")
    consts, wl_mm = ph.sem("consts"), ph.sem("wl_mm")
    q_mm, k_mm, l_mm, l_ok = ph.sem("q_mm"), ph.sem("k_mm"), ph.sem("l_mm"), ph.sem("l_ok")
    v_mm, v_ok = ph.sem("v_mm"), ph.sem("v_ok")
    part = lambda w: w.rearrange("(c p) n -> p c n", p=P)
    pairs = [(wkT[:, :, :], part(a["WkT"])), (wvT[:, :, :], part(a["WvT_a"])), (wq[:, :, :], part(a["L0_attn_a_W_q"])),
             (wd[:, :, :], part(a["L0_attn_a_W_down_kv"])), (wuk[:, :], a["L0_attn_a_W_up_k"]),
             (wuv[:, :], a["L0_attn_a_W_up_v"])]
    loaded = 16 * len(pairs)

    with nc.Block() as block:
        @block.sync
        def _(sp):
            ph.start(sp)
            load_once(sp, weights, pairs)
            with sp.Fori(0, B) as b:
                for h in range(HB):
                    split.sync(sp, b, h)
            split.all_written(sp)

        @block.gpsimd
        def _(pool):
            ln.pool_setup()
            pool.wait_ge(ln.rs, START + 1)
            nc.gpsimd.memset(V[:, :, :, :, HD], 1.0)
            ln.pool(pool, 0)

            def turn(b, h, first, last):
                g = b * HB + h
                if not last:
                    ln.pool(pool, g + 1)
                if not first:
                    split.pool(pool, g - 1, 1 - h)
            batch_turns(pool, turn)
            split.pool(pool, NG - 1, 1)

        @block.vector
        def _(dve):
            dve.wait_ge(weights, loaded)
            nc.vector.tensor_tensor(wkT[:, :, :], wkT[:, :, :], wvT[:, :, :], ALU.add).then_inc(consts, 1)
            ln.vector(dve, 0)
            dve.wait_ge(wl_mm, START + 1)
            nc.vector.tensor_copy(wlat[:, :, :], ps_q[:, 0, 0:DC * DL].rearrange("p (c n) -> p c n", c=DC)
                                  ).then_inc(consts, 1)

            def turn(b, h, first, last):
                g = b * HB + h
                if not last:
                    ln.vector(dve, g + 1)
                for k in range(G // 2):
                    dve.wait_ge(v_mm, START + g * (G // 2) + k + 1)
                    for j in range(2):
                        nc.vector.tensor_copy(V[:, ds(b, 1), :, h * G + 2 * k + j, 0:HD],
                                              ps_v[:, j, :].rearrange("p (a h d) -> p a h d", h=H, a=1)
                                              ).then_inc(v_ok, 1)
                split.vector(dve, g, h)
            batch_turns(dve, turn)

        @block.scalar
        def _(act):
            def turn(b, h, first, last):
                g = b * HB + h
                act.wait_ge(l_mm, START + g + 1)
                act.wait_ge(v_mm, START + g * (G // 2))
                nc.scalar.copy(latT[:, :], ps_l[0:DL, :]).then_inc(l_ok, 1)
                act.wait_ge(split.third, START + g - 1)
                act.wait_ge(q_mm, START + g + 1)
                nc.scalar.copy(split.F[h][:, 0, :, :], ps_q[:, :, :]).then_inc(split.f_ok, 1)
                act.wait_ge(k_mm, START + g + 1)
                nc.scalar.copy(split.F[h][:, 1, :, :], ps_k[:, :, :]).then_inc(split.f_ok, 1)
                if not last:
                    ln.scalar(act, g + 1)
                split.scalar_first(act, b, h)
                if not first:
                    split.scalar_second(act, g - 1, 1 - h)
            ln.scalar(act, 0)
            batch_turns(act, turn)
            split.scalar_second(act, NG - 1, 1)

        @block.tensor
        def _(pe):
            pe.wait_ge(weights, loaded)
            pe.wait_ge(consts, START + 1)
            for c in range(DC):
                for k in range(DC):
                    i = nc.tensor.matmul(ps_q[:, 0, c * DL:(c + 1) * DL], wkT[:, k, c * P:(c + 1) * P],
                                         wd[:, k, :], start=(k == 0), stop=(k == DC - 1))
            i.then_inc(wl_mm, 1)
            pe.wait_ge(consts, START + 2)

            def turn(g, last):
                pe.wait_ge(ln.hTok, START + (g + 1) * DC)
                pe.wait_ge(l_ok, START + g)
                for k in range(DC):
                    i = nc.tensor.matmul(ps_l[0:DL, :], wlat[:, k, :], hT[:, k, ds(g * GT, GT)],
                                         start=(k == 0), stop=(k == DC - 1))
                i.then_inc(l_mm, 1)
                pe.wait_ge(split.f_ok, START + 2 * g)
                for c in range(DC):
                    for k in range(DC):
                        i = nc.tensor.matmul(ps_q[:, c, :], wq[:, k, c * P:(c + 1) * P], hT[:, k, ds(g * GT, GT)],
                                             start=(k == 0), stop=(k == DC - 1))
                i.then_inc(q_mm, 1)
                pe.wait_ge(l_ok, START + g + 1)
                for c in range(DC):
                    i = nc.tensor.matmul(ps_k[:, c, :], wuk[:, c * P:(c + 1) * P], latT[:, :], start=True, stop=True)
                i.then_inc(k_mm, 1)
                if not last:
                    ln.tensor(pe, g + 1)
                for k in range(G // 2):
                    pe.wait_ge(v_ok, START + g * G + 2 * k)
                    for j in range(2):
                        t = (2 * k + j) * P
                        i = nc.tensor.matmul(ps_v[:, j, :], latT[:, t:t + P], wuv[:, :], start=True, stop=True)
                    i.then_inc(v_mm, 1)
            ln.tensor(pe, 0)
            with pe.Fori(0, NG - 1) as g:
                turn(g, False)
            turn(NG - 1, True)


def project_rotary(nc, ph, X, ident, a, parts, V):
    HB = T // GT
    hT = ph.sb("hT", [P, 2, DC, GT])
    w = ph.sb("w", [P, DC, 3 * D])
    wr = ph.sb("wr", [P, DC, 2 * D])
    cos, sin = ph.sb("cos", [P, T]), ph.sb("sin", [P, T])
    AB = ph.sb("AB", [P, 2, 2, DC, GT])
    ps_t = ph.ps("ps_t", [P, DC, GT])
    ps_q, ps_r = ph.ps("ps_q", [P, DC, GT]), ph.ps("ps_r", [P, DC, GT])
    ps_v = ph.ps("ps_v", [P, 2, D])
    ln = LayerNorm(ph, X, ident, hT, ps_t)
    split = Split(ph, parts)
    weights = ph.dma_sem("weights")
    consts, r_mm, ab_ok = ph.sem("consts"), ph.sem("r_mm"), ph.sem("ab_ok")
    v_mm, v_ok = ph.sem("v_mm"), ph.sem("v_ok")
    pairs = [(w[:, :, :], a["qkv_wT"].rearrange("(c p) n -> p c n", p=P)), (cos[:, :], a["cos"]), (sin[:, :], a["sin"])]
    loaded = 16 * len(pairs)

    with nc.Block() as block:
        @block.sync
        def _(sp):
            ph.start(sp)
            load_once(sp, weights, pairs)
            with sp.Fori(0, B) as b:
                for h in range(HB):
                    split.sync(sp, b, h)
            split.all_written(sp)

        @block.gpsimd
        def _(pool):
            ln.pool_setup()
            pool.wait_ge(ln.rs, START + 1)
            nc.gpsimd.memset(V[:, :, :, :, HD], 1.0)
            ln.pool(pool, 0)

            def turn(b, h, first, last):
                g = b * HB + h
                if not last:
                    ln.pool(pool, g + 1)
                pool.wait_ge(split.third, START + g - 1)
                for s in range(2):
                    pool.wait_ge(ab_ok, START + 2 * g + s + 1)
                    nc.gpsimd.tensor_tensor(split.F[h][:, s, :, :], AB[:, s, 0, :, :], AB[:, s, 1, :, :],
                                            ALU.add).then_inc(split.f_ok, 1)
                if not first:
                    split.pool(pool, g - 1, 1 - h)
            batch_turns(pool, turn)
            split.pool(pool, NG - 1, 1)

        @block.vector
        def _(dve):
            dve.wait_ge(weights, loaded)
            pair = lambda t: t[:, :, 0:2 * D].rearrange("p c (n two) -> p c n two", two=2)
            nc.vector.tensor_scalar(pair(wr)[:, :, :, 0], pair(w)[:, :, :, 1], -1.0, None, ALU.mult).then_inc(consts, 1)
            nc.vector.tensor_copy(pair(wr)[:, :, :, 1], pair(w)[:, :, :, 0]).then_inc(consts, 1)
            ln.vector(dve, 0)

            def turn(b, h, first, last):
                g = b * HB + h
                if not last:
                    ln.vector(dve, g + 1)
                both = lambda t: t[:, h * GT:(h + 1) * GT].unsqueeze(1).to_broadcast([P, DC, GT])
                for s in range(2):
                    dve.wait_ge(split.f_ok, START + 2 * g + s - 1)
                    dve.wait_ge(r_mm, START + 2 * g + s + 1)
                    nc.vector.tensor_tensor(AB[:, s, 0, :, :], ps_q[:, :, :], both(cos), ALU.mult)
                    nc.vector.tensor_tensor(AB[:, s, 1, :, :], ps_r[:, :, :], both(sin), ALU.mult).then_inc(ab_ok, 1)
                for k in range(G // 2):
                    dve.wait_ge(v_mm, START + g * (G // 2) + k + 1)
                    for j in range(2):
                        nc.vector.tensor_copy(V[:, ds(b, 1), :, h * G + 2 * k + j, 0:HD],
                                              ps_v[:, j, :].rearrange("p (a h d) -> p a h d", h=H, a=1)
                                              ).then_inc(v_ok, 1)
                split.vector(dve, g, h)
            batch_turns(dve, turn)

        @block.scalar
        def _(act):
            def turn(b, h, first, last):
                g = b * HB + h
                if not last:
                    ln.scalar(act, g + 1, (h + 1) % 2)
                split.scalar_first(act, b, h)
                if not first:
                    split.scalar_second(act, g - 1, 1 - h)
            ln.scalar(act, 0, 0)
            batch_turns(act, turn)
            split.scalar_second(act, NG - 1, 1)

        @block.tensor
        def _(pe):
            pe.wait_ge(weights, loaded)
            pe.wait_ge(consts, START + 2)

            def turn(g, h, last):
                pe.wait_ge(ln.hTok, START + (g + 1) * DC)
                for s in range(2):
                    pe.wait_ge(ab_ok, START + 2 * g + s)
                    for out, weight in ((ps_q, w), (ps_r, wr)):
                        for c in range(DC):
                            for k in range(DC):
                                n = s * D + c * P
                                i = nc.tensor.matmul(out[:, c, :], weight[:, k, n:n + P], hT[:, h, k, :],
                                                     start=(k == 0), stop=(k == DC - 1))
                    i.then_inc(r_mm, 1)
                if not last:
                    ln.tensor(pe, g + 1)
                for k in range(G // 2):
                    pe.wait_ge(v_ok, START + g * G + 2 * k)
                    for j in range(2):
                        t = (2 * k + j) * P
                        for c in range(DC):
                            i = nc.tensor.matmul(ps_v[:, j, :], hT[:, h, c, t:t + P], w[:, c, 2 * D:3 * D],
                                                 start=(c == 0), stop=(c == DC - 1))
                    i.then_inc(v_mm, 1)
            ln.tensor(pe, 0)
            with pe.Fori(0, B - 1) as b:
                for h in range(HB):
                    turn(b * HB + h, h, False)
            for h in range(HB):
                turn((B - 1) * HB + h, h, h == HB - 1)


def heads_decay(nc, ph, ident, a, parts, V, AO):
    qs = [ph.sb(f"qs{i}", [STACK, T], BF16) for i in range(2)]
    ks = [ph.sb(f"ks{i}", [STACK, T], BF16) for i in range(2)]
    table = ph.sb("table", [P, 2 * T - P])
    gather = ph.sb("gather", [P, HD + 1])
    NBUF = 4
    SD = [ph.sb(f"SD{i}", [P, T]) for i in range(NBUF)]
    PM = [ph.sb(f"PM{i}", [P, T]) for i in range(NBUF)]
    PT = [ph.sb(f"PT{i}", [P, TB, GT]) for i in range(2)]
    W = 32
    Vs = [ph.sb(f"Vs{i}", [P, TB, W]) for i in range(2)]
    OT = ph.sb("OT", [P, GT])
    U = 2 * TB
    mx, nb = ph.sb("mx", [P, U]), ph.sb("nb", [P, U])
    minus, rc = ph.sb("minus", [P, 1]), ph.sb("rc", [P, G])
    ps_s = [ph.ps(f"ps_s{i}", [P, 2, GT]) for i in range(2)]
    ps_t = ph.ps("ps_t", [P, 2, GT])
    ps_v, ps_o = ph.ps("ps_v", [P, GT]), ph.ps("ps_o", [P, GT])
    tabled = ph.dma_sem("tabled")
    loads = [ph.dma_sem(f"loads{i}") for i in range(2)]
    s_mm, m_ok, nb_ok, e_ok = ph.sem("s_mm"), ph.sem("m_ok"), ph.sem("nb_ok"), ph.sem("e_ok")
    ta_mm, tb_mm, ta_ok, tb_ok = ph.sem("ta_mm"), ph.sem("tb_mm"), ph.sem("ta_ok"), ph.sem("tb_ok")
    pv_mm, ot_ok, o_mm, n_ok = ph.sem("pv_mm"), ph.sem("ot_ok"), ph.sem("o_mm"), ph.sem("n_ok")
    passed, minus_ok, vs_ok = ph.sem("passed"), ph.sem("minus_ok"), ph.sem("vs_ok")
    NP = B * H // 2
    ND = 2 * len(PAIRS)
    UH = U // G

    with nc.Block() as block:
        @block.sync
        def _(sp):
            ph.start(sp)
            sp.dma_start(table[:, :], a["decay"]).then_inc(tabled, 16)
            sp.dma_start(gather[:, :], a["gather"]).then_inc(tabled, 16)

            def load(n, s):
                rows = ds(n * HD, HD)
                for r, both in enumerate(PAIRS):
                    for which, (st, part) in enumerate(zip((qs[s], ks[s]), both)):
                        sp.dma_start(st[r * HD:(r + 1) * HD, :], parts[which, part, rows, :]).then_inc(loads[s], 16)
            load(0, 0)
            load(1, 1)
            with sp.Fori(1, NP) as pr:
                for s in range(2):
                    sp.wait_ge(s_mm, START + (pr * 2 + s - 1) * TB)
                    load(pr * 2 + s, s)

        @block.gpsimd
        def _(pool):
            Vn = V[:, :, :, :, :].rearrange("p b h t d -> p (b h) t d")
            for s in range(2):
                nc.gpsimd.memset(Vs[s][:, :, :], 0.0).then_inc(minus_ok, 1)
            nc.gpsimd.memset(minus[:, :], -1.0).then_inc(minus_ok, 1)
            pool.wait_ge(minus_ok, START + 3)
            with pool.Fori(0, NP) as pr:
                for u in range(U):
                    if u % TB == 1:
                        s = u // TB
                        pool.wait_ge(pv_mm, START + (pr * 2 + s) * 2 - 2)
                        pool.sem_inc(passed, 1)
                        nc.gpsimd.tensor_copy(Vs[s][:, :, 0:HD + 1],
                                              Vn[:, ds(pr * 2 + s, 1), :, :].rearrange("p a t d -> p (a t) d")
                                              ).then_inc(vs_ok, 1)
                    pool.wait_ge(m_ok, START + pr * U + u + 1)
                    nc.gpsimd.tensor_tensor(nb[:, u:u + 1], mx[:, u:u + 1], minus[:, :], ALU.mult).then_inc(nb_ok, 1)

        @block.vector
        def _(dve):
            dve.wait_ge(tabled, 32)

            def most(i, u):
                dve.wait_ge(s_mm, START + i + 1)
                dve.wait_ge(e_ok, START + i + 1 - NBUF)
                dve.sem_inc(passed, 1)
                t = u % TB
                nc.vector.tensor_tensor_reduce(SD[u % NBUF][:, :],
                                               ps_s[u % 2][:, :, :].rearrange("p a n -> p (a n)"),
                                               table[:, (TB - 1 - t) * P:(TB - 1 - t) * P + T], 1.0, -3e38,
                                               ALU.mult, ALU.max, accum_out=mx[:, u:u + 1]).then_inc(m_ok, 1)

            def copy(i, u):
                dve.wait_ge(ta_mm, START + i + 1)
                q = u % G * P
                nc.vector.tensor_copy(PT[u // G % 2][:, 0:G, q:q + P],
                                      ps_t[:, 0, :].rearrange("p (k q) -> p k q", k=G)).then_inc(ta_ok, 1)

            def norm(n, half, hh):
                dve.wait_ge(o_mm, START + hh + 1)
                o = ps_o[:, 0:G * (HD + 1)].rearrange("p (t d) -> p t d", t=G)
                nc.vector.reciprocal(rc[:, :], o[:, :, HD])
                dve.drain()
                to = AO[:, ds(n // H, 1), half * G:(half + 1) * G, ds(n % H, 1), :].rearrange("p b t h d -> p (b t h) d")
                nc.vector.tensor_tensor(to, o[:, :, 0:HD],
                                        rc[:, :].unsqueeze(2).to_broadcast([P, G, HD]), ALU.mult).then_inc(n_ok, 1)

            def turn(pr, first, last):
                for u in range(U):
                    i = pr * U + u
                    if not (last and u >= U - 2):
                        most(i + 2, (u + 2) % U)
                    copy(i, u)
                    if u % G == 0 and not (first and u < 2 * G):
                        v = u // G - 2
                        norm(pr * 2 + v // 2, v % 2, pr * UH + v)
            most(0, 0)
            most(1, 1)
            turn(0, True, False)
            with dve.Fori(1, NP - 1) as pr:
                turn(pr, False, False)
            turn(NP - 1, False, True)
            norm(NP * 2 - 1, 0, NP * UH - 2)
            norm(NP * 2 - 1, 1, NP * UH - 1)

        @block.scalar
        def _(act):
            def exp(i, u):
                act.wait_ge(nb_ok, START + i + 1)
                act.wait_ge(tb_mm, START + i + 1 - NBUF)
                nc.scalar.activation(PM[u % NBUF][:, :], SD[u % NBUF][:, :], ACT.Exp, bias=nb[:, u:u + 1]
                                     ).then_inc(e_ok, 1)

            def copy(i, u):
                act.wait_ge(tb_mm, START + i + 1)
                q = u % G * P
                nc.scalar.copy(PT[u // G % 2][:, G:, q:q + P],
                               ps_t[:, 1, :].rearrange("p (k q) -> p k q", k=G)).then_inc(tb_ok, 1)

            def collect(hh):
                act.wait_ge(pv_mm, START + hh + 1)
                nc.scalar.copy(OT[:, :], ps_v[:, :]).then_inc(ot_ok, 1)

            def turn(pr, first, last):
                for u in range(U):
                    i = pr * U + u
                    if not (last and u == U - 1):
                        exp(i + 1, (u + 1) % U)
                    copy(i, u)
                    if u % G == 2 and not (first and u < G):
                        collect(pr * UH + u // G - 1)
            exp(0, 0)
            turn(0, True, False)
            with act.Fori(1, NP - 1) as pr:
                turn(pr, False, False)
            turn(NP - 1, False, True)
            collect(NP * UH - 1)

        @block.tensor
        def _(pe):
            pe.wait_ge(tabled, 32)

            def scores(i, u):
                s, t = u // TB, u % TB
                pe.wait_ge(m_ok, START + i - 1)
                for k in range(2):
                    x = nc.tensor.matmul(ps_s[u % 2][:, k, :], qs[s][:, t * P:(t + 1) * P],
                                         ks[s][:, k * GT:(k + 1) * GT], start=True, stop=True)
                x.then_inc(s_mm, 1)

            def transposes(i, u):
                pe.wait_ge(e_ok, START + i + 1)
                for bank, out, done in ((0, ta_ok, ta_mm), (1, tb_ok, tb_mm)):
                    pe.wait_ge(out, START + i)
                    for k in range(G):
                        at = (bank * G + k) * P
                        x = nc.tensor.transpose(ps_t[:, bank, k * P:(k + 1) * P], PM[u % NBUF][:, at:at + P],
                                                ident[:, :])
                    x.then_inc(done, 1)

            def values(n, hh, v, r, i):
                if r == 0:
                    pe.wait_ge(ta_ok, START + i)
                    pe.wait_ge(tb_ok, START + i)
                    pe.wait_ge(ot_ok, START + hh)
                    if v % 2 == 0:
                        pe.wait_ge(vs_ok, START + n + 1)
                for j in range(G):
                    x = nc.tensor.matmul(ps_v[j * W:(j + 1) * W, :], Vs[v // 2][:, 2 * j + r, :],
                                         PT[v % 2][:, 2 * j + r, :], start=(r == 0), stop=(r == 1),
                                         tile_position=(0, j * W))
                if r == 1:
                    x.then_inc(pv_mm, 1)

            def gathered(hh):
                pe.wait_ge(ot_ok, START + hh + 1)
                pe.wait_ge(n_ok, START + hh)
                for t in range(G):
                    x = nc.tensor.matmul(ps_o[:, t * (HD + 1):(t + 1) * (HD + 1)], OT[:, t * P:(t + 1) * P],
                                         gather[:, :], start=True, stop=True)
                x.then_inc(o_mm, 1)

            def turn(pr, first, last):
                for u in range(U):
                    i = pr * U + u
                    if not (last and u >= U - 3):
                        if u == U - 3:
                            pe.wait_ge(loads[0], 16 * ND * (pr + 2))
                        if u == TB - 3:
                            pe.wait_ge(loads[1], 16 * ND * (pr + 1))
                        scores(i + 3, (u + 3) % U)
                    transposes(i, u)
                    if first and u < G:
                        continue
                    v, r = u // G - 1, u % G
                    if r < 2:
                        values(pr * 2 + v // 2, pr * UH + v, v % UH, r, pr * U + u - r)
                    if r == 3:
                        gathered(pr * UH + v)
            pe.wait_ge(loads[0], 16 * ND)
            scores(0, 0)
            scores(1, 1)
            scores(2, 2)
            turn(0, True, False)
            with pe.Fori(1, NP - 1) as pr:
                turn(pr, False, False)
            turn(NP - 1, False, True)
            for r in range(2):
                values(NP * 2 - 1, NP * UH - 1, UH - 1, r, NP * U)
            gathered(NP * UH - 1)


def heads_window(nc, ph, ident, a, parts, V, AO):
    NGL = 4
    WK = 2 * P + NGL
    W = 32
    qs = [ph.sb(f"qs{i}", [STACK, T], BF16) for i in range(2)]
    ks = [ph.sb(f"ks{i}", [STACK, T], BF16) for i in range(2)]
    table = ph.sb("table", [P, 3, WK])
    NBUF = 4
    SD = [ph.sb(f"SD{i}", [P, WK]) for i in range(NBUF)]
    PM = [ph.sb(f"PM{i}", [P, WK]) for i in range(NBUF)]
    PT = [ph.sb(f"PT{i}", [P, G, 2, P]) for i in range(2)]
    PG = [ph.sb(f"PG{i}", [NGL, G, P]) for i in range(2)]
    Vs = [ph.sb(f"Vs{i}", [P, TB, W]) for i in range(2)]
    OT = ph.sb("OT", [P, P])
    U = 2 * TB
    mx, nb = ph.sb("mx", [P, U]), ph.sb("nb", [P, U])
    minus, rc = ph.sb("minus", [P, 1]), ph.sb("rc", [P, G])
    ps_s = [ph.ps(f"ps_s{i}", [P, GT]) for i in range(2)]
    ps_t = [ph.ps(f"ps_t{i}", [P, 2, 2, P]) for i in range(2)]
    ps_g = [ph.ps(f"ps_g{i}", [P, 4, P]) for i in range(2)]
    ps_v, ps_o = ph.ps("ps_v", [P, GT]), ph.ps("ps_o", [P, GT])
    tabled = ph.dma_sem("tabled")
    loads = [ph.dma_sem(f"loads{i}") for i in range(2)]
    s_mm, m_ok, nb_ok, e_ok = ph.sem("s_mm"), ph.sem("m_ok"), ph.sem("nb_ok"), ph.sem("e_ok")
    t_mm, g_mm, t_ok, g_ok = ph.sem("t_mm"), ph.sem("g_mm"), ph.sem("t_ok"), ph.sem("g_ok")
    pv_mm, ot_ok, o_mm, n_ok = ph.sem("pv_mm"), ph.sem("ot_ok"), ph.sem("o_mm"), ph.sem("n_ok")
    passed, minus_ok, vs_ok = ph.sem("passed"), ph.sem("minus_ok"), ph.sem("vs_ok")
    NP = B * H // 2
    ND = 2 * len(PAIRS)
    UH = U // G
    PG_HEAD = TB // 2 - 1

    def keys(t):
        if t == 0:
            return [(0, P)]
        return [((t - 1) * P, 2 * P)] + ([(0, NGL)] if t >= 2 else [])

    def width(t):
        return sum(n for _, n in keys(t))

    with nc.Block() as block:
        @block.sync
        def _(sp):
            ph.start(sp)
            sp.dma_start(table[:, :, :], a["masks"].rearrange("p (m k) -> p m k", m=3)).then_inc(tabled, 16)

            def load(n, s):
                rows = ds(n * HD, HD)
                for r, both in enumerate(PAIRS):
                    for which, (st, part) in enumerate(zip((qs[s], ks[s]), both)):
                        sp.dma_start(st[r * HD:(r + 1) * HD, :], parts[which, part, rows, :]).then_inc(loads[s], 16)
            load(0, 0)
            load(1, 1)
            with sp.Fori(1, NP) as pr:
                for s in range(2):
                    sp.wait_ge(s_mm, START + (pr * 2 + s - 1) * TB)
                    load(pr * 2 + s, s)

        @block.gpsimd
        def _(pool):
            Vn = V[:, :, :, :, :].rearrange("p b h t d -> p (b h) t d")
            for s in range(2):
                nc.gpsimd.memset(Vs[s][:, :, :], 0.0).then_inc(minus_ok, 1)
            nc.gpsimd.memset(minus[:, :], -1.0).then_inc(minus_ok, 1)
            pool.wait_ge(minus_ok, START + 3)
            with pool.Fori(0, NP) as pr:
                for u in range(U):
                    if u % TB == 2:
                        s = u // TB
                        pool.wait_ge(pv_mm, START + (pr * 2 + s) * 2 - 2)
                        pool.sem_inc(passed, 1)
                        nc.gpsimd.tensor_copy(Vs[s][:, :, 0:HD + 1],
                                              Vn[:, ds(pr * 2 + s, 1), :, :].rearrange("p a t d -> p (a t) d")
                                              ).then_inc(vs_ok, 1)
                    pool.wait_ge(m_ok, START + pr * U + u + 1)
                    nc.gpsimd.tensor_tensor(nb[:, u:u + 1], mx[:, u:u + 1], minus[:, :], ALU.mult).then_inc(nb_ok, 1)

        @block.vector
        def _(dve):
            dve.wait_ge(tabled, 16)

            def most(i, u):
                dve.wait_ge(s_mm, START + i + 1)
                dve.wait_ge(e_ok, START + i + 1 - NBUF)
                dve.sem_inc(passed, 1)
                n = width(u % TB)
                nc.vector.tensor_tensor_reduce(SD[u % NBUF][:, 0:n], ps_s[u % 2][:, 0:n],
                                               table[:, min(u % TB, 2), 0:n], HD ** -0.5, -3e38,
                                               ALU.add, ALU.max, accum_out=mx[:, u:u + 1]).then_inc(m_ok, 1)

            def copy(pair, u):
                dve.wait_ge(t_mm, START + pair + 1)
                first = 1 if u % TB == 1 else 0
                flat = lambda t: t.rearrange("p s k q -> p (s k) q")[:, first:4, :]
                nc.vector.tensor_copy(flat(PT[u // G % 2][:, u % G - 1:u % G + 1, :, :]),
                                      flat(ps_t[u // 2 % 2][:, :, :, :])).then_inc(t_ok, 1)

            def norm(n, half, hh):
                dve.wait_ge(o_mm, START + hh + 1)
                o = ps_o[:, 0:P].rearrange("p (t d) -> p t d", t=G)
                nc.vector.reciprocal(rc[:, :], o[:, :, HD])
                dve.drain()
                to = AO[:, ds(n // H, 1), half * G:(half + 1) * G, ds(n % H, 1), :].rearrange("p b t h d -> p (b t h) d")
                nc.vector.tensor_tensor(to, o[:, :, 0:HD],
                                        rc[:, :].unsqueeze(2).to_broadcast([P, G, HD]), ALU.mult).then_inc(n_ok, 1)

            def turn(pr, first, last):
                for u in range(U):
                    if not (last and u >= U - 2):
                        most(pr * U + u + 2, (u + 2) % U)
                    if u % 2 == 1:
                        copy(pr * (U // 2) + u // 2, u)
                    if u % G == 0 and not (first and u < 2 * G):
                        v = u // G - 2
                        norm(pr * 2 + v // 2, v % 2, pr * UH + v)
            most(0, 0)
            most(1, 1)
            turn(0, True, False)
            with dve.Fori(1, NP - 1) as pr:
                turn(pr, False, False)
            turn(NP - 1, False, True)
            norm(NP * 2 - 1, 0, NP * UH - 2)
            norm(NP * 2 - 1, 1, NP * UH - 1)

        @block.scalar
        def _(act):
            def exp(i, pair, u):
                act.wait_ge(nb_ok, START + i + 1)
                act.wait_ge(t_mm, START + pair - 1)
                n = width(u % TB)
                nc.scalar.activation(PM[u % NBUF][:, 0:n], SD[u % NBUF][:, 0:n], ACT.Exp, bias=nb[:, u:u + 1]
                                     ).then_inc(e_ok, 1)

            def copy(n, u):
                k = u % TB // 2
                act.wait_ge(g_mm, START + n * PG_HEAD + k)
                nc.scalar.copy(PG[u // G % 2][:, u % G - 1:u % G + 1, :], ps_g[k % 2][0:NGL, 0:2, :]).then_inc(g_ok, 1)

            def collect(hh):
                act.wait_ge(pv_mm, START + hh + 1)
                nc.scalar.copy(OT[:, :], ps_v[:, 0:P]).then_inc(ot_ok, 1)

            def turn(pr, first, last):
                for u in range(U):
                    if not (last and u == U - 1):
                        exp(pr * U + u + 1, pr * (U // 2) + (u + 1) // 2, (u + 1) % U)
                    if u % TB > 2 and u % 2 == 1:
                        copy(pr * 2 + u // TB, u)
                    if u % G == 2 and not (first and u < G):
                        collect(pr * UH + u // G - 1)
            exp(0, 0, 0)
            turn(0, True, False)
            with act.Fori(1, NP - 1) as pr:
                turn(pr, False, False)
            turn(NP - 1, False, True)
            collect(NP * UH - 1)

        @block.tensor
        def _(pe):
            def scores(i, u):
                s, t = u // TB, u % TB
                pe.wait_ge(m_ok, START + i - 1)
                at = 0
                for k0, n in keys(t):
                    x = nc.tensor.matmul(ps_s[u % 2][:, at:at + n], qs[s][:, t * P:(t + 1) * P], ks[s][:, k0:k0 + n],
                                         start=True, stop=True)
                    at += n
                x.then_inc(s_mm, 1)

            def transposes(i, pair, n, u):
                t = u % TB
                pe.wait_ge(e_ok, START + i + 1)
                if u % 2 == 0:
                    pe.wait_ge(t_ok, START + pair - 1)
                pm, bank = PM[u % NBUF], ps_t[u // 2 % 2]
                if t >= 2:
                    if u % 2 == 0:
                        pe.wait_ge(g_ok, START + n * PG_HEAD + max(t // 2 - 2, 0))
                    y = nc.tensor.transpose(ps_g[t // 2 % 2][0:NGL, u % 2, :], pm[:, 2 * P:WK], ident[:, :])
                    if u % 2 == 1:
                        y.then_inc(g_mm, 1)
                for k in range(2 if t else 1):
                    x = nc.tensor.transpose(bank[:, u % 2, k if t else 1, :], pm[:, k * P:(k + 1) * P], ident[:, :])
                if u % 2 == 1:
                    x.then_inc(t_mm, 1)

            def values(n, hh, v):
                half = v % 2
                pe.wait_ge(t_ok, START + (hh + 1) * 2)
                pe.wait_ge(g_ok, START + n * PG_HEAD + (PG_HEAD if half else 1))
                pe.wait_ge(ot_ok, START + hh)
                if half == 0:
                    pe.wait_ge(vs_ok, START + n + 1)
                for k in (1, 0, 2):
                    for j in range(G):
                        t = half * G + j
                        if t + k < 1 or (k == 2 and t < 2):
                            continue
                        out = ps_v[j * W:(j + 1) * W, 0:P]
                        stop = k == (0 if t == 1 else 1 if t == 0 else 2)
                        if k == 2:
                            x = nc.tensor.matmul(out, Vs[v // 2][0:NGL, 0, :], PG[half][:, j, :],
                                                 start=False, stop=stop, tile_position=(0, j * W))
                        else:
                            x = nc.tensor.matmul(out, Vs[v // 2][:, t - 1 + k, :], PT[half][:, j, k, :],
                                                 start=(k == 1), stop=stop, tile_position=(0, j * W))
                x.then_inc(pv_mm, 1)

            def turned(hh):
                pe.wait_ge(ot_ok, START + hh + 1)
                pe.wait_ge(n_ok, START + hh)
                nc.tensor.transpose(ps_o[:, 0:P], OT[:, :], ident[:, :]).then_inc(o_mm, 1)

            def turn(pr, first, last):
                for u in range(U):
                    i = pr * U + u
                    if not (last and u >= U - 3):
                        if u == U - 3:
                            pe.wait_ge(loads[0], 16 * ND * (pr + 2))
                        if u == TB - 3:
                            pe.wait_ge(loads[1], 16 * ND * (pr + 1))
                        scores(i + 3, (u + 3) % U)
                    transposes(i, pr * (U // 2) + u // 2, pr * 2 + u // TB, u)
                    v = u // G - 1
                    if u % G == 1 and not (first and v < 0):
                        values(pr * 2 + v // 2, pr * UH + v, v % UH)
                    if u % G == 3 and not (first and v < 0):
                        turned(pr * UH + v)
            pe.wait_ge(loads[0], 16 * ND)
            scores(0, 0)
            scores(1, 1)
            scores(2, 2)
            turn(0, True, False)
            with pe.Fori(1, NP - 1) as pr:
                turn(pr, False, False)
            turn(NP - 1, False, True)
            values(NP * 2 - 1, NP * UH - 1, UH - 1)
            turned(NP * UH - 1)


def project_out(nc, ph, X, ident, w, AO):
    wo = ph.sb("wo", [P, DC, D])
    AT = ph.sb("AT", [P, 2, DC, GT])
    ps_t = ph.ps("ps_t", [P, DC, GT])
    ps_o = ph.ps("ps_o", [P, 2, GT])
    weights = ph.dma_sem("weights")
    tr, at_ok, o_mm, o_add = ph.sem("tr"), ph.sem("at_ok"), ph.sem("o_mm"), ph.sem("o_add")
    HC = H // DC
    with nc.Block() as block:
        @block.sync
        def _(sp):
            ph.start(sp)
            sp.dma_start(wo[:, :, :], w.rearrange("(c p) n -> p c n", p=P)).then_inc(weights, 16)

        @block.scalar
        def _(act):
            for g in range(NG):
                act.wait_ge(o_mm, START + 2 * g - 2)
                for c in range(DC):
                    act.wait_ge(tr, START + g * DC + c + 1)
                    nc.scalar.copy(AT[:, g % 2, c, :], ps_t[:, c, :]).then_inc(at_ok, 1)

        @block.vector
        def _(dve):
            for g in range(NG):
                for k in range(G // 2):
                    dve.wait_ge(o_mm, START + 2 * g + k + 1)
                    x2 = X[:, g * G + 2 * k:g * G + 2 * k + 2, :]
                    nc.vector.tensor_tensor(x2, ps_o[:, k, :].rearrange("p (j d) -> p j d", j=2), x2,
                                            ALU.add).then_inc(o_add, 1)

        @block.tensor
        def _(pe):
            pe.wait_ge(weights, 16)

            def transposes(g):
                for c in range(DC):
                    pe.wait_ge(at_ok, START + (g - 1) * DC + c + 1)
                    for j in range(G):
                        tile = g * G + j
                        x = nc.tensor.transpose(ps_t[:, c, j * P:(j + 1) * P],
                                                AO[:, tile // TB, tile % TB, c * HC:(c + 1) * HC, :].rearrange(
                                                    "p h d -> p (h d)"), ident[:, :])
                    x.then_inc(tr, 1)
            transposes(0)
            for g in range(NG):
                if g < NG - 1:
                    transposes(g + 1)
                pe.wait_ge(at_ok, START + (g + 1) * DC)
                pe.wait_ge(o_add, START + 2 * g)
                for k in range(G // 2):
                    for j in (2 * k, 2 * k + 1):
                        for c in range(DC):
                            x = nc.tensor.matmul(ps_o[:, k, (j % 2) * D:(j % 2 + 1) * D],
                                                 AT[:, g % 2, c, j * P:(j + 1) * P], wo[:, c, :],
                                                 start=(c == 0), stop=(c == DC - 1))
                    x.then_inc(o_mm, 1)


STAGES = "AMBMCFDF"


def network(nc, a):
    ctx = ExitStack()
    with ctx:
        top = Phase(nc, ctx, "top")
        X = top.sb("X", [P, NT, D])
        ident = top.sb("ident", [P, P])
        loaded, stored = top.sem("loaded"), top.sem("stored")
        with nc.Block() as block:
            @block.sync
            def _(sp):
                sp.dma_start(X[:, :, :], a["L0_attn_a_x"].rearrange("b (j p) d -> p (b j) d", p=P)).then_inc(loaded, 16)
                sp.dma_start(ident[:, :], a["ident"]).then_inc(loaded, 16)
                sp.wait_ge(loaded, 32)
        for n, stage in enumerate(STAGES):
            with ExitStack() as own:
                ph = Phase(nc, own, f"s{n}{stage}")
                if stage == "A":
                    attention(nc, ph, X, ident, a, "decay")
                if stage == "M":
                    expert_ffn(nc, ph, X, ident, a)
                if stage == "B":
                    retention(nc, ph, X, ident, a)
                if stage == "C":
                    attention(nc, ph, X, ident, a, "window")
                if stage == "D":
                    gated_recurrence(nc, ph, X, ident, a)
                if stage == "F":
                    low_rank_ffn(nc, ph, X, ident, a["L1_ffn_U1"], a["L1_ffn_V1"], a["L1_ffn_b1"],
                                 a["L1_ffn_U2"], a["L1_ffn_V2"], a["L1_ffn_b2"], a["ones"])
        with nc.Block() as block:
            @block.sync
            def _(sp):
                sp.dma_start(a["out"].rearrange("b (j p) d -> p (b j) d", p=P), X[:, :, :]).then_inc(stored, 16)
                sp.wait_ge(stored, 16)


def shape_constants():
    f = np.float32
    distance = np.abs(np.arange(2 * T - P)[None, :] - (T - P) - np.arange(P)[:, None]).astype(f)
    decay = np.exp(f(-0.01) * distance) * f(D ** -0.5)
    inv_freq = (f(1.0) / f(10000.0) ** (np.arange(0, HD, 2, dtype=f) / f(HD))).astype(f)
    freqs = np.arange(T, dtype=f)[:, None] * inv_freq[None, :]
    emb = np.tile(np.concatenate([freqs, freqs], 1).T, (P // HD, 1)).astype(f)
    q, k = np.arange(P)[:, None], np.arange(2 * P)[None, :]
    seen = (k <= q + P) & ((q + P - k <= 128) | (k // 64 == (q + P) // 64))
    masks = np.zeros((P, 3, 2 * P + 4), f)
    masks[:, 0, 0:P] = np.where(k[:, 0:P] <= q, 0.0, -3e38)
    masks[:, 1, 0:2 * P] = np.where(seen | ((k < 4) & (k <= q + P)), 0.0, -3e38)
    masks[:, 2, 0:2 * P] = np.where(seen, 0.0, -3e38)
    return {"decay": decay, "cos": np.cos(emb), "sin": np.sin(emb), "masks": masks.reshape(P, -1), "ident": np.eye(P, dtype=np.float32), "ones": np.ones((P, T), np.float32),
            "gather": np.tile(np.eye(32, dtype=f)[:, 0:HD + 1], (4, 1)), "reverse": np.eye(P, dtype=f)[::-1].copy(),
            "batch_base": (np.arange(2)[:, None, None] * (T // 2) + np.arange(B)[None, :, None] * T
                           + np.zeros((1, 1, 8))).astype(f).reshape(-1, 1)}


def laid_out(inputs):
    arrays = {k: np.ascontiguousarray(v) for k, v in inputs.items()}
    for name in ("Wq", "Wv", "Wg", "Wo"):
        arrays[name + "T"] = np.ascontiguousarray(arrays.pop("L0_attn_b_" + name).T)
    arrays["qkv_wT"] = np.ascontiguousarray(arrays.pop("L1_attn_a_qkv_w").T)
    arrays["out_wT"] = np.ascontiguousarray(arrays.pop("L1_attn_a_out_w").T)
    arrays["WkT"] = np.ascontiguousarray(arrays.pop("L0_attn_a_W_k").T)
    arrays["WvT_a"] = np.ascontiguousarray(arrays.pop("L0_attn_a_W_v").T)
    arrays["beta_rows"] = np.repeat(arrays.pop("L0_attn_b_beta"), HD)
    return arrays


def kernel(**inputs):
    import concourse.bacc as bacc
    from concourse.bass_utils import run_bass_kernel_spmd

    nc = bacc.Bacc("TRN2", target_bir_lowering=False, num_devices=1)
    arrays = {**laid_out(inputs), **shape_constants()}
    a = {k: nc.dram_tensor(f"in_{k}", v.shape, mybir.dt.from_np(v.dtype), kind="ExternalInput").ap()
         for k, v in arrays.items()}
    a["out"] = nc.dram_tensor("out", (B, T, D), F32, kind="ExternalOutput").ap()
    network(nc, a)
    r = run_bass_kernel_spmd(nc, [{f"in_{k}": v for k, v in arrays.items()}], core_ids=[0])
    return r.results[0]["out"]
```

```python
import numpy as np
from contextlib import ExitStack

import concourse.bass as bass
from concourse import mybir

F32 = mybir.dt.float32
F32R = mybir.dt.float32r
BF16 = mybir.dt.bfloat16
U32 = mybir.dt.uint32
ALU = mybir.AluOpType
ACT = mybir.ActivationFunctionType
AXX = mybir.AxisListType.X
ds = bass.ds

P = 128
B, T, D = 4, 1024, 256
NT = B * T // P
TB = T // P
DC = D // P
G = 4
GT = G * P
NG = NT // G
H, HD = 16, 16
EPS = 1e-5
START = 4


class Phase:

    def __init__(self, nc, ctx, name):
        self.nc, self.ctx, self.name = nc, ctx, name
        self.sems, self.dma_sems, self.all_sems = [], [], []
        ctx.callback(self.finish)

    def sb(self, name, shape, dt=F32):
        return self.ctx.enter_context(self.nc.sbuf_tensor(f"{self.name}_{name}", shape, dt))

    def ps(self, name, shape, dt=F32):
        return self.ctx.enter_context(self.nc.psum_tensor(f"{self.name}_{name}", shape, dt))

    def sem(self, name):
        s = self.nc.alloc_semaphore(f"{self.name}_{name}")
        self.sems.append(s)
        self.all_sems.append(s)
        return s

    def dma_sem(self, name, start=0):
        s = self.nc.alloc_semaphore(f"{self.name}_{name}")
        self.all_sems.append(s)
        if start:
            self.dma_sems.append((s, start))
        return s

    def finish(self):
        if self.all_sems:
            self.nc.clear_and_free_semaphores(self.all_sems)
            self.nc.all_engine_barrier()

    def start(self, eng):
        for s in self.sems:
            eng.sem_inc(s, START)
        for s, n in self.dma_sems:
            eng.sem_inc(s, n)


class LayerNorm:

    def __init__(self, ph, X, ident, hT, ps_t, buffers=1):
        self.nc, self.X, self.ident, self.hT, self.ps_t, self.buffers = ph.nc, X, ident, hT, ps_t, buffers
        self.st = [ph.sb(f"ln_st{s}", [P, G, 6]) for s in range(buffers)]
        self.mv = [ph.sb(f"ln_mv{s}", [P, G, 2]) for s in range(buffers)]
        self.ve = [ph.sb(f"ln_ve{s}", [P, G]) for s in range(buffers)]
        self.mhalf = ph.sb("ln_mhalf", [P, G])
        self.eps = ph.sb("ln_eps", [P, G])
        self.rstd = ph.sb("ln_rstd", [P, G])
        self.h = [ph.sb(f"ln_h{s}", [P, G, D]) for s in range(buffers)]
        self.moments = ph.sem("ln_moments")
        self.veps = ph.sem("ln_veps")
        self.rs = ph.sem("ln_rs")
        self.hrow = ph.sem("ln_hrow")
        self.trans = ph.sem("ln_trans")
        self.hTok = ph.sem("ln_hT")

    def pool_setup(self):
        self.nc.gpsimd.memset(self.eps[:, :], EPS)
        self.nc.gpsimd.memset(self.mhalf[:, :], -0.5).then_inc(self.rs, 1)

    def vector(self, v, g):
        self.vector_moments(v, g)
        self.vector_rows(v, g)

    def vector_moments(self, v, g, s=0):
        for j in range(G):
            self.nc.vector.bn_stats(self.st[s][:, j, :], self.X[:, ds(g * G + j, 1), :])
        v.drain()
        for j in range(G):
            self.nc.vector.bn_aggr(self.mv[s][:, j, :], self.st[s][:, j, :]).then_inc(self.moments, 1)

    def vector_rows(self, v, g, s=0):
        v.wait_ge(self.rs, START + g + 2)
        v.wait_ge(self.trans, START + (g + 1 - self.buffers) * DC)
        for j in range(G):
            self.nc.vector.tensor_scalar(self.h[s][:, j, :], self.X[:, ds(g * G + j, 1), :],
                                         self.mv[s][:, j, 0:1], self.rstd[:, j:j + 1],
                                         ALU.subtract, ALU.mult).then_inc(self.hrow, 1)

    def pool(self, p, g, s=0):
        p.wait_ge(self.moments, START + (g + 1) * G)
        self.nc.gpsimd.tensor_tensor(self.ve[s][:, :], self.mv[s][:, :, 1], self.eps[:, :], ALU.add
                                     ).then_inc(self.veps, 1)
        p.wait_ge(self.veps, START + g + 1)
        p.wait_ge(self.hrow, START + g * G)
        self.nc.gpsimd.tensor_tensor(self.rstd[:, :], self.ve[s][:, :], self.mhalf[:, :], ALU.pow).then_inc(self.rs, 1)

    def tensor(self, t, g, s=0):
        t.wait_ge(self.hrow, START + (g + 1) * G)
        t.wait_ge(self.hTok, START + g * DC)
        for c in range(DC):
            for j in range(G):
                last = self.nc.tensor.transpose(self.ps_t[:, c, j * P:(j + 1) * P],
                                                self.h[s][:, j, c * P:(c + 1) * P], self.ident[:, :])
            last.then_inc(self.trans, 1)

    def scalar(self, s, g, slot=None):
        for c in range(DC):
            s.wait_ge(self.trans, START + g * DC + c + 1)
            to = self.hT[:, c, ds(g * GT, GT)] if slot is None else self.hT[:, slot, c, :]
            self.nc.scalar.copy(to, self.ps_t[:, c, :]).then_inc(self.hTok, 1)


def load_once(eng, sem, pairs):
    for dst, src in pairs:
        eng.dma_start(dst, src).then_inc(sem, 16)


def skewed_turns(eng, turn):
    with eng.Fori(0, B - 1) as b:
        for h in range(2):
            turn(b * 2 + h, h, True, True)
    turn(NG - 2, 0, True, False)
    turn(NG - 1, 1, False, False)


def low_rank_ffn(nc, ph, X, ident, U1, V1, b1, U2, V2, b2, out=None):
    R, FF = U1.shape[1], V1.shape[1]
    M = FF // P
    hT = ph.sb("hT", [P, 2, DC, GT])
    u1 = ph.sb("u1", [P, DC, R])
    v1 = ph.sb("v1", [P, FF])
    bias1 = ph.sb("bias1", [P, M])
    u2 = ph.sb("u2", [P, M, R])
    v2 = ph.sb("v2", [P, D])
    bias2 = ph.sb("bias2", [P, D])
    PT, QT = ph.sb("PT", [P, GT]), ph.sb("QT", [P, GT])
    HT = ph.sb("HT", [P, M, GT])
    ps_t = ph.ps("ps_t", [P, DC, GT])
    ps_p = ph.ps("ps_p", [P, GT])
    ps_h = ph.ps("ps_h", [P, 2, GT])
    ps_q = ph.ps("ps_q", [P, GT])
    ps_o = ph.ps("ps_o", [P, 2, GT])
    ln = LayerNorm(ph, X, ident, hT, ps_t)
    weights, stored = ph.dma_sem("weights"), ph.dma_sem("stored")
    p_mm, p_sb = ph.sem("p_mm"), ph.sem("p_sb")
    h_mm, h_sb = ph.sem("h_mm"), ph.sem("h_sb")
    q_mm, q_sb = ph.sem("q_mm"), ph.sem("q_sb")
    b_add, passed = ph.sem("b_add"), ph.sem("passed")
    o_mm, o_add = ph.sem("o_mm"), ph.sem("o_add")
    pairs = [(u1[:, :, :], U1.rearrange("(c p) r -> p c r", p=P)), (v1[0:R, :], V1), (v1[R:P, :], V1),
             (bias1[:, :], b1.rearrange("(m p) -> p m", p=P)),
             (u2[:, :, :], U2.rearrange("(m p) r -> p m r", p=P)), (v2[0:R, :], V2), (v2[R:P, :], V2),
             (bias2[:, :], b2.rearrange("(a d) -> a d", a=1).to_broadcast([P, D]))]
    loaded = 16 * len(pairs)

    with nc.Block() as block:
        @block.sync
        def _(sp):
            ph.start(sp)
            with nc.allow_non_contiguous_dma(reason="a bias laid out over partitions"):
                load_once(sp, weights, pairs)
            sp.wait_ge(weights, loaded)
            if out is not None:
                for g in range(NG):
                    sp.wait_ge(o_add, START + (g + 1) * (G // 2))
                    sp.dma_start(out.rearrange("b (j p) d -> p (b j) d", p=P)[:, g * G:(g + 1) * G, :],
                                 X[:, g * G:(g + 1) * G, :]).then_inc(stored, 16)
                sp.wait_ge(stored, 16 * NG)

        @block.gpsimd
        def _(pool):
            ln.pool_setup()
            pool.wait_ge(ln.rs, START + 1)
            ln.pool(pool, 0)
            ln.pool(pool, 1)
            pool.wait_ge(weights, loaded)

            def turn(g, h, following, more):
                if more:
                    ln.pool(pool, g + 2)
                x4 = X[:, ds(g * G, G), :]
                pool.wait_ge(ln.hrow, START + (g + 1) * G)
                pool.sem_inc(passed, 1)
                nc.gpsimd.tensor_tensor(x4, x4, bias2[:, :].unsqueeze(1).to_broadcast([P, G, D]),
                                        ALU.add).then_inc(b_add, 1)
            skewed_turns(pool, turn)

        @block.vector
        def _(dve):
            ln.vector(dve, 0)
            ln.vector(dve, 1)

            def turn(g, h, following, more):
                if more:
                    ln.vector(dve, g + 2)
                dve.wait_ge(b_add, START + g + 1)
                for k in range(G // 2):
                    dve.wait_ge(o_mm, START + g * (G // 2) + k + 1)
                    x2 = X[:, ds(g * G + 2 * k, 2), :]
                    nc.vector.tensor_tensor(x2, ps_o[:, k, :].rearrange("p (j d) -> p j d", j=2), x2,
                                            ALU.add).then_inc(o_add, 1)
            skewed_turns(dve, turn)

        @block.scalar
        def _(act):
            act.wait_ge(weights, loaded)

            def first(g):
                act.wait_ge(p_mm, START + g + 1)
                nc.scalar.copy(PT[:, :], ps_p[:, :]).then_inc(p_sb, 1)

            def turn(g, h, following, more):
                act.wait_ge(q_mm, START + g)
                for m in range(M):
                    act.wait_ge(h_mm, START + g * M + m + 1)
                    nc.scalar.activation(HT[:, m, :], ps_h[:, m % 2, :], ACT.Gelu_apprx_tanh,
                                         bias=bias1[:, m:m + 1]).then_inc(h_sb, 1)
                act.wait_ge(q_mm, START + g + 1)
                act.wait_ge(o_mm, START + g * (G // 2))
                nc.scalar.copy(QT[:, :], ps_q[:, :]).then_inc(q_sb, 1)
                if following:
                    first(g + 1)
                if more:
                    ln.scalar(act, g + 2, h)
            ln.scalar(act, 0, 0)
            ln.scalar(act, 1, 1)
            first(0)
            skewed_turns(act, turn)

        @block.tensor
        def _(pe):
            pe.wait_ge(weights, loaded)

            def first(g, h):
                pe.wait_ge(ln.hTok, START + (g + 1) * DC)
                pe.wait_ge(p_sb, START + g)
                for c in range(DC):
                    i = nc.tensor.matmul(ps_p[c * R:(c + 1) * R, :], u1[:, c, :], hT[:, h, c, :],
                                         start=True, stop=True, tile_position=(0, c * R))
                i.then_inc(p_mm, 1)

            def hidden(g, m):
                pe.wait_ge(h_sb, START + g * M + m - 1)
                nc.tensor.matmul(ps_h[:, m % 2, :], v1[:, m * P:(m + 1) * P], PT[:, :],
                                 start=True, stop=True).then_inc(h_mm, 1)

            def down(g, m):
                pe.wait_ge(h_sb, START + g * M + m + 2)
                for j in range(2):
                    i = nc.tensor.matmul(ps_q[j * R:(j + 1) * R, :], u2[:, m + j, :], HT[:, m + j, :],
                                         start=(m == 0), stop=(m == M - 2), tile_position=(0, j * R))
                if m == M - 2:
                    i.then_inc(q_mm, 1)

            def turn(g, h, following, more):
                pe.wait_ge(p_sb, START + g + 1)
                pe.wait_ge(q_sb, START + g)
                for m in range(M):
                    hidden(g, m)
                    if m >= 3 and m % 2:
                        down(g, m - 3)
                if more:
                    ln.tensor(pe, g + 2)
                down(g, M - 2)
                if following:
                    first(g + 1, 1 - h)
                pe.wait_ge(q_sb, START + g + 1)
                pe.wait_ge(o_add, START + g * (G // 2))
                for k in range(G // 2):
                    for j in (2 * k, 2 * k + 1):
                        i = nc.tensor.matmul(ps_o[:, k, (j % 2) * D:(j % 2 + 1) * D], QT[:, j * P:(j + 1) * P],
                                             v2[:, :], start=True, stop=True)
                    i.then_inc(o_mm, 1)
            ln.tensor(pe, 0)
            ln.tensor(pe, 1)
            first(0, 0)
            skewed_turns(pe, turn)


def retention(nc, ph, X, ident, a):
    hT = ph.sb("hT", [P, DC, B * T])
    wq, wv, wg, wo = (ph.sb(n, [P, DC, D]) for n in ("wq", "wv", "wg", "wo"))
    mean_w = ph.sb("mean_w", [P, P])
    beta_in, lam = ph.sb("beta_in", [P, DC]), ph.sb("lam", [P, DC])
    gamma, shift = ph.sb("gamma", [P, DC]), ph.sb("shift", [P, DC])
    eps = ph.sb("eps", [P, 1])
    S = ph.sb("S", [P, DC, GT])
    carry = ph.sb("carry", [P, DC])
    Y, DM, SQ = (ph.sb(n, [P, DC, GT]) for n in ("Y", "DM", "SQ"))
    gate = [ph.sb(f"gate{i}", [P, DC, GT]) for i in range(2)]
    Z = ph.sb("Z", [P, DC, GT])
    sd, rstd = ph.sb("sd", [P, GT]), ph.sb("rstd", [P, GT])
    ps_t = ph.ps("ps_t", [P, DC, GT])
    ps_v = ph.ps("ps_v", [P, DC, GT])
    ps_q = ph.ps("ps_q", [P, DC, GT])
    ps_m, ps_r = ph.ps("ps_m", [P, GT]), ph.ps("ps_r", [P, GT])
    ln = LayerNorm(ph, X, ident, hT, ps_t)
    weights = ph.dma_sem("weights")
    consts = ph.sem("consts")
    v_mm, scan = ph.sem("v_mm"), ph.sem("scan")
    q_mm, y_ok = ph.sem("q_mm"), ph.sem("y_ok")
    g_mm, gate_ok = ph.sem("g_mm"), ph.sem("gate_ok")
    m_mm, d_ok = ph.sem("m_mm"), ph.sem("d_ok")
    sq_ok, r_mm = ph.sem("sq_ok"), ph.sem("r_mm")
    sd_ok, z_ok = ph.sem("sd_ok"), ph.sem("z_ok")
    o_mm, o_add = ph.sem("o_mm"), ph.sem("o_add")
    part = lambda w: w.rearrange("(c p) n -> p c n", p=P)
    col = lambda w: w.rearrange("(c p) -> p c", p=P)
    pairs = [(wv[:, :, :], part(a["WvT"])), (wq[:, :, :], part(a["WqT"])), (wg[:, :, :], part(a["WgT"])),
             (wo[:, :, :], part(a["WoT"])), (beta_in[:, :], col(a["beta_rows"])),
             (gamma[:, :], col(a["L0_attn_b_ln_gamma"])), (shift[:, :], col(a["L0_attn_b_ln_beta"]))]
    loaded = 16 * len(pairs)

    with nc.Block() as block:
        @block.sync
        def _(sp):
            ph.start(sp)
            with nc.allow_non_contiguous_dma(reason="vectors laid out over partitions"):
                load_once(sp, weights, pairs)
            sp.wait_ge(weights, loaded)

        @block.gpsimd
        def _(pool):
            ln.pool_setup()
            pool.wait_ge(ln.rs, START + 1)
            with pool.Fori(0, NG) as g:
                ln.pool(pool, g)

        @block.vector
        def _(dve):
            nc.vector.memset(eps[:, :], EPS)
            nc.vector.memset(mean_w[:, :], 1.0 / D).then_inc(consts, 1)
            ln.vector(dve, 0)
            ln.vector(dve, 1)
            dve.wait_ge(consts, START + 2)

            def states(g, h):
                for c in range(DC):
                    dve.wait_ge(v_mm, START + g * DC + c + 1)
                    nc.vector.tensor_tensor_scan(S[:, c, :], lam[:, c:c + 1].to_broadcast([P, GT]), ps_v[:, c, :],
                                                 0.0 if h == 0 else carry[:, c:c + 1],
                                                 ALU.mult, ALU.add).then_inc(scan, 1)

            def with_q(g):
                for c in range(DC):
                    dve.wait_ge(q_mm, START + g * DC + c + 1)
                    dve.wait_ge(scan, START + g * DC + c + 1)
                    nc.vector.tensor_tensor(Y[:, c, :], ps_q[:, c, :], S[:, c, :], ALU.mult).then_inc(y_ok, 1)
                nc.vector.tensor_copy(carry[:, :], S[:, :, GT - 1])

            def turn(g, h, following, more):
                dve.wait_ge(m_mm, START + g + 1)
                for c in range(DC):
                    nc.vector.tensor_tensor(DM[:, c, :], Y[:, c, :], ps_m[:, :], ALU.subtract).then_inc(d_ok, 1)
                if more:
                    ln.vector_moments(dve, g + 2)
                if following:
                    states(g + 1, 1 - h)
                dve.wait_ge(sd_ok, START + g + 1)
                nc.vector.reciprocal(rstd[:, :], sd[:, :])
                dve.drain()
                for c in range(DC):
                    nc.vector.scalar_tensor_tensor(Z[:, c, :], DM[:, c, :], gamma[:, c:c + 1], rstd[:, :],
                                                   ALU.mult, ALU.mult)
                if following:
                    with_q(g + 1)
                dve.drain()
                dve.wait_ge(gate_ok, START + (g + 1) * DC)
                for c in range(DC):
                    nc.vector.scalar_tensor_tensor(Z[:, c, :], Z[:, c, :], shift[:, c:c + 1], gate[h][:, c, :],
                                                   ALU.add, ALU.mult).then_inc(z_ok, 1)
                if more:
                    ln.vector_rows(dve, g + 2)
                for k in range(G // 2):
                    dve.wait_ge(o_mm, START + g * (G // 2) + k + 1)
                    x2 = X[:, ds(g * G + 2 * k, 2), :]
                    nc.vector.tensor_tensor(x2, ps_q[:, k, :].rearrange("p (j d) -> p j d", j=2), x2,
                                            ALU.add).then_inc(o_add, 1)
            states(0, 0)
            with_q(0)
            dve.drain()
            skewed_turns(dve, turn)

        @block.scalar
        def _(act):
            act.wait_ge(weights, loaded)
            act.wait_ge(consts, START + 1)
            nc.scalar.activation(lam[:, :], beta_in[:, :], ACT.Sigmoid).then_inc(consts, 1)
            ln.scalar(act, 0)

            ln.scalar(act, 1)

            def gate_of(g, h):
                act.wait_ge(z_ok, START + (g - 1) * DC)
                for c in range(DC):
                    act.wait_ge(g_mm, START + g * DC + c + 1)
                    nc.scalar.activation(gate[h][:, c, :], ps_v[:, c, :], ACT.Silu).then_inc(gate_ok, 1)
            gate_of(0, 0)

            def turn(g, h, following, more):
                act.wait_ge(r_mm, START + g)
                for c in range(DC):
                    act.wait_ge(d_ok, START + g * DC + c + 1)
                    nc.scalar.activation(SQ[:, c, :], DM[:, c, :], ACT.Square).then_inc(sq_ok, 1)
                act.wait_ge(r_mm, START + g + 1)
                act.wait_ge(z_ok, START + g * DC)
                nc.scalar.activation(sd[:, :], ps_r[:, :], ACT.Sqrt, bias=eps[:, 0:1]).then_inc(sd_ok, 1)
                if following:
                    gate_of(g + 1, 1 - h)
                if more:
                    ln.scalar(act, g + 2)
            skewed_turns(act, turn)

        @block.tensor
        def _(pe):
            pe.wait_ge(weights, loaded)
            pe.wait_ge(consts, START + 1)

            def project(out, w, g, done):
                for c in range(DC):
                    for k in range(DC):
                        i = nc.tensor.matmul(out[:, c, :], w[:, k, c * P:(c + 1) * P], hT[:, k, ds(g * GT, GT)],
                                             start=(k == 0), stop=(k == DC - 1))
                    i.then_inc(done, 1)

            def mean(out, src, done):
                for c in range(DC):
                    i = nc.tensor.matmul(out[:, :], mean_w[:, :], src[:, c, :], start=(c == 0), stop=(c == DC - 1))
                i.then_inc(done, 1)

            def values(g):
                pe.wait_ge(ln.hTok, START + (g + 1) * DC)
                pe.wait_ge(gate_ok, START + g * DC)
                project(ps_v, wv, g, v_mm)

            def queries(g):
                pe.wait_ge(o_add, START + (g - 1) * (G // 2))
                project(ps_q, wq, g, q_mm)

            def gates(g):
                pe.wait_ge(scan, START + (g + 1) * DC)
                project(ps_v, wg, g, g_mm)

            def turn(g, h, following, more):
                pe.wait_ge(d_ok, START + g * DC)
                pe.wait_ge(y_ok, START + (g + 1) * DC)
                mean(ps_m, Y, m_mm)
                if following:
                    values(g + 1)
                pe.wait_ge(sd_ok, START + g)
                pe.wait_ge(sq_ok, START + (g + 1) * DC)
                mean(ps_r, SQ, r_mm)
                if following:
                    queries(g + 1)
                    gates(g + 1)
                if more:
                    ln.tensor(pe, g + 2)
                if following:
                    pe.wait_ge(y_ok, START + (g + 2) * DC)
                pe.wait_ge(z_ok, START + (g + 1) * DC)
                for k in range(G // 2):
                    for j in (2 * k, 2 * k + 1):
                        for c in range(DC):
                            i = nc.tensor.matmul(ps_q[:, k, (j % 2) * D:(j % 2 + 1) * D],
                                                 Z[:, c, j * P:(j + 1) * P], wo[:, c, :],
                                                 start=(c == 0), stop=(c == DC - 1))
                    i.then_inc(o_mm, 1)
            ln.tensor(pe, 0)
            ln.tensor(pe, 1)
            values(0)
            queries(0)
            gates(0)
            skewed_turns(pe, turn)


def gated_recurrence(nc, ph, X, ident, a):
    K = 4
    hT = ph.sb("hT", [P, DC, B * T])
    wi, wf, wg, wo = (ph.sb(n, [P, DC, D]) for n in ("wi", "wf", "wg", "wo"))
    conv_i, conv_f = ph.sb("conv_i", [P, DC, K]), ph.sb("conv_f", [P, DC, K])
    gnorm = ph.sb("gnorm", [P, DC])
    mean_w = ph.sb("mean_w", [P, 1])
    eps = ph.sb("eps", [P, 1])
    RAW = ph.sb("RAW", [P, 2, DC, K - 1 + GT])
    CV = ph.sb("CV", [P, 2, DC, GT])
    FG, OM = ph.sb("FG", [P, DC, GT]), ph.sb("OM", [P, DC, GT])
    SI = ph.sb("SI", [P, DC, GT])
    O = ph.sb("O", [P, DC, GT])
    carry = ph.sb("carry", [P, DC])
    SQ, Z = ph.sb("SQ", [P, DC, GT]), ph.sb("Z", [P, DC, GT])
    gate = [ph.sb(f"gate{i}", [P, DC, GT]) for i in range(2)]
    ms, rms = ph.sb("ms", [P, G]), ph.sb("rms", [P, G])
    ps_t = ph.ps("ps_t", [P, DC, GT])
    ps_i = ph.ps("ps_i", [P, DC, GT])
    ps_f = ph.ps("ps_f", [P, DC, GT])
    ps_r = ph.ps("ps_r", [P, GT])
    ln = LayerNorm(ph, X, ident, hT, ps_t)
    weights = ph.dma_sem("weights")
    consts = ph.sem("consts")
    raw_mm, raw_ok = ph.sem("raw_mm"), ph.sem("raw_ok")
    conv_ok, act_ok = ph.sem("conv_ok"), ph.sem("act_ok")
    i_ok, o_ok = ph.sem("i_ok"), ph.sem("o_ok")
    g_mm, gate_ok = ph.sem("g_mm"), ph.sem("gate_ok")
    sq_ok, r_mm = ph.sem("sq_ok"), ph.sem("r_mm")
    ms_ok, rms_ok = ph.sem("ms_ok"), ph.sem("rms_ok")
    z_ok, o_mm, o_add = ph.sem("z_ok"), ph.sem("o_mm"), ph.sem("o_add")
    part = lambda w: w.rearrange("(c p) n -> p c n", p=P)
    pairs = [(wi[:, :, :], part(a["L1_attn_b_Wi"])), (wf[:, :, :], part(a["L1_attn_b_Wf"])),
             (wg[:, :, :], part(a["L1_attn_b_Wg"])), (wo[:, :, :], part(a["L1_attn_b_Wo"])),
             (conv_i[:, :, :], part(a["L1_attn_b_conv_i"])), (conv_f[:, :, :], part(a["L1_attn_b_conv_f"])),
             (gnorm[:, :], a["L1_attn_b_g_norm_weight"].rearrange("(c p) -> p c", p=P))]
    loaded = 16 * len(pairs)
    passed = ph.sem("passed")

    with nc.Block() as block:
        @block.sync
        def _(sp):
            ph.start(sp)
            with nc.allow_non_contiguous_dma(reason="vectors laid out over partitions"):
                load_once(sp, weights, pairs)
            sp.wait_ge(weights, loaded)

        @block.gpsimd
        def _(pool):
            ln.pool_setup()
            pool.wait_ge(ln.rs, START + 1)
            ln.pool(pool, 0)
            ln.pool(pool, 1)

            def turn(g, more):
                if more:
                    ln.pool(pool, g + 2)
                pool.wait_ge(o_add, START + g * G)
                pool.wait_ge(ms_ok, START + g + 1)
                pool.sem_inc(passed, 1)
                nc.gpsimd.tensor_tensor(rms[:, :], ms[:, :], ln.mhalf[:, :], ALU.pow).then_inc(rms_ok, 1)
            with pool.Fori(0, NG - 2) as g:
                turn(g, True)
            for g in (NG - 2, NG - 1):
                turn(g, False)

        @block.vector
        def _(dve):
            nc.vector.memset(eps[:, :], EPS)
            nc.vector.memset(mean_w[:, :], 1.0 / D).then_inc(consts, 1)
            ln.vector(dve, 0)
            ln.vector(dve, 1)
            dve.wait_ge(weights, loaded)

            def convolve(g):
                for n, (s, w) in enumerate(((1, conv_f), (0, conv_i))):
                    for c in range(DC):
                        dve.wait_ge(raw_ok, START + g * 2 * DC + n * DC + c + 1)
                        nc.vector.tensor_scalar(CV[:, s, c, :], RAW[:, s, c, 0:GT], w[:, c, 0:1], None, ALU.mult)
                    for k in range(1, K):
                        dve.drain()
                        for c in range(DC):
                            i = nc.vector.scalar_tensor_tensor(CV[:, s, c, :], RAW[:, s, c, k:k + GT],
                                                               w[:, c, k:k + 1], CV[:, s, c, :], ALU.mult, ALU.add)
                            if k == K - 1:
                                i.then_inc(conv_ok, 1)

            def turn(g, h, following, more):
                dve.wait_ge(act_ok, START + (g + 1) * 3 * DC)
                for c in range(DC):
                    nc.vector.tensor_tensor(SI[:, c, :], SI[:, c, :], OM[:, c, :], ALU.mult).then_inc(i_ok, 1)
                for c in range(DC):
                    dve.wait_ge(i_ok, START + g * DC + c + 1)
                    nc.vector.tensor_tensor_scan(O[:, c, :], FG[:, c, :], SI[:, c, :],
                                                 0.0 if h == 0 else carry[:, c:c + 1],
                                                 ALU.mult, ALU.add).then_inc(o_ok, 1)
                dve.drain()
                nc.vector.tensor_copy(carry[:, :], O[:, :, GT - 1])
                dve.wait_ge(gate_ok, START + (g + 1) * DC)
                for c in range(DC):
                    nc.vector.scalar_tensor_tensor(Z[:, c, :], O[:, c, :], gnorm[:, c:c + 1], gate[h][:, c, :],
                                                   ALU.mult, ALU.mult).then_inc(z_ok, 1)
                if more:
                    ln.vector(dve, g + 2)
                if following:
                    convolve(g + 1)
                dve.wait_ge(rms_ok, START + g + 1)
                for j in range(G):
                    if j % 2 == 0:
                        dve.wait_ge(o_mm, START + g * (G // 2) + j // 2 + 1)
                    x1 = X[:, ds(g * G + j, 1), :].rearrange("p a d -> p (a d)")
                    nc.vector.scalar_tensor_tensor(x1, ps_f[:, j // 2, (j % 2) * D:(j % 2 + 1) * D], rms[:, j:j + 1],
                                                   x1, ALU.mult, ALU.add).then_inc(o_add, 1)
            convolve(0)
            skewed_turns(dve, turn)

        @block.scalar
        def _(act):
            act.wait_ge(weights, loaded)
            act.wait_ge(consts, START + 1)
            ln.scalar(act, 0)

            def raw(g, h):
                act.wait_ge(conv_ok, START + g * 2 * DC)
                for s, ps in ((0, ps_i), (1, ps_f)):
                    for c in range(DC):
                        if h == 0:
                            nc.scalar.memzero(RAW[:, s, c, 0:K - 1])
                        else:
                            nc.scalar.copy(RAW[:, s, c, 0:K - 1], RAW[:, s, c, GT:GT + K - 1])
                act.drain()
                for n, (s, ps) in enumerate(((1, ps_f), (0, ps_i))):
                    for c in range(DC):
                        act.wait_ge(raw_mm, START + g * 2 * DC + n * DC + c + 1)
                        nc.scalar.copy(RAW[:, s, c, K - 1:], ps[:, c, :]).then_inc(raw_ok, 1)

            def gate_of(g, h):
                act.wait_ge(z_ok, START + (g - 1) * DC)
                for c in range(DC):
                    act.wait_ge(g_mm, START + g * DC + c + 1)
                    nc.scalar.activation(gate[h][:, c, :], ps_i[:, c, :], ACT.Silu).then_inc(gate_ok, 1)

            def gates(g):
                act.wait_ge(conv_ok, START + g * 2 * DC + DC)
                for c in range(DC):
                    nc.scalar.activation(FG[:, c, :], CV[:, 1, c, :], ACT.Sigmoid).then_inc(act_ok, 1)
                act.wait_ge(act_ok, START + g * 3 * DC + DC)
                for c in range(DC):
                    nc.scalar.activation(OM[:, c, :], FG[:, c, :], ACT.Copy, bias=1.0, scale=-1.0).then_inc(act_ok, 1)
                act.wait_ge(conv_ok, START + (g + 1) * 2 * DC)
                for c in range(DC):
                    nc.scalar.activation(SI[:, c, :], CV[:, 0, c, :], ACT.Silu).then_inc(act_ok, 1)

            def turn(g, h, following, more):
                for c in range(DC):
                    act.wait_ge(o_ok, START + g * DC + c + 1)
                    nc.scalar.activation(SQ[:, c, :], O[:, c, :], ACT.Square).then_inc(sq_ok, 1)
                if following:
                    raw(g + 1, 1 - h)
                act.wait_ge(r_mm, START + g + 1)
                act.wait_ge(rms_ok, START + g)
                nc.scalar.activation(ms[:, :], ps_r[:, 0:G], ACT.Identity, bias=eps[:, 0:1]).then_inc(ms_ok, 1)
                if following:
                    gate_of(g + 1, 1 - h)
                if more:
                    ln.scalar(act, g + 2)
                if following:
                    gates(g + 1)
            ln.scalar(act, 1)
            raw(0, 0)
            gate_of(0, 0)
            gates(0)
            skewed_turns(act, turn)

        @block.tensor
        def _(pe):
            pe.wait_ge(weights, loaded)
            pe.wait_ge(consts, START + 1)

            def project(out, w, g, done):
                for c in range(DC):
                    for k in range(DC):
                        i = nc.tensor.matmul(out[:, c, :], w[:, k, c * P:(c + 1) * P], hT[:, k, ds(g * GT, GT)],
                                             start=(k == 0), stop=(k == DC - 1))
                    i.then_inc(done, 1)

            def inputs(g):
                pe.wait_ge(ln.hTok, START + (g + 1) * DC)
                pe.wait_ge(o_add, START + (g - 1) * G)
                project(ps_f, wf, g, raw_mm)
                pe.wait_ge(gate_ok, START + g * DC)
                project(ps_i, wi, g, raw_mm)

            def gates(g):
                pe.wait_ge(raw_ok, START + (g + 1) * 2 * DC)
                project(ps_i, wg, g, g_mm)

            def turn(g, h, following, more):
                if following:
                    inputs(g + 1)
                pe.wait_ge(ms_ok, START + g)
                pe.wait_ge(sq_ok, START + (g + 1) * DC)
                for j in range(G):
                    for c in range(DC):
                        i = nc.tensor.matmul(ps_r[:, j:j + 1], SQ[:, c, j * P:(j + 1) * P], mean_w[:, :],
                                             start=(c == 0), stop=(c == DC - 1))
                i.then_inc(r_mm, 1)
                if following:
                    gates(g + 1)
                if more:
                    ln.tensor(pe, g + 2)
                pe.wait_ge(z_ok, START + (g + 1) * DC)
                for k in range(G // 2):
                    for j in (2 * k, 2 * k + 1):
                        for c in range(DC):
                            i = nc.tensor.matmul(ps_f[:, k, (j % 2) * D:(j % 2 + 1) * D],
                                                 Z[:, c, j * P:(j + 1) * P], wo[:, c, :],
                                                 start=(c == 0), stop=(c == DC - 1))
                    i.then_inc(o_mm, 1)
            ln.tensor(pe, 0)
            ln.tensor(pe, 1)
            inputs(0)
            gates(0)
            skewed_turns(pe, turn)


def expert_ffn(nc, ph, X, ident, a):
    E, FF = a["L0_ffn_w1"].shape[0], a["L0_ffn_w1"].shape[2]
    KT = 2 * T // E
    C = KT // P
    R = B * E
    M = FF // P
    h_rows = nc.dram_tensor(f"{ph.name}_h_rows", (B * T, D), F32, kind="Internal").ap()
    acc = nc.dram_tensor(f"{ph.name}_acc", (B * T, D), F32, kind="Internal").ap()
    idxT = ph.sb("idxT", [P, C, R], U32)
    gT = ph.sb("gT", [P, C, R])
    raw = Raw(ph, a, M)
    with ExitStack() as own:
        route(nc, Phase(nc, own, ph.name + "r"), X, ident, a, E, R, C, KT, h_rows, acc, idxT, gT, raw)
    with ExitStack() as own:
        experts(nc, Phase(nc, own, ph.name + "e"), ident, E, C, M, h_rows, acc, idxT, gT, raw)
    with ExitStack() as own:
        add_rounded(nc, Phase(nc, own, ph.name + "a"), X, acc, raw)


class Raw:

    def __init__(self, ph, a, M):
        self.w1 = ph.sb("raw_w1", [P, DC, M * P])
        self.w2 = ph.sb("raw_w2", [P, M, D])
        self.w1_in, self.w2_in = ph.dma_sem("raw_w1_in"), ph.dma_sem("raw_w2_in")
        self.sums_in = ph.dma_sem("raw_sums_in")
        self.a = a

    @staticmethod
    def as_rows(t):
        return t[:, :, :].rearrange("p a n -> p (a n)").rearrange("p (j d) -> p j d", d=D)

    def load_w1(self, sp, e):
        sp.dma_start(self.w1[:, :, :], self.a["L0_ffn_w1"][ds(e, 1), :, :].rearrange(
            "a (c p) f -> p (a c) f", p=P)).then_inc(self.w1_in, 16)

    def load_w2(self, sp, e):
        sp.dma_start(self.w2[:, :, :], self.a["L0_ffn_w2"][ds(e, 1), :, :].rearrange(
            "a (m p) d -> p (a m) d", p=P)).then_inc(self.w2_in, 16)


def route(nc, ph, X, ident, a, E, R, C, KT, h_rows, acc, idxT, gT, raw):
    TH = T // 2
    hT = ph.sb("hT", [P, DC, B * T])
    gate_w = ph.sb("gate_w", [P, DC, E])
    base = ph.sb("base", [2 * R, 1])
    reverse = ph.sb("reverse", [P, P])
    zeros = ph.sb("zeros", [P, G, D])
    scT = ph.sb("scT", [E, B * T])
    sc, ex, pr = (ph.sb(n, [P, TB, B, E]) for n in ("sc", "ex", "pr"))
    mx, sm, rc = (ph.sb(n, [P, TB, B]) for n in ("mx", "sm", "rc"))
    PR = [ph.sb(f"PR{i}", [2 * R, TH]) for i in range(2)]
    vals, idx = ph.sb("vals", [2 * R, KT]), ph.sb("idx", [2 * R, KT], U32)
    rowf = ph.sb("rowf", [2 * R, KT])
    both = ph.sb("both", [P, 2, C, 2 * R])
    first, step = ph.sb("first", [P, C, R]), ph.sb("step", [P, C, R])
    ps_t = ph.ps("ps_t", [P, DC, GT])
    ps_s = ph.ps("ps_s", [P, GT])
    ps_x = ph.ps("ps_x", [P, TB, B, E])
    ps_p = ph.ps("ps_p", [P, TH])
    ps_i = ph.ps("ps_i", [P, 2, C, 2 * R])
    ps_r = ph.ps("ps_r", [P, 2, C, R])
    ln = LayerNorm(ph, X, ident, hT, ps_t, buffers=2)
    weights, zeroed = ph.dma_sem("weights"), ph.dma_sem("zeroed")
    rows_out = [ph.dma_sem(f"rows_out{s}") for s in range(2)]
    zeros_ok = ph.sem("zeros_ok")
    s_mm, s_sb = ph.sem("s_mm"), ph.sem("s_sb")
    x_tr, x_ok, e_ok, p_ok = ph.sem("x_tr"), ph.sem("x_ok"), ph.sem("e_ok"), ph.sem("p_ok")
    p_tr, p_sb, top_ok = ph.sem("p_tr"), ph.sem("p_sb"), ph.sem("top_ok")
    eight_ok, struck = ph.sem("eight_ok"), ph.sem("struck")
    i_tr, i_ok, r_mm = ph.sem("i_tr"), ph.sem("i_ok"), ph.sem("r_mm")

    with nc.Block() as block:
        @block.sync
        def _(sp):
            ph.start(sp)
            sp.dma_start(gate_w[:, :, :], a["L0_ffn_gate_w"].rearrange("(c p) e -> p c e", p=P)).then_inc(weights, 16)
            sp.dma_start(base[:, :], a["batch_base"]).then_inc(weights, 16)
            sp.dma_start(reverse[:, :], a["reverse"]).then_inc(weights, 16)
            with sp.Fori(0, NG // 2) as p:
                for s in range(2):
                    sp.wait_ge(ln.hrow, START + (p * 2 + s + 1) * G)
                    sp.dma_start(h_rows[ds((p * 2 + s) * GT, GT), :].rearrange("(j p) d -> p j d", p=P),
                                 ln.h[s][:, :, :]).then_inc(rows_out[s], 16)
            sp.wait_ge(zeros_ok, START + 1)
            for g in range(NG):
                sp.dma_start(acc[g * GT:(g + 1) * GT, :].rearrange("(j p) d -> p j d", p=P),
                             zeros[:, :, :]).then_inc(zeroed, 16)
            raw.load_w1(sp, 0)
            raw.load_w2(sp, 0)
            for s in range(2):
                sp.wait_ge(rows_out[s], 16 * (NG // 2))
            sp.wait_ge(zeroed, 16 * NG)

        @block.gpsimd
        def _(pool):
            ln.pool_setup()
            pool.wait_ge(ln.rs, START + 1)
            with pool.Fori(0, NG // 2) as p:
                for s in range(2):
                    ln.pool(pool, p * 2 + s, s)

        @block.vector
        def _(dve):
            nc.vector.memset(zeros[:, :, :], 0.0).then_inc(zeros_ok, 1)
            ln.vector_moments(dve, 0)
            for s in range(2):
                ln.vector_moments(dve, s + 1, 1 - s)
                ln.vector_rows(dve, s, s)
            with dve.Fori(1, NG // 2 - 1) as p:
                for s in range(2):
                    ln.vector_moments(dve, p * 2 + s + 1, 1 - s)
                    dve.wait_ge(rows_out[s], 16 * p)
                    ln.vector_rows(dve, p * 2 + s, s)
            ln.vector_moments(dve, NG - 1, 1)
            for s in range(2):
                dve.wait_ge(rows_out[s], 16 * (NG // 2 - 1))
                ln.vector_rows(dve, NG - 2 + s, s)
            wide = lambda m: m[:, :, :].rearrange("p j b -> p (j b)").unsqueeze(2).to_broadcast([P, TB * B, E])
            flat = lambda m: m[:, :, :, :].rearrange("p j b e -> p (j b) e")
            dve.wait_ge(x_tr, START + 1)
            nc.vector.tensor_copy(flat(sc), flat(ps_x))
            dve.drain()
            nc.vector.tensor_reduce(mx[:, :, :].rearrange("p j b -> p (j b)"), flat(sc), AXX, ALU.max)
            dve.drain()
            nc.vector.tensor_tensor(flat(sc), flat(sc), wide(mx), ALU.subtract).then_inc(x_ok, 1)
            dve.wait_ge(e_ok, START + 1)
            nc.vector.tensor_reduce(sm[:, :, :].rearrange("p j b -> p (j b)"), flat(ex), AXX, ALU.add)
            dve.drain()
            nc.vector.reciprocal(rc[:, :, :], sm[:, :, :])
            dve.drain()
            nc.vector.tensor_tensor(flat(pr), flat(ex), wide(rc), ALU.mult).then_inc(p_ok, 1)
            dve.wait_ge(p_sb, START + 1)
            dve.wait_ge(weights, 48)
            for r in range(KT // 8):
                now, after, eight = PR[r % 2], PR[(r + 1) % 2], slice(8 * r, 8 * r + 8)
                if r:
                    dve.wait_ge(struck, START + r)
                nc.vector.max(vals[:, eight], now[:, :]).then_inc(eight_ok, 1)
                dve.wait_ge(eight_ok, START + r + 1)
                if r < KT // 8 - 1:
                    nc.vector.match_replace(after[:, :], vals[:, eight], now[:, :], -1.0).then_inc(struck, 1)
                nc.vector.max_index(idx[:, eight], vals[:, eight], now[:, :])
            dve.drain()
            nc.vector.tensor_copy(rowf[:, :], idx[:, :])
            dve.drain()
            nc.vector.tensor_scalar(rowf[:, :], rowf[:, :], base[:, 0:1], None, ALU.add).then_inc(top_ok, 1)
            dve.wait_ge(i_tr, START + 1)
            nc.vector.tensor_copy(both[:, :, :, :], ps_i[:, :, :, :]).then_inc(i_ok, 1)
            dve.wait_ge(r_mm, START + 1)
            row, prob = both[:, 0, :, 0:R], both[:, 1, :, 0:R]
            nc.vector.tensor_tensor(gT[:, :, :], prob, ps_r[:, 1, :, :], ALU.max)
            nc.vector.tensor_tensor(first[:, :, :], prob, ps_r[:, 1, :, :], ALU.is_ge)
            nc.vector.tensor_tensor(step[:, :, :], row, ps_r[:, 0, :, :], ALU.subtract)
            dve.drain()
            nc.vector.tensor_tensor(step[:, :, :], step[:, :, :], first[:, :, :], ALU.mult)
            dve.drain()
            nc.vector.tensor_tensor(step[:, :, :], step[:, :, :], ps_r[:, 0, :, :], ALU.add)
            dve.drain()
            nc.vector.tensor_copy(idxT[:, :, :], step[:, :, :])

        @block.scalar
        def _(act):
            def scored(g):
                act.wait_ge(s_mm, START + g + 1)
                nc.scalar.copy(scT[:, ds(g * GT, GT)], ps_s[0:E, :]).then_inc(s_sb, 1)
            ln.scalar(act, 0)
            with act.Fori(0, NG - 1) as g:
                ln.scalar(act, g + 1)
                scored(g)
            scored(NG - 1)
            act.wait_ge(x_ok, START + 1)
            nc.scalar.activation(ex[:, :, :, :], sc[:, :, :, :], ACT.Exp).then_inc(e_ok, 1)
            act.wait_ge(p_tr, START + 1)
            nc.scalar.copy(PR[0][:, :], ps_p[0:2 * R, :]).then_inc(p_sb, 1)

        @block.tensor
        def _(pe):
            pe.wait_ge(weights, 48)
            def score(g):
                pe.wait_ge(ln.hTok, START + (g + 1) * DC)
                pe.wait_ge(s_sb, START + g)
                for c in range(DC):
                    i = nc.tensor.matmul(ps_s[0:E, :], gate_w[:, c, :], hT[:, c, ds(g * GT, GT)],
                                         start=(c == 0), stop=(c == DC - 1))
                i.then_inc(s_mm, 1)
            ln.tensor(pe, 0)
            with pe.Fori(0, NG // 2 - 1) as p:
                for s in range(2):
                    ln.tensor(pe, p * 2 + s + 1, 1 - s)
                    score(p * 2 + s)
            ln.tensor(pe, NG - 1, 1)
            score(NG - 2)
            score(NG - 1)
            pe.wait_ge(s_sb, START + NG)
            for b in range(B):
                for j in range(TB):
                    i = nc.tensor.transpose(ps_x[:, j % G * 2 + j // G, b, :], scT[:, (b * TB + j) * P:(b * TB + j + 1) * P],
                                            ident[0:E, 0:E])
            i.then_inc(x_tr, 1)
            pe.wait_ge(p_ok, START + 1)
            for j in range(G):
                i = nc.tensor.transpose(ps_p[0:2 * R, j * P:(j + 1) * P],
                                        pr[:, 2 * j:2 * j + 2, :, :].rearrange("p h b e -> p (h b e)"), ident[:, :])
            i.then_inc(p_tr, 1)
            pe.wait_ge(top_ok, START + 1)
            for s, src in enumerate((rowf, vals)):
                for c in range(C):
                    i = nc.tensor.transpose(ps_i[:, s, c, :], src[:, c * P:(c + 1) * P], ident[0:2 * R, 0:2 * R])
            i.then_inc(i_tr, 1)
            pe.wait_ge(i_ok, START + 1)
            for s in range(2):
                for c in range(C):
                    i = nc.tensor.matmul(ps_r[:, s, C - 1 - c, :], reverse[:, :], both[:, s, c, R:2 * R],
                                         start=True, stop=True)
            i.then_inc(r_mm, 1)


def experts(nc, ph, ident, E, C, M, h_rows, acc, idxT, gT, raw):
    HV = 2
    BH = B // HV
    NH = 4
    w1p = [[ph.sb(f"w1_{n}{i}", [P, DC, M * P], F32R) for n in ("top", "rest")] for i in range(2)]
    w2p = [[ph.sb(f"w2_{n}{i}", [P, M, D], F32R) for n in ("top", "rest")] for i in range(2)]
    cols = ph.sb("cols", [P, B, C], U32)
    xg = ph.sb("xg", [P, HV, G, D])
    xT = [ph.sb(f"xT_{n}", [P, DC, GT], F32R) for n in ("top", "rest")]
    hid = ph.sb("hid", [P, NH, GT])
    HT = [ph.sb(f"HT_{n}", [P, M, GT], F32R) for n in ("top", "rest")]
    ys = ph.sb("ys", [P, HV, G, D])
    ps_t = ph.ps("ps_t", [P, DC, GT])
    ps_h = ph.ps("ps_h", [P, NH, GT])
    ps_o = ph.ps("ps_o", [P, 2, GT])
    gathered = [ph.dma_sem(f"gathered{v}") for v in range(HV)]
    added = [ph.dma_sem(f"added{v}") for v in range(HV)]
    cols_ok, tr, x_top, x_rest = ph.sem("cols_ok"), ph.sem("tr"), ph.sem("x_top"), ph.sem("x_rest")
    w_top, w_rest = ph.sem("w_top"), ph.sem("w_rest")
    h_mm, h_top, h_rest = ph.sem("h_mm"), ph.sem("h_top"), ph.sem("h_rest")
    o_mm, y_ok = ph.sem("o_mm"), ph.sem("y_ok")
    passed = ph.sem("passed")
    EP = E // 2
    PARTS3 = ((0, 0), (0, 1), (1, 0))

    def quarter(s, k):
        if k < 2:
            return [t[:, k, :] for t in (raw.w1, *w1p[s])]
        half = slice((k - 2) * M // 2, (k - 1) * M // 2)
        return [t[:, half, :] for t in (raw.w2, *w2p[s])]

    def expert_turns(eng, turn):
        for s in range(2):
            turn(s, s, s == 0, False)
        with eng.Fori(1, EP - 1) as ep:
            for s in range(2):
                turn(ep * 2 + s, s, False, False)
        for s in range(2):
            turn(E - 2 + s, s, False, s == 1)
    cells = lambda t, e: t[:, :, :].rearrange("p c (b e) -> p b c e", e=E)[:, :, :, ds(e, 1)]

    with nc.Block() as block:
        @block.sync
        def _(sp):
            ph.start(sp)

            with sp.Fori(1, E) as e:
                sp.wait_ge(w_rest, START + 4 * (e - 1) + 2)
                raw.load_w1(sp, e)
                sp.wait_ge(w_rest, START + 4 * (e - 1) + 4)
                raw.load_w2(sp, e)
            sp.wait_ge(w_rest, START + 4 * E)
            sp.wait_ge(added[0], 16 * G * E)
            for n, t in enumerate((raw.w1, raw.w2)):
                sp.dma_start(raw.as_rows(t), sums_of(acc, 2 * n, 2)).then_inc(raw.sums_in, 16)
            sp.wait_ge(added[1], 16 * G * E)

        @block.gpsimd
        def _(pool):
            def gather(e, v):
                pool.wait_ge(tr, START + HV * (e - 1) + v + 1)
                pool.sem_inc(passed, 1)
                rows(v)

            def rows(v):
                for k in range(G):
                    pool.indirect_dma_start(out=xg[:, v, k, :], out_offset=None, in_=h_rows[:, :],
                                            in_offset=bass.IndirectOffsetOnAxis(
                                                ap=cols[:, BH * v + k // C, k % C:k % C + 1], axis=0)
                                            ).then_inc(gathered[v], 16)

            def scatter(e, v, first=False):
                if not first:
                    pool.wait_ge(added[v], 16 * G * e)
                for k in range(G):
                    pool.wait_ge(y_ok, START + (e * HV + v) * G + k + 1)
                    pool.sem_inc(passed, 1)
                    pool.indirect_dma_start(out=acc[:, :], out_offset=bass.IndirectOffsetOnAxis(
                                                ap=keep[:, BH * v + k // C, k % C:k % C + 1], axis=0),
                                            in_=ys[:, v, k, :], in_offset=None,
                                            compute_op=ALU.add).then_inc(added[v], 16)
            keep = ph.sb("keep", [P, B, C], U32)

            nc.gpsimd.tensor_copy(cols[:, :, :].unsqueeze(3), cells(idxT, 0)).then_inc(cols_ok, 1)
            pool.wait_ge(cols_ok, START + 1)
            for v in range(HV):
                rows(v)
            def step(e, first):
                for v in range(HV):
                    pool.wait_ge(gathered[v], 16 * G * (e + 1))
                    if not first:
                        pool.wait_ge(added[v], 16 * G * e)
                pool.sem_inc(passed, 1)
                nc.gpsimd.tensor_copy(keep[:, :, :], cols[:, :, :]).then_inc(cols_ok, 1)
                pool.wait_ge(cols_ok, START + 2 * e + 2)
                pool.sem_inc(passed, 1)
                nc.gpsimd.tensor_copy(cols[:, :, :].unsqueeze(3), cells(idxT, e + 1)).then_inc(cols_ok, 1)
                pool.wait_ge(cols_ok, START + 2 * e + 3)
                pool.sem_inc(passed, 1)
                for v in range(HV):
                    gather(e + 1, v)
                    scatter(e, v, first)
            step(0, True)
            with pool.Fori(1, E - 1) as e:
                step(e, False)
            for v in range(HV):
                pool.wait_ge(gathered[v], 16 * G * E)
                pool.wait_ge(added[v], 16 * G * (E - 1))
            nc.gpsimd.tensor_copy(keep[:, :, :], cols[:, :, :]).then_inc(cols_ok, 1)
            pool.wait_ge(cols_ok, START + 2 * E)
            for v in range(HV):
                scatter(E - 1, v)

        @block.vector
        def _(dve):
            def weights(e, s, ks):
                for k in ks:
                    dve.wait_ge(w_top, START + 4 * e + k + 1)
                    whole, top, rest = quarter(s, k)
                    nc.vector.tensor_tensor(rest, whole, top.bitcast(F32), ALU.subtract).then_inc(w_rest, 1)

            def transposed(i):
                for c in range(DC):
                    dve.wait_ge(x_top, START + i * DC + c + 1)
                    nc.vector.tensor_tensor(xT[1][:, c, :], ps_t[:, c, :], xT[0][:, c, :].bitcast(F32),
                                            ALU.subtract).then_inc(x_rest, 1)

            def hidden(i):
                for m in range(M):
                    dve.wait_ge(h_top, START + i * M + m + 1)
                    nc.vector.tensor_tensor(HT[1][:, m, :], hid[:, m % NH, :], HT[0][:, m, :].bitcast(F32),
                                            ALU.subtract).then_inc(h_rest, 1)

            def weigh(e, v, first):
                if not first:
                    dve.wait_ge(added[v], 16 * G * e)
                for k in range(G):
                    if k % 2 == 0:
                        dve.wait_ge(o_mm, START + (e * HV + v) * 2 + k // 2 + 1)
                    b, c = BH * v + k // C, k % C
                    nc.vector.tensor_scalar(ys[:, v, k, :], ps_o[:, k // 2, (k % 2) * D:(k % 2 + 1) * D],
                                            gT[:, c, ds(b * E + e, 1)], None, ALU.mult).then_inc(y_ok, 1)

            def turn(e, s, first, last):
                for v in range(HV):
                    i = e * HV + v
                    hidden(i)
                    if not (last and v == 1):
                        transposed(i + 1)
                    if not last:
                        weights(e + 1, 1 - s, (2 * v, 2 * v + 1))
                    weigh(e, v, first)
            weights(0, 0, range(2))
            transposed(0)
            weights(0, 0, range(2, 4))
            expert_turns(dve, turn)

        @block.scalar
        def _(act):
            def weights(e, s, ks):
                for k in ks:
                    if k % 2 == 0:
                        act.wait_ge(raw.w2_in if k else raw.w1_in, 16 * (e + 1))
                    whole, top, _ = quarter(s, k)
                    nc.scalar.copy(top, whole).then_inc(w_top, 1)

            def transposed(i):
                act.wait_ge(tr, START + i + 1)
                for c in range(DC):
                    nc.scalar.copy(xT[0][:, c, :], ps_t[:, c, :]).then_inc(x_top, 1)

            def hidden(i):
                for m in range(M):
                    act.wait_ge(h_mm, START + i * M + m + 1)
                    act.wait_ge(h_rest, START + i * M + m + 1 - NH)
                    nc.scalar.activation(hid[:, m % NH, :], ps_h[:, m % NH, :], ACT.Gelu_apprx_tanh)
                    nc.scalar.activation(HT[0][:, m, :], ps_h[:, m % NH, :], ACT.Gelu_apprx_tanh).then_inc(h_top, 1)

            def turn(e, s, first, last):
                for v in range(HV):
                    i = e * HV + v
                    hidden(i)
                    if not (last and v == 1):
                        transposed(i + 1)
                    if not last:
                        weights(e + 1, 1 - s, (2 * v, 2 * v + 1))
            weights(0, 0, range(2))
            transposed(0)
            weights(0, 0, range(2, 4))
            expert_turns(act, turn)

        @block.tensor
        def _(pe):
            def transposes(e, i, v):
                pe.wait_ge(gathered[v], 16 * G * (e + 1))
                pe.wait_ge(x_rest, START + i * DC)
                for c in range(DC):
                    for k in range(G):
                        x = nc.tensor.transpose(ps_t[:, c, k * P:(k + 1) * P], xg[:, v, k, c * P:(c + 1) * P],
                                                ident[:, :])
                x.then_inc(tr, 1)

            def turn(e, s, first, last):
                for v in range(HV):
                    i = e * HV + v
                    if v == 0:
                        pe.wait_ge(w_rest, START + 4 * e + 2)
                    pe.wait_ge(x_rest, START + (i + 1) * DC)
                    for m in range(M):
                        pe.wait_ge(h_top, START + i * M + m + 1 - NH)
                        n = 0
                        for c in range(DC):
                            for wp, xp in PARTS3:
                                x = nc.tensor.matmul(ps_h[:, m % NH, :], w1p[s][wp][:, c, m * P:(m + 1) * P],
                                                     xT[xp][:, c, :], start=(n == 0), stop=(n == 3 * DC - 1))
                                n += 1
                        x.then_inc(h_mm, 1)
                    if not (last and v == 1):
                        transposes(e + v, i + 1, 1 - v)
                    if v == 0:
                        pe.wait_ge(w_rest, START + 4 * e + 4)
                    pe.wait_ge(y_ok, START + i * G)
                    for m in range(M):
                        pe.wait_ge(h_rest, START + i * M + m + 1)
                        for k in range(G):
                            for n, (hp, wp) in enumerate(PARTS3):
                                x = nc.tensor.matmul(ps_o[:, k // 2, (k % 2) * D:(k % 2 + 1) * D],
                                                     HT[hp][:, m, k * P:(k + 1) * P], w2p[s][wp][:, m, :],
                                                     start=(m == 0 and k % 2 == 0 and n == 0),
                                                     stop=(m == M - 1 and k % 2 == 1 and n == 2))
                            if m == M - 1 and k % 2:
                                x.then_inc(o_mm, 1)
            transposes(0, 0, 0)
            expert_turns(pe, turn)


def sums_of(acc, g, n):
    return acc[g * GT:(g + n) * GT, :].rearrange("(j p) d -> p j d", p=P)


def add_rounded(nc, ph, X, acc, raw):
    NQ = NG // 2
    A = [raw.as_rows(raw.w1), raw.as_rows(raw.w2)]
    A += [ph.sb(f"A{q}", [P, 2 * G, D])[:, :, :] for q in range(2, NQ)]
    A16 = ph.sb("A16", [P, NQ, 2 * G, D], BF16)
    loads = [ph.dma_sem(f"loads{q}") for q in range(NQ)]
    rounded = ph.sem("rounded")
    with nc.Block() as block:
        @block.sync
        def _(sp):
            ph.start(sp)
            for q in range(2, NQ):
                sp.dma_start(A[q], sums_of(acc, 2 * q, 2)).then_inc(loads[q], 16)

        @block.vector
        def _(dve):
            dve.wait_ge(raw.sums_in, 32)
            for q in range(NQ):
                if q >= 2:
                    dve.wait_ge(loads[q], 16)
                nc.vector.tensor_copy(A16[:, q, :, :], A[q]).then_inc(rounded, 1)
                dve.wait_ge(rounded, START + q + 1)
                x8 = X[:, q * 2 * G:(q + 1) * 2 * G, :]
                nc.vector.tensor_tensor(x8, x8, A16[:, q, :, :], ALU.add)


PARTS = 3
PAIRS = [(0, 0), (1, 0), (2, 0), (0, 1), (1, 1), (0, 2)]
STACK = len(PAIRS) * HD


def attention(nc, ph, X, ident, a, kind, rest=None):
    parts = nc.dram_tensor(f"{ph.name}_parts", (2, PARTS, B * D, T), BF16, kind="Internal").ap()
    V = ph.sb("V", [P, B, H, TB, HD + 1])
    with ExitStack() as own:
        if kind == "decay":
            project_latent(nc, Phase(nc, own, ph.name + "p"), X, ident, a, parts, V, rest)
        else:
            project_rotary(nc, Phase(nc, own, ph.name + "p"), X, ident, a, parts, V)
    AO = ph.sb("AO", [P, B, TB, H, HD])
    with ExitStack() as own:
        if kind == "decay":
            heads_decay(nc, Phase(nc, own, ph.name + "h"), ident, a, parts, V, AO)
        else:
            heads_window(nc, Phase(nc, own, ph.name + "h"), ident, a, parts, V, AO)
    with ExitStack() as own:
        project_out(nc, Phase(nc, own, ph.name + "o"), X, ident,
                    a["L0_attn_a_W_o"] if kind == "decay" else a["out_wT"], AO)


class Split:

    def __init__(self, ph, parts):
        self.nc, self.parts = ph.nc, parts
        self.F = [ph.sb(f"sp_F{s}", [P, 2, DC, GT]) for s in range(2)]
        self.R = [ph.sb(f"sp_R{s}", [P, 2, DC, GT]) for s in range(2)]
        self.out = [[ph.sb(f"sp_{n}{s}", [P, 2, DC, GT], BF16) for s in range(2)] for n in range(PARTS)]
        self.f_ok = ph.sem("sp_f")
        self.first, self.rest = ph.sem("sp_first"), ph.sem("sp_rest")
        self.second, self.third = ph.sem("sp_second"), ph.sem("sp_third")
        self.GROUP = 16 * 2 * PARTS
        self.written = [ph.dma_sem(f"sp_written{s}", 16) for s in range(2)]

    def scalar_first(self, act, b, s):
        act.wait_ge(self.written[s], 16 + self.GROUP * b)
        act.wait_ge(self.f_ok, START + 2 * (b * 2 + s) + 2)
        self.nc.scalar.copy(self.out[0][s][:, :, :, :], self.F[s][:, :, :, :]).then_inc(self.first, 1)

    def scalar_second(self, act, g, s):
        act.wait_ge(self.rest, START + g + 1)
        self.nc.scalar.copy(self.out[1][s][:, :, :, :], self.R[s][:, :, :, :]).then_inc(self.second, 1)

    def vector(self, dve, g, s):
        dve.wait_ge(self.first, START + g + 1)
        dve.wait_ge(self.third, START + g - 1)
        self.nc.vector.tensor_tensor(self.R[s][:, :, :, :], self.F[s][:, :, :, :], self.out[0][s][:, :, :, :],
                                     ALU.subtract).then_inc(self.rest, 1)

    def pool(self, pool, g, s):
        pool.wait_ge(self.second, START + g + 1)
        self.nc.gpsimd.tensor_tensor(self.out[2][s][:, :, :, :], self.R[s][:, :, :, :], self.out[1][s][:, :, :, :],
                                     ALU.subtract).then_inc(self.third, 1)

    def sync(self, sp, b, h):
        for n, done in enumerate((self.first, self.second, self.third)):
            sp.wait_ge(done, START + b * 2 + h + 1)
            for w in range(2):
                sp.dma_start(self.parts[w, n, ds(b * D, D), h * GT:(h + 1) * GT].rearrange("(c p) t -> p c t", p=P),
                             self.out[n][h][:, w, :, :]).then_inc(self.written[h], 16)

    def all_written(self, sp):
        for s in range(2):
            sp.wait_ge(self.written[s], 16 + self.GROUP * B)


def load_head(sp, parts, n, q, k, loaded):
    rows, at = ds(n * HD, HD), 0
    for last in range(PARTS):
        m = PARTS - last
        to = slice(at * HD, (at + m) * HD)
        sp.dma_start(q[to, :], parts[0, 0:m, rows, :]).then_inc(loaded, 16)
        sp.dma_start(k[to, :], parts[1, last:last + 1, rows, :].to_broadcast([m, HD, T])).then_inc(loaded, 16)
        at += m


def batch_turns(eng, turn):
    for h in range(2):
        turn(0, h, h == 0, True)
    with eng.Fori(1, B - 1) as b:
        for h in range(2):
            turn(b, h, False, True)
    for h in range(2):
        turn(B - 1, h, False, False)


def project_latent(nc, ph, X, ident, a, parts, V, rest):
    DL = a["L0_attn_a_W_down_kv"].shape[1]
    HB = T // GT
    hT = ph.sb("hT", [P, DC, B * T])
    wq = ph.sb("wq", [P, DC, D])
    wkT, wvT = ph.sb("wkT", [P, DC, D]), ph.sb("wvT", [P, DC, D])
    wd = ph.sb("wd", [P, DC, DL])
    wuk, wuv = ph.sb("wuk", [DL, D]), ph.sb("wuv", [DL, D])
    wlat = ph.sb("wlat", [P, DC, DL])
    latT = ph.sb("latT", [DL, GT])
    ps_t = ph.ps("ps_t", [P, DC, GT])
    ps_q = ph.ps("ps_q", [P, DC, GT])
    ps_k = ph.ps("ps_k", [P, DC, GT])
    ps_l = ph.ps("ps_l", [P, GT])
    ps_v = ph.ps("ps_v", [P, 2, D])
    ln = LayerNorm(ph, X, ident, hT, ps_t)
    split = Split(ph, parts)
    weights = ph.dma_sem("weights")
    consts, wl_mm = ph.sem("consts"), ph.sem("wl_mm")
    q_mm, k_mm, l_mm, l_ok = ph.sem("q_mm"), ph.sem("k_mm"), ph.sem("l_mm"), ph.sem("l_ok")
    v_mm, v_ok = ph.sem("v_mm"), ph.sem("v_ok")
    part = lambda w: w.rearrange("(c p) n -> p c n", p=P)
    pairs = [(wkT[:, :, :], part(a["WkT"])), (wvT[:, :, :], part(a["WvT_a"])), (wq[:, :, :], part(a["L0_attn_a_W_q"])),
             (wd[:, :, :], part(a["L0_attn_a_W_down_kv"])), (wuk[:, :], a["L0_attn_a_W_up_k"]),
             (wuv[:, :], a["L0_attn_a_W_up_v"])]
    loaded = 16 * len(pairs)

    with nc.Block() as block:
        @block.sync
        def _(sp):
            ph.start(sp)
            load_once(sp, weights, pairs)
            with sp.Fori(0, B) as b:
                for h in range(HB):
                    split.sync(sp, b, h)
            split.all_written(sp)

        @block.gpsimd
        def _(pool):
            ln.pool_setup()
            pool.wait_ge(ln.rs, START + 1)
            nc.gpsimd.memset(V[:, :, :, :, HD], 1.0)
            ln.pool(pool, 0)
            ln.pool(pool, 1)

            def turn(b, h, first, more):
                g = b * HB + h
                if more:
                    ln.pool(pool, g + 2)
                if not first:
                    split.pool(pool, g - 1, 1 - h)
            batch_turns(pool, turn)
            split.pool(pool, NG - 1, 1)

        @block.vector
        def _(dve):
            dve.wait_ge(weights, loaded)
            nc.vector.tensor_tensor(wkT[:, :, :], wkT[:, :, :], wvT[:, :, :], ALU.add).then_inc(consts, 1)
            ln.vector(dve, 0)
            dve.wait_ge(wl_mm, START + 1)
            nc.vector.tensor_copy(wlat[:, :, :], ps_q[:, 0, 0:DC * DL].rearrange("p (c n) -> p c n", c=DC)
                                  ).then_inc(consts, 1)
            ln.vector(dve, 1)
            dve.wait_ge(rest, 16)

            def turn(b, h, first, more):
                g = b * HB + h
                if more:
                    ln.vector_moments(dve, g + 2)
                for k in range(G // 2):
                    dve.wait_ge(v_mm, START + g * (G // 2) + k + 1)
                    for j in range(2):
                        nc.vector.tensor_copy(V[:, ds(b, 1), :, h * G + 2 * k + j, 0:HD],
                                              ps_v[:, j, :].rearrange("p (a h d) -> p a h d", h=H, a=1)
                                              ).then_inc(v_ok, 1)
                if more:
                    ln.vector_rows(dve, g + 2)
                split.vector(dve, g, h)
            batch_turns(dve, turn)

        @block.scalar
        def _(act):
            def turn(b, h, first, more):
                g = b * HB + h
                act.wait_ge(l_mm, START + g + 1)
                act.wait_ge(v_mm, START + g * (G // 2))
                nc.scalar.copy(latT[:, :], ps_l[0:DL, :]).then_inc(l_ok, 1)
                act.wait_ge(split.third, START + g - 1)
                act.wait_ge(q_mm, START + g + 1)
                nc.scalar.copy(split.F[h][:, 0, :, :], ps_q[:, :, :]).then_inc(split.f_ok, 1)
                act.wait_ge(k_mm, START + g + 1)
                nc.scalar.copy(split.F[h][:, 1, :, :], ps_k[:, :, :]).then_inc(split.f_ok, 1)
                if more or h == 0:
                    ln.scalar(act, g + 1)
                split.scalar_first(act, b, h)
                if not first:
                    split.scalar_second(act, g - 1, 1 - h)
            ln.scalar(act, 0)
            batch_turns(act, turn)
            split.scalar_second(act, NG - 1, 1)

        @block.tensor
        def _(pe):
            pe.wait_ge(weights, loaded)
            pe.wait_ge(consts, START + 1)
            for c in range(DC):
                for k in range(DC):
                    i = nc.tensor.matmul(ps_q[:, 0, c * DL:(c + 1) * DL], wkT[:, k, c * P:(c + 1) * P],
                                         wd[:, k, :], start=(k == 0), stop=(k == DC - 1))
            i.then_inc(wl_mm, 1)
            pe.wait_ge(consts, START + 2)

            def turn(g, following):
                pe.wait_ge(ln.hTok, START + (g + 1) * DC)
                pe.wait_ge(l_ok, START + g)
                for k in range(DC):
                    i = nc.tensor.matmul(ps_l[0:DL, :], wlat[:, k, :], hT[:, k, ds(g * GT, GT)],
                                         start=(k == 0), stop=(k == DC - 1))
                i.then_inc(l_mm, 1)
                pe.wait_ge(split.f_ok, START + 2 * g)
                for c in range(DC):
                    for k in range(DC):
                        i = nc.tensor.matmul(ps_q[:, c, :], wq[:, k, c * P:(c + 1) * P], hT[:, k, ds(g * GT, GT)],
                                             start=(k == 0), stop=(k == DC - 1))
                i.then_inc(q_mm, 1)
                if following:
                    ln.tensor(pe, g + 1)
                pe.wait_ge(l_ok, START + g + 1)
                for c in range(DC):
                    i = nc.tensor.matmul(ps_k[:, c, :], wuk[:, c * P:(c + 1) * P], latT[:, :], start=True, stop=True)
                i.then_inc(k_mm, 1)
                for k in range(G // 2):
                    pe.wait_ge(v_ok, START + g * G + 2 * k)
                    for j in range(2):
                        t = (2 * k + j) * P
                        i = nc.tensor.matmul(ps_v[:, j, :], latT[:, t:t + P], wuv[:, :], start=True, stop=True)
                    i.then_inc(v_mm, 1)
            ln.tensor(pe, 0)
            with pe.Fori(0, NG - 1) as g:
                turn(g, True)
            turn(NG - 1, False)


def project_rotary(nc, ph, X, ident, a, parts, V):
    HB = T // GT
    hT = ph.sb("hT", [P, 2, DC, GT])
    w = ph.sb("w", [P, DC, 3 * D])
    wr = ph.sb("wr", [P, DC, 2 * D])
    cos, sin = ph.sb("cos", [P, T]), ph.sb("sin", [P, T])
    AB = ph.sb("AB", [P, 2, 2, DC, GT])
    ps_t = ph.ps("ps_t", [P, DC, GT])
    ps_q, ps_r = ph.ps("ps_q", [P, DC, GT]), ph.ps("ps_r", [P, DC, GT])
    ps_v = ph.ps("ps_v", [P, 2, D])
    ln = LayerNorm(ph, X, ident, hT, ps_t)
    split = Split(ph, parts)
    weights = ph.dma_sem("weights")
    consts, r_mm, ab_ok = ph.sem("consts"), ph.sem("r_mm"), ph.sem("ab_ok")
    v_mm, v_ok = ph.sem("v_mm"), ph.sem("v_ok")
    pairs = [(w[:, :, :], a["qkv_wT"].rearrange("(c p) n -> p c n", p=P)), (cos[:, :], a["cos"]), (sin[:, :], a["sin"])]
    loaded = 16 * len(pairs)

    with nc.Block() as block:
        @block.sync
        def _(sp):
            ph.start(sp)
            load_once(sp, weights, pairs)
            with sp.Fori(0, B) as b:
                for h in range(HB):
                    split.sync(sp, b, h)
            split.all_written(sp)

        @block.gpsimd
        def _(pool):
            ln.pool_setup()
            pool.wait_ge(ln.rs, START + 1)
            nc.gpsimd.memset(V[:, :, :, :, HD], 1.0)
            ln.pool(pool, 0)
            ln.pool(pool, 1)

            def turn(b, h, first, more):
                g = b * HB + h
                pool.wait_ge(split.third, START + g - 1)
                for s in range(2):
                    pool.wait_ge(ab_ok, START + (2 * g + s + 1) * DC)
                    nc.gpsimd.tensor_tensor(split.F[h][:, s, :, :], AB[:, s, 0, :, :], AB[:, s, 1, :, :],
                                            ALU.add).then_inc(split.f_ok, 1)
                if more:
                    ln.pool(pool, g + 2)
                if not first:
                    split.pool(pool, g - 1, 1 - h)
            batch_turns(pool, turn)
            split.pool(pool, NG - 1, 1)

        @block.vector
        def _(dve):
            dve.wait_ge(weights, loaded)
            pair = lambda t: t[:, :, 0:2 * D].rearrange("p c (n two) -> p c n two", two=2)
            nc.vector.tensor_scalar(pair(wr)[:, :, :, 0], pair(w)[:, :, :, 1], -1.0, None, ALU.mult).then_inc(consts, 1)
            nc.vector.tensor_copy(pair(wr)[:, :, :, 1], pair(w)[:, :, :, 0]).then_inc(consts, 1)
            ln.vector(dve, 0)
            ln.vector(dve, 1)

            def turn(b, h, first, more):
                g = b * HB + h
                now = lambda t: t[:, h * GT:(h + 1) * GT]
                for s in range(2):
                    dve.wait_ge(split.f_ok, START + 2 * g + s - 1)
                    for c in range(DC):
                        dve.wait_ge(r_mm, START + (2 * g + s) * DC + c + 1)
                        nc.vector.tensor_tensor(AB[:, s, 0, c, :], ps_q[:, c, :], now(cos), ALU.mult)
                        nc.vector.tensor_tensor(AB[:, s, 1, c, :], ps_r[:, c, :], now(sin), ALU.mult
                                                ).then_inc(ab_ok, 1)
                if more:
                    ln.vector_moments(dve, g + 2)
                if more:
                    ln.vector_rows(dve, g + 2)
                split.vector(dve, g, h)
            batch_turns(dve, turn)

        @block.scalar
        def _(act):
            def turn(b, h, first, more):
                g = b * HB + h
                if more or h == 0:
                    ln.scalar(act, g + 1, 1 - h)
                if not first:
                    split.scalar_second(act, g - 1, 1 - h)
                for k in range(G // 2):
                    act.wait_ge(v_mm, START + g * (G // 2) + k + 1)
                    for j in range(2):
                        nc.scalar.copy(V[:, ds(b, 1), :, h * G + 2 * k + j, 0:HD],
                                       ps_v[:, j, :].rearrange("p (a h d) -> p a h d", h=H, a=1)
                                       ).then_inc(v_ok, 1)
                split.scalar_first(act, b, h)
            ln.scalar(act, 0, 0)
            batch_turns(act, turn)
            split.scalar_second(act, NG - 1, 1)

        @block.tensor
        def _(pe):
            pe.wait_ge(weights, loaded)
            pe.wait_ge(consts, START + 2)

            def turn(g, h, following):
                pe.wait_ge(ln.hTok, START + (g + 1) * DC)
                for s in range(2):
                    for c in range(DC):
                        pe.wait_ge(ab_ok, START + (2 * g + s - 1) * DC + c + 1)
                        for out, weight in ((ps_q, w), (ps_r, wr)):
                            for k in range(DC):
                                i = nc.tensor.matmul(out[:, c, :], weight[:, k, s * D + c * P:s * D + (c + 1) * P],
                                                     hT[:, h, k, :], start=(k == 0), stop=(k == DC - 1))
                        i.then_inc(r_mm, 1)
                    if s == 0 and following:
                        ln.tensor(pe, g + 1)
                for k in range(G // 2):
                    pe.wait_ge(v_ok, START + g * G + 2 * k)
                    for j in range(2):
                        t = (2 * k + j) * P
                        for c in range(DC):
                            i = nc.tensor.matmul(ps_v[:, j, :], hT[:, h, c, t:t + P], w[:, c, 2 * D:3 * D],
                                                 start=(c == 0), stop=(c == DC - 1))
                    i.then_inc(v_mm, 1)
            ln.tensor(pe, 0)
            with pe.Fori(0, B - 1) as b:
                for h in range(HB):
                    turn(b * HB + h, h, True)
            for h in range(HB):
                turn((B - 1) * HB + h, h, h == 0)


def heads_decay(nc, ph, ident, a, parts, V, AO):
    qs = [ph.sb(f"qs{i}", [STACK, T], BF16) for i in range(2)]
    ks = [ph.sb(f"ks{i}", [STACK, T], BF16) for i in range(2)]
    table = ph.sb("table", [P, 2 * T - P])
    gather = ph.sb("gather", [P, HD + 1])
    NBUF = 4
    SD = [ph.sb(f"SD{i}", [P, T]) for i in range(NBUF)]
    PM = [ph.sb(f"PM{i}", [P, T]) for i in range(NBUF)]
    PT = [ph.sb(f"PT{i}", [P, TB, GT]) for i in range(2)]
    W = 32
    Vs = [ph.sb(f"Vs{i}", [P, TB, W]) for i in range(2)]
    OT = [ph.sb(f"OT{i}", [P, GT]) for i in range(2)]
    U = 2 * TB
    mx, nb = ph.sb("mx", [P, U]), ph.sb("nb", [P, U])
    minus, rc = ph.sb("minus", [P, 1]), ph.sb("rc", [P, G])
    ps_s = [ph.ps(f"ps_s{i}", [P, 2, GT]) for i in range(2)]
    ps_t = ph.ps("ps_t", [P, 2, GT])
    ps_v, ps_o = ph.ps("ps_v", [P, GT]), ph.ps("ps_o", [P, GT])
    tabled = ph.dma_sem("tabled")
    loads = [ph.dma_sem(f"loads{i}") for i in range(2)]
    s_mm, m_ok, nb_ok, e_ok = ph.sem("s_mm"), ph.sem("m_ok"), ph.sem("nb_ok"), ph.sem("e_ok")
    ta_mm, tb_mm, ta_ok, tb_ok = ph.sem("ta_mm"), ph.sem("tb_mm"), ph.sem("ta_ok"), ph.sem("tb_ok")
    pv_mm, ot_ok, o_mm, n_ok = ph.sem("pv_mm"), ph.sem("ot_ok"), ph.sem("o_mm"), ph.sem("n_ok")
    passed, minus_ok, vs_ok = ph.sem("passed"), ph.sem("minus_ok"), ph.sem("vs_ok")
    NP = B * H // 2
    ND = 2 * PARTS
    UH = U // G

    with nc.Block() as block:
        @block.sync
        def _(sp):
            ph.start(sp)
            sp.dma_start(table[:, :], a["decay"]).then_inc(tabled, 16)
            sp.dma_start(gather[:, :], a["gather"]).then_inc(tabled, 16)

            def load(n, s):
                load_head(sp, parts, n, qs[s], ks[s], loads[s])
            load(0, 0)
            load(1, 1)
            with sp.Fori(1, NP) as pr:
                for s in range(2):
                    sp.wait_ge(s_mm, START + (pr * 2 + s - 1) * TB)
                    load(pr * 2 + s, s)

        @block.gpsimd
        def _(pool):
            Vn = V[:, :, :, :, :].rearrange("p b h t d -> p (b h) t d")
            for s in range(2):
                nc.gpsimd.memset(Vs[s][:, :, :], 0.0).then_inc(minus_ok, 1)
            nc.gpsimd.memset(minus[:, :], -1.0).then_inc(minus_ok, 1)
            pool.wait_ge(minus_ok, START + 3)
            with pool.Fori(0, NP) as pr:
                for u in range(U):
                    if u % TB == 1:
                        s = u // TB
                        pool.wait_ge(pv_mm, START + (pr * 2 + s) * 2 - 2)
                        pool.sem_inc(passed, 1)
                        nc.gpsimd.tensor_copy(Vs[s][:, :, 0:HD + 1],
                                              Vn[:, ds(pr * 2 + s, 1), :, :].rearrange("p a t d -> p (a t) d")
                                              ).then_inc(vs_ok, 1)
                    pool.wait_ge(m_ok, START + pr * U + u + 1)
                    nc.gpsimd.tensor_tensor(nb[:, u:u + 1], mx[:, u:u + 1], minus[:, :], ALU.mult).then_inc(nb_ok, 1)

        @block.vector
        def _(dve):
            dve.wait_ge(tabled, 32)

            def most(i, u):
                dve.wait_ge(s_mm, START + i + 1)
                dve.wait_ge(e_ok, START + i + 1 - NBUF)
                dve.sem_inc(passed, 1)
                t = u % TB
                nc.vector.tensor_tensor_reduce(SD[u % NBUF][:, :],
                                               ps_s[u % 2][:, :, :].rearrange("p a n -> p (a n)"),
                                               table[:, (TB - 1 - t) * P:(TB - 1 - t) * P + T], 1.0, -3e38,
                                               ALU.mult, ALU.max, accum_out=mx[:, u:u + 1]).then_inc(m_ok, 1)

            def copy(i, u):
                dve.wait_ge(ta_mm, START + i + 1)
                q = u % G * P
                nc.vector.tensor_copy(PT[u // G % 2][:, 0:G, q:q + P],
                                      ps_t[:, 0, :].rearrange("p (k q) -> p k q", k=G)).then_inc(ta_ok, 1)

            def norm(n, half, hh):
                dve.wait_ge(o_mm, START + hh + 1)
                o = ps_o[:, 0:G * (HD + 1)].rearrange("p (t d) -> p t d", t=G)
                nc.vector.reciprocal(rc[:, :], o[:, :, HD])
                dve.drain()
                to = AO[:, ds(n // H, 1), half * G:(half + 1) * G, ds(n % H, 1), :].rearrange("p b t h d -> p (b t h) d")
                nc.vector.tensor_tensor(to, o[:, :, 0:HD],
                                        rc[:, :].unsqueeze(2).to_broadcast([P, G, HD]), ALU.mult).then_inc(n_ok, 1)

            def turn(pr, first, last):
                for u in range(U):
                    i = pr * U + u
                    if not (last and u >= U - 2):
                        most(i + 2, (u + 2) % U)
                    if u % G != 0:
                        copy(i, u)
                    v = u // G - 3
                    if u % G == 0 and not (first and v < 0):
                        norm(pr * 2 + v // 2, v % 2, pr * UH + v)
            most(0, 0)
            most(1, 1)
            turn(0, True, False)
            with dve.Fori(1, NP - 1) as pr:
                turn(pr, False, False)
            turn(NP - 1, False, True)
            norm(NP * 2 - 2, 1, NP * UH - 3)
            norm(NP * 2 - 1, 0, NP * UH - 2)
            norm(NP * 2 - 1, 1, NP * UH - 1)

        @block.scalar
        def _(act):
            def exp(i, u):
                act.wait_ge(nb_ok, START + i + 1)
                act.wait_ge(tb_mm, START + i + 1 - NBUF)
                nc.scalar.activation(PM[u % NBUF][:, :], SD[u % NBUF][:, :], ACT.Exp, bias=nb[:, u:u + 1]
                                     ).then_inc(e_ok, 1)

            def copy(i, u):
                act.wait_ge(tb_mm, START + i + 1)
                q = u % G * P
                nc.scalar.copy(PT[u // G % 2][:, G:, q:q + P],
                               ps_t[:, 1, :].rearrange("p (k q) -> p k q", k=G)).then_inc(tb_ok, 1)

            def copy_too(i, u):
                act.wait_ge(ta_mm, START + i + 1)
                q = u % G * P
                nc.scalar.copy(PT[u // G % 2][:, 0:G, q:q + P],
                               ps_t[:, 0, :].rearrange("p (k q) -> p k q", k=G)).then_inc(ta_ok, 1)

            def collect(hh, v):
                act.wait_ge(pv_mm, START + hh + 1)
                nc.scalar.copy(OT[v % 2][:, :], ps_v[:, :]).then_inc(ot_ok, 1)

            def turn(pr, first, last):
                for u in range(U):
                    i = pr * U + u
                    if not (last and u == U - 1):
                        exp(i + 1, (u + 1) % U)
                    if u % G == 0:
                        copy_too(i, u)
                    copy(i, u)
                    if u % G == 3 and not (first and u < G):
                        collect(pr * UH + u // G - 1, u // G - 1)
            exp(0, 0)
            turn(0, True, False)
            with act.Fori(1, NP - 1) as pr:
                turn(pr, False, False)
            turn(NP - 1, False, True)
            collect(NP * UH - 1, 1)

        @block.tensor
        def _(pe):
            pe.wait_ge(tabled, 32)

            def scores(i, u):
                s, t = u // TB, u % TB
                pe.wait_ge(m_ok, START + i - 1)
                for k in range(2):
                    x = nc.tensor.matmul(ps_s[u % 2][:, k, :], qs[s][:, t * P:(t + 1) * P],
                                         ks[s][:, k * GT:(k + 1) * GT], start=True, stop=True)
                x.then_inc(s_mm, 1)

            def transposes(i, u):
                pe.wait_ge(e_ok, START + i + 1)
                for bank, out, done in ((0, ta_ok, ta_mm), (1, tb_ok, tb_mm)):
                    pe.wait_ge(out, START + i)
                    for k in range(G):
                        at = (bank * G + k) * P
                        x = nc.tensor.transpose(ps_t[:, bank, k * P:(k + 1) * P], PM[u % NBUF][:, at:at + P],
                                                ident[:, :])
                    x.then_inc(done, 1)

            def values(n, hh, v, r, i):
                if r == 0:
                    pe.wait_ge(ta_ok, START + i)
                    pe.wait_ge(tb_ok, START + i)
                    pe.wait_ge(ot_ok, START + hh)
                    if v % 2 == 0:
                        pe.wait_ge(vs_ok, START + n + 1)
                for j in range(G):
                    x = nc.tensor.matmul(ps_v[j * W:(j + 1) * W, :], Vs[v // 2][:, 2 * j + r, :],
                                         PT[v % 2][:, 2 * j + r, :], start=(r == 0), stop=(r == 1),
                                         tile_position=(0, j * W))
                if r == 1:
                    x.then_inc(pv_mm, 1)

            def gathered(hh, v, part):
                if part == 0:
                    pe.wait_ge(ot_ok, START + hh + 1)
                    pe.wait_ge(n_ok, START + hh)
                for t in (2 * part, 2 * part + 1):
                    x = nc.tensor.matmul(ps_o[:, t * (HD + 1):(t + 1) * (HD + 1)], OT[v % 2][:, t * P:(t + 1) * P],
                                         gather[:, :], start=True, stop=True)
                if part == 1:
                    x.then_inc(o_mm, 1)

            def turn(pr, first, last):
                for u in range(U):
                    i = pr * U + u
                    if not (last and u >= U - 3):
                        if u == U - 3:
                            pe.wait_ge(loads[0], 16 * ND * (pr + 2))
                        if u == TB - 3:
                            pe.wait_ge(loads[1], 16 * ND * (pr + 1))
                        scores(i + 3, (u + 3) % U)
                    transposes(i, u)
                    r = u % G
                    v = u // G - (2 if r % 2 else 1)
                    if first and v < 0:
                        continue
                    if r % 2:
                        gathered(pr * UH + v, v, r // 2)
                    else:
                        values(pr * 2 + v // 2, pr * UH + v, v % UH, r // 2, pr * U + u - r)
            pe.wait_ge(loads[0], 16 * ND)
            scores(0, 0)
            scores(1, 1)
            scores(2, 2)
            turn(0, True, False)
            with pe.Fori(1, NP - 1) as pr:
                turn(pr, False, False)
            turn(NP - 1, False, True)
            for v in (UH - 2, UH - 1):
                for r in range(2):
                    if v == UH - 1:
                        values(NP * 2 - 1, NP * UH - 1, UH - 1, r, NP * U)
                for r in range(2):
                    gathered(NP * UH - UH + v, v, r)


def heads_window(nc, ph, ident, a, parts, V, AO):
    NGL = 4
    WK = 2 * P + NGL
    W = 32
    qs = [ph.sb(f"qs{i}", [STACK, T], BF16) for i in range(2)]
    ks = [ph.sb(f"ks{i}", [STACK, T], BF16) for i in range(2)]
    table = ph.sb("table", [P, 3, WK])
    NBUF = 4
    SD = [ph.sb(f"SD{i}", [P, WK]) for i in range(NBUF)]
    PM = [ph.sb(f"PM{i}", [P, WK]) for i in range(NBUF)]
    PT = [ph.sb(f"PT{i}", [P, G, 2, P]) for i in range(2)]
    PG = [ph.sb(f"PG{i}", [NGL, G, P]) for i in range(2)]
    Vs = [ph.sb(f"Vs{i}", [P, TB, W]) for i in range(2)]
    OT = ph.sb("OT", [P, P])
    U = 2 * TB
    mx, nb = ph.sb("mx", [P, U]), ph.sb("nb", [P, U])
    minus, rc = ph.sb("minus", [P, 1]), ph.sb("rc", [P, G])
    ps_s = [ph.ps(f"ps_s{i}", [P, GT]) for i in range(2)]
    ps_t = [ph.ps(f"ps_t{i}", [P, 2, 2, P]) for i in range(2)]
    ps_g = [ph.ps(f"ps_g{i}", [P, 4, P]) for i in range(2)]
    ps_v, ps_o = ph.ps("ps_v", [P, GT]), ph.ps("ps_o", [P, GT])
    tabled = ph.dma_sem("tabled")
    loads = [ph.dma_sem(f"loads{i}") for i in range(2)]
    s_mm, m_ok, nb_ok, e_ok = ph.sem("s_mm"), ph.sem("m_ok"), ph.sem("nb_ok"), ph.sem("e_ok")
    t_mm, g_mm, t_ok, g_ok = ph.sem("t_mm"), ph.sem("g_mm"), ph.sem("t_ok"), ph.sem("g_ok")
    pv_mm, ot_ok, o_mm, n_ok = ph.sem("pv_mm"), ph.sem("ot_ok"), ph.sem("o_mm"), ph.sem("n_ok")
    passed, minus_ok, vs_ok = ph.sem("passed"), ph.sem("minus_ok"), ph.sem("vs_ok")
    NP = B * H // 2
    ND = 2 * PARTS
    UH = U // G
    PG_HEAD = TB // 2 - 1

    def keys(t):
        if t == 0:
            return [(0, P)]
        return [((t - 1) * P, 2 * P)] + ([(0, NGL)] if t >= 2 else [])

    def width(t):
        return sum(n for _, n in keys(t))

    with nc.Block() as block:
        @block.sync
        def _(sp):
            ph.start(sp)
            sp.dma_start(table[:, :, :], a["masks"].rearrange("p (m k) -> p m k", m=3)).then_inc(tabled, 16)

            def load(n, s):
                load_head(sp, parts, n, qs[s], ks[s], loads[s])
            load(0, 0)
            load(1, 1)
            with sp.Fori(1, NP) as pr:
                for s in range(2):
                    sp.wait_ge(s_mm, START + (pr * 2 + s - 1) * TB)
                    load(pr * 2 + s, s)

        @block.gpsimd
        def _(pool):
            Vn = V[:, :, :, :, :].rearrange("p b h t d -> p (b h) t d")
            for s in range(2):
                nc.gpsimd.memset(Vs[s][:, :, :], 0.0).then_inc(minus_ok, 1)
            nc.gpsimd.memset(minus[:, :], -1.0).then_inc(minus_ok, 1)
            pool.wait_ge(minus_ok, START + 3)
            with pool.Fori(0, NP) as pr:
                for u in range(U):
                    if u % TB == 2:
                        s = u // TB
                        pool.wait_ge(pv_mm, START + (pr * 2 + s) * 2 - 2)
                        pool.sem_inc(passed, 1)
                        nc.gpsimd.tensor_copy(Vs[s][:, :, 0:HD + 1],
                                              Vn[:, ds(pr * 2 + s, 1), :, :].rearrange("p a t d -> p (a t) d")
                                              ).then_inc(vs_ok, 1)
                    pool.wait_ge(m_ok, START + pr * U + u + 1)
                    nc.gpsimd.tensor_tensor(nb[:, u:u + 1], mx[:, u:u + 1], minus[:, :], ALU.mult).then_inc(nb_ok, 1)

        @block.vector
        def _(dve):
            dve.wait_ge(tabled, 16)

            def most(i, u):
                dve.wait_ge(s_mm, START + i + 1)
                dve.wait_ge(e_ok, START + i + 1 - NBUF)
                dve.sem_inc(passed, 1)
                n = width(u % TB)
                nc.vector.tensor_tensor_reduce(SD[u % NBUF][:, 0:n], ps_s[u % 2][:, 0:n],
                                               table[:, min(u % TB, 2), 0:n], HD ** -0.5, -3e38,
                                               ALU.add, ALU.max, accum_out=mx[:, u:u + 1]).then_inc(m_ok, 1)

            def copy(pair, u):
                dve.wait_ge(t_mm, START + pair + 1)
                first = 1 if u % TB == 1 else 0
                flat = lambda t: t.rearrange("p s k q -> p (s k) q")[:, first:4, :]
                nc.vector.tensor_copy(flat(PT[u // G % 2][:, u % G - 1:u % G + 1, :, :]),
                                      flat(ps_t[u // 2 % 2][:, :, :, :])).then_inc(t_ok, 1)

            def norm(n, half, hh):
                dve.wait_ge(o_mm, START + hh + 1)
                o = ps_o[:, 0:P].rearrange("p (t d) -> p t d", t=G)
                nc.vector.reciprocal(rc[:, :], o[:, :, HD])
                dve.drain()
                to = AO[:, ds(n // H, 1), half * G:(half + 1) * G, ds(n % H, 1), :].rearrange("p b t h d -> p (b t h) d")
                nc.vector.tensor_tensor(to, o[:, :, 0:HD],
                                        rc[:, :].unsqueeze(2).to_broadcast([P, G, HD]), ALU.mult).then_inc(n_ok, 1)

            def turn(pr, first, last):
                for u in range(U):
                    if not (last and u >= U - 2):
                        most(pr * U + u + 2, (u + 2) % U)
                    if u % 2 == 1 and not (u % TB == 1):
                        copy(pr * (U // 2) + u // 2, u)
                    if u % G == 0 and not (first and u < 2 * G):
                        v = u // G - 2
                        norm(pr * 2 + v // 2, v % 2, pr * UH + v)
            most(0, 0)
            most(1, 1)
            turn(0, True, False)
            with dve.Fori(1, NP - 1) as pr:
                turn(pr, False, False)
            turn(NP - 1, False, True)
            norm(NP * 2 - 1, 0, NP * UH - 2)
            norm(NP * 2 - 1, 1, NP * UH - 1)

        @block.scalar
        def _(act):
            def exp(i, pair, u):
                act.wait_ge(nb_ok, START + i + 1)
                act.wait_ge(t_mm, START + pair - 1)
                n = width(u % TB)
                nc.scalar.activation(PM[u % NBUF][:, 0:n], SD[u % NBUF][:, 0:n], ACT.Exp, bias=nb[:, u:u + 1]
                                     ).then_inc(e_ok, 1)

            def copy(n, u):
                k = u % TB // 2
                act.wait_ge(g_mm, START + n * PG_HEAD + k)
                nc.scalar.copy(PG[u // G % 2][:, u % G - 1:u % G + 1, :], ps_g[k % 2][0:NGL, 0:2, :]).then_inc(g_ok, 1)

            def copy_tiles(pair, u):
                act.wait_ge(t_mm, START + pair + 1)
                first = 1 if u % TB == 1 else 0
                flat = lambda t: t.rearrange("p s k q -> p (s k) q")[:, first:4, :]
                nc.scalar.copy(flat(PT[u // G % 2][:, u % G - 1:u % G + 1, :, :]),
                                      flat(ps_t[u // 2 % 2][:, :, :, :])).then_inc(t_ok, 1)

            def collect(hh):
                act.wait_ge(pv_mm, START + hh + 1)
                nc.scalar.copy(OT[:, :], ps_v[:, 0:P]).then_inc(ot_ok, 1)

            def turn(pr, first, last):
                for u in range(U):
                    if not (last and u == U - 1):
                        exp(pr * U + u + 1, pr * (U // 2) + (u + 1) // 2, (u + 1) % U)
                    if u % TB == 1:
                        copy_tiles(pr * (U // 2) + u // 2, u)
                    if u % TB > 2 and u % 2 == 1:
                        copy(pr * 2 + u // TB, u)
                    if u % G == 2 and not (first and u < G):
                        collect(pr * UH + u // G - 1)
            exp(0, 0, 0)
            turn(0, True, False)
            with act.Fori(1, NP - 1) as pr:
                turn(pr, False, False)
            turn(NP - 1, False, True)
            collect(NP * UH - 1)

        @block.tensor
        def _(pe):
            def scores(i, u):
                s, t = u // TB, u % TB
                pe.wait_ge(m_ok, START + i - 1)
                at = 0
                for k0, n in keys(t):
                    x = nc.tensor.matmul(ps_s[u % 2][:, at:at + n], qs[s][:, t * P:(t + 1) * P], ks[s][:, k0:k0 + n],
                                         start=True, stop=True)
                    at += n
                x.then_inc(s_mm, 1)

            def transposes(i, pair, n, u):
                t = u % TB
                pe.wait_ge(e_ok, START + i + 1)
                if u % 2 == 0:
                    pe.wait_ge(t_ok, START + pair - 1)
                pm, bank = PM[u % NBUF], ps_t[u // 2 % 2]
                if t >= 2:
                    if u % 2 == 0:
                        pe.wait_ge(g_ok, START + n * PG_HEAD + max(t // 2 - 2, 0))
                    y = nc.tensor.transpose(ps_g[t // 2 % 2][0:NGL, u % 2, :], pm[:, 2 * P:WK], ident[:, :])
                    if u % 2 == 1:
                        y.then_inc(g_mm, 1)
                for k in range(2 if t else 1):
                    x = nc.tensor.transpose(bank[:, u % 2, k if t else 1, :], pm[:, k * P:(k + 1) * P], ident[:, :])
                if u % 2 == 1:
                    x.then_inc(t_mm, 1)

            def values(n, hh, v):
                half = v % 2
                pe.wait_ge(t_ok, START + (hh + 1) * 2)
                pe.wait_ge(g_ok, START + n * PG_HEAD + (PG_HEAD if half else 1))
                pe.wait_ge(ot_ok, START + hh)
                if half == 0:
                    pe.wait_ge(vs_ok, START + n + 1)
                for k in (1, 0, 2):
                    for j in range(G):
                        t = half * G + j
                        if t + k < 1 or (k == 2 and t < 2):
                            continue
                        out = ps_v[j * W:(j + 1) * W, 0:P]
                        stop = k == (0 if t == 1 else 1 if t == 0 else 2)
                        if k == 2:
                            x = nc.tensor.matmul(out, Vs[v // 2][0:NGL, 0, :], PG[half][:, j, :],
                                                 start=False, stop=stop, tile_position=(0, j * W))
                        else:
                            x = nc.tensor.matmul(out, Vs[v // 2][:, t - 1 + k, :], PT[half][:, j, k, :],
                                                 start=(k == 1), stop=stop, tile_position=(0, j * W))
                x.then_inc(pv_mm, 1)

            def turned(hh):
                pe.wait_ge(ot_ok, START + hh + 1)
                pe.wait_ge(n_ok, START + hh)
                nc.tensor.transpose(ps_o[:, 0:P], OT[:, :], ident[:, :]).then_inc(o_mm, 1)

            def turn(pr, first, last):
                for u in range(U):
                    i = pr * U + u
                    if not (last and u >= U - 3):
                        if u == U - 3:
                            pe.wait_ge(loads[0], 16 * ND * (pr + 2))
                        if u == TB - 3:
                            pe.wait_ge(loads[1], 16 * ND * (pr + 1))
                        scores(i + 3, (u + 3) % U)
                    transposes(i, pr * (U // 2) + u // 2, pr * 2 + u // TB, u)
                    v = u // G - 1
                    if u % G == 1 and not (first and v < 0):
                        values(pr * 2 + v // 2, pr * UH + v, v % UH)
                    if u % G == 3 and not (first and v < 0):
                        turned(pr * UH + v)
            pe.wait_ge(loads[0], 16 * ND)
            scores(0, 0)
            scores(1, 1)
            scores(2, 2)
            turn(0, True, False)
            with pe.Fori(1, NP - 1) as pr:
                turn(pr, False, False)
            turn(NP - 1, False, True)
            values(NP * 2 - 1, NP * UH - 1, UH - 1)
            turned(NP * UH - 1)


def project_out(nc, ph, X, ident, w, AO):
    wo = ph.sb("wo", [P, DC, D])
    AT = ph.sb("AT", [P, 2, DC, GT])
    ps_t = ph.ps("ps_t", [P, DC, GT])
    ps_o = ph.ps("ps_o", [P, 2, GT])
    weights = ph.dma_sem("weights")
    tr, at_ok, o_mm, o_add = ph.sem("tr"), ph.sem("at_ok"), ph.sem("o_mm"), ph.sem("o_add")
    HC = H // DC
    with nc.Block() as block:
        @block.sync
        def _(sp):
            ph.start(sp)
            sp.dma_start(wo[:, :, :], w.rearrange("(c p) n -> p c n", p=P)).then_inc(weights, 16)

        @block.scalar
        def _(act):
            for g in range(NG):
                act.wait_ge(o_mm, START + 2 * g - 2)
                for c in range(DC):
                    act.wait_ge(tr, START + g * DC + c + 1)
                    nc.scalar.copy(AT[:, g % 2, c, :], ps_t[:, c, :]).then_inc(at_ok, 1)

        @block.vector
        def _(dve):
            for g in range(NG):
                for k in range(G // 2):
                    dve.wait_ge(o_mm, START + 2 * g + k + 1)
                    x2 = X[:, g * G + 2 * k:g * G + 2 * k + 2, :]
                    nc.vector.tensor_tensor(x2, ps_o[:, k, :].rearrange("p (j d) -> p j d", j=2), x2,
                                            ALU.add).then_inc(o_add, 1)

        @block.tensor
        def _(pe):
            pe.wait_ge(weights, 16)

            def transposes(g):
                for c in range(DC):
                    pe.wait_ge(at_ok, START + (g - 1) * DC + c + 1)
                    for j in range(G):
                        tile = g * G + j
                        x = nc.tensor.transpose(ps_t[:, c, j * P:(j + 1) * P],
                                                AO[:, tile // TB, tile % TB, c * HC:(c + 1) * HC, :].rearrange(
                                                    "p h d -> p (h d)"), ident[:, :])
                    x.then_inc(tr, 1)
            transposes(0)
            for g in range(NG):
                if g < NG - 1:
                    transposes(g + 1)
                pe.wait_ge(at_ok, START + (g + 1) * DC)
                pe.wait_ge(o_add, START + 2 * g)
                for k in range(G // 2):
                    for j in (2 * k, 2 * k + 1):
                        for c in range(DC):
                            x = nc.tensor.matmul(ps_o[:, k, (j % 2) * D:(j % 2 + 1) * D],
                                                 AT[:, g % 2, c, j * P:(j + 1) * P], wo[:, c, :],
                                                 start=(c == 0), stop=(c == DC - 1))
                    x.then_inc(o_mm, 1)


STAGES = "AMBMCFDF"


def network(nc, a):
    ctx = ExitStack()
    with ctx:
        top = Phase(nc, ctx, "top")
        X = top.sb("X", [P, NT, D])
        ident = top.sb("ident", [P, P])
        loaded, rest = top.sem("loaded"), top.sem("rest")
        with nc.Block() as block:
            @block.sync
            def _(sp):
                x = a["L0_attn_a_x"].rearrange("b (j p) d -> p (b j) d", p=P)
                sp.dma_start(ident[:, :], a["ident"]).then_inc(loaded, 16)
                sp.dma_start(X[:, 0:2 * G, :], x[:, 0:2 * G, :]).then_inc(loaded, 16)
                sp.dma_start(X[:, 2 * G:, :], x[:, 2 * G:, :]).then_inc(rest, 16)
                sp.wait_ge(loaded, 32)
        for n, stage in enumerate(STAGES):
            with ExitStack() as own:
                ph = Phase(nc, own, f"s{n}{stage}")
                if stage == "A":
                    attention(nc, ph, X, ident, a, "decay", rest)
                if stage == "M":
                    expert_ffn(nc, ph, X, ident, a)
                if stage == "B":
                    retention(nc, ph, X, ident, a)
                if stage == "C":
                    attention(nc, ph, X, ident, a, "window")
                if stage == "D":
                    gated_recurrence(nc, ph, X, ident, a)
                if stage == "F":
                    low_rank_ffn(nc, ph, X, ident, a["L1_ffn_U1"], a["L1_ffn_V1"], a["L1_ffn_b1"],
                                 a["L1_ffn_U2"], a["L1_ffn_V2"], a["L1_ffn_b2"],
                                 a["out"] if n == len(STAGES) - 1 else None)


def shape_constants():
    f = np.float32
    distance = np.abs(np.arange(2 * T - P)[None, :] - (T - P) - np.arange(P)[:, None]).astype(f)
    decay = np.exp(f(-0.01) * distance) * f(D ** -0.5)
    inv_freq = (f(1.0) / f(10000.0) ** (np.arange(0, HD, 2, dtype=f) / f(HD))).astype(f)
    freqs = np.arange(T, dtype=f)[:, None] * inv_freq[None, :]
    emb = np.tile(np.concatenate([freqs, freqs], 1).T, (P // HD, 1)).astype(f)
    q, k = np.arange(P)[:, None], np.arange(2 * P)[None, :]
    seen = (k <= q + P) & ((q + P - k <= 128) | (k // 64 == (q + P) // 64))
    masks = np.zeros((P, 3, 2 * P + 4), f)
    masks[:, 0, 0:P] = np.where(k[:, 0:P] <= q, 0.0, -3e38)
    masks[:, 1, 0:2 * P] = np.where(seen | ((k < 4) & (k <= q + P)), 0.0, -3e38)
    masks[:, 2, 0:2 * P] = np.where(seen, 0.0, -3e38)
    return {"decay": decay, "cos": np.cos(emb), "sin": np.sin(emb), "masks": masks.reshape(P, -1),
            "ident": np.eye(P, dtype=f),
            "gather": np.tile(np.eye(32, dtype=f)[:, 0:HD + 1], (4, 1)), "reverse": np.eye(P, dtype=f)[::-1].copy(),
            "batch_base": (np.arange(2)[:, None, None] * (T // 2) + np.arange(B)[None, :, None] * T
                           + np.zeros((1, 1, 8))).astype(f).reshape(-1, 1)}


def laid_out(inputs):
    arrays = {k: np.ascontiguousarray(v) for k, v in inputs.items()}
    for name in ("Wq", "Wv", "Wg", "Wo"):
        arrays[name + "T"] = np.ascontiguousarray(arrays.pop("L0_attn_b_" + name).T)
    arrays["qkv_wT"] = np.ascontiguousarray(arrays.pop("L1_attn_a_qkv_w").T)
    arrays["out_wT"] = np.ascontiguousarray(arrays.pop("L1_attn_a_out_w").T)
    arrays["WkT"] = np.ascontiguousarray(arrays.pop("L0_attn_a_W_k").T)
    arrays["WvT_a"] = np.ascontiguousarray(arrays.pop("L0_attn_a_W_v").T)
    arrays["beta_rows"] = np.repeat(arrays.pop("L0_attn_b_beta"), HD)
    return arrays


def kernel(**inputs):
    import concourse.bacc as bacc
    from concourse.bass_utils import run_bass_kernel_spmd

    nc = bacc.Bacc("TRN2", target_bir_lowering=False, num_devices=1)
    arrays = {**laid_out(inputs), **shape_constants()}
    a = {k: nc.dram_tensor(f"in_{k}", v.shape, mybir.dt.from_np(v.dtype), kind="ExternalInput").ap()
         for k, v in arrays.items()}
    a["out"] = nc.dram_tensor("out", (B, T, D), F32, kind="ExternalOutput").ap()
    network(nc, a)
    r = run_bass_kernel_spmd(nc, [{f"in_{k}": v for k, v in arrays.items()}], core_ids=[0])
    return r.results[0]["out"]
```
